# Optimizing a Trainium2 kernel written in Bass

```python
import numpy as np
import jax
import jax.numpy as jnp

def _softmax(x, axis=-1):
    return jax.nn.softmax(x, axis=axis)

def _gelu(x):
    return jax.nn.gelu(x, approximate=True)

def _silu(x):
    return jax.nn.silu(x)

def _sigmoid(x):
    return jax.nn.sigmoid(x)

def _layernorm(x, axis=-1, eps=1e-05):
    m = jnp.mean(x, axis=axis, keepdims=True)
    v = jnp.var(x, axis=axis, keepdims=True)
    return (x - m) / jnp.sqrt(v + eps)

def _scatter_add(tgt, idx, src, axis=0):
    return tgt.at[idx].add(src)

def _segment_sum(src, seg, n):
    return jax.ops.segment_sum(src, seg, n)
kernel_name = 'mk_gnn_ffn_d1_gnn_r64_48b2d5'

def setup_inputs(seed: int=0):
    np.random.seed(seed)
    _w = jnp.asarray

    def _rec_inputs():
        import jax
        import jax.numpy as jnp
        _gk = jax.random.key(seed)
        x = -8.776e-05 + 1 * jax.random.normal(jax.random.fold_in(_gk, 1), (10000, 512), jnp.float32)
        _s = jax.random.randint(jax.random.fold_in(_gk, 2), (1250,), 0, 10000, jnp.int32)
        _d = jax.random.randint(jax.random.fold_in(_gk, 3), (1250,), 0, 10000, jnp.int32)
        _loop = jnp.arange(10000, dtype=jnp.int32)
        src = jnp.concatenate([_s, _d, _loop])
        dst = jnp.concatenate([_d, _s, _loop])
        _o = jnp.argsort(dst, stable=True)
        src = src[_o]
        dst = dst[_o]
        return (x, src, dst)
    x, src, dst = _rec_inputs()

    def _L0_gnn_setup():
        import jax, jax.numpy as jnp
        import numpy as np
        N_NODES = 10000
        IN_F = 512
        OUT_F = 512
        N_EDGES = 2500
        GRID_SIZE = 5
        SPLINE_ORDER = 3
        ALPHA = 0.2

        def _grid():
            step = 2.0 / GRID_SIZE
            return jnp.arange(-SPLINE_ORDER, GRID_SIZE + SPLINE_ORDER + 1, dtype=jnp.float32) * step - 1.0

        def _b_splines(x, grid):
            x = x[..., None]
            bases = ((x >= grid[:-1]) & (x < grid[1:])).astype(x.dtype)
            for p in range(1, SPLINE_ORDER + 1):
                left = (x - grid[:-(p + 1)]) / (grid[p:-1] - grid[:-(p + 1)]) * bases[..., :-1]
                right = (grid[p + 1:] - x) / (grid[p + 1:] - grid[1:-p]) * bases[..., 1:]
                bases = left + right
            return bases
        key = jax.random.key(seed)
        k1, k2, k3, k4, k5, k6 = jax.random.split(key, 6)
        h = jax.random.normal(k1, (N_NODES, IN_F), dtype=jnp.float32)
        edge_index = jax.random.randint(k2, (2, N_EDGES), 0, N_NODES, dtype=jnp.int64)
        xav = float(np.sqrt(2.0 / (IN_F + OUT_F))) * 1.414
        W = jax.random.normal(k3, (IN_F, OUT_F), dtype=jnp.float32) * xav
        a = jax.random.normal(k4, (2 * OUT_F, 1), dtype=jnp.float32) * float(np.sqrt(2.0 / (2 * OUT_F + 1)))
        base_w = jax.random.normal(k5, (OUT_F, IN_F), dtype=jnp.float32) * xav
        n_coef = GRID_SIZE + SPLINE_ORDER
        spline_w = jax.random.normal(k6, (OUT_F, IN_F, n_coef), dtype=jnp.float32) * 0.1
        return {'h': h, 'W': W, 'a': a, 'base_w': base_w, 'spline_w': spline_w, 'edge_index': edge_index}
    _L0_gnn_all = _L0_gnn_setup()
    _L0_gnn_in = {k: v for k, v in _L0_gnn_all.items() if k in ('W', 'a', 'base_w', 'spline_w')}
    del _L0_gnn_all

    def _L0_ffn_setup():
        import jax, jax.numpy as jnp
        import numpy as np
        CAPACITY_FACTOR = 1.2
        key = jax.random.key(seed)
        k1, k2, k3 = jax.random.split(key, 3)
        B, S, D, E = (8, 64, 512, 16)
        x = jax.random.normal(k1, (B, S, D), dtype=jnp.float32)
        switch_w = jax.random.normal(k2, (E, D), dtype=jnp.float32) * 0.02
        switch_b = jnp.zeros((E,), dtype=jnp.float32)
        expert_w = jax.random.normal(k3, (E, D, D), dtype=jnp.float32) * 0.02
        expert_b = jnp.zeros((E, D), dtype=jnp.float32)
        return {'x': x, 'switch_w': switch_w, 'switch_b': switch_b, 'expert_w': expert_w, 'expert_b': expert_b}
    _L0_ffn_all = _L0_ffn_setup()
    _L0_ffn_in = {k: v for k, v in _L0_ffn_all.items() if k in ('switch_w', 'switch_b', 'expert_w', 'expert_b')}
    del _L0_ffn_all
    return {'x': x, 'src': src, 'dst': dst, 'L0_gnn_W': _L0_gnn_in['W'], 'L0_gnn_a': _L0_gnn_in['a'], 'L0_gnn_base_w': _L0_gnn_in['base_w'], 'L0_gnn_spline_w': _L0_gnn_in['spline_w'], 'L0_ffn_switch_w': _L0_ffn_in['switch_w'], 'L0_ffn_switch_b': _L0_ffn_in['switch_b'], 'L0_ffn_expert_w': _L0_ffn_in['expert_w'], 'L0_ffn_expert_b': _L0_ffn_in['expert_b']}

def reference(x, src, dst, L0_gnn_W, L0_gnn_a, L0_gnn_base_w, L0_gnn_spline_w, L0_ffn_switch_w, L0_ffn_switch_b, L0_ffn_expert_w, L0_ffn_expert_b):
    import jax
    import jax.numpy as jnp

    def _L0_gnn_ref(h, W, a, base_w, spline_w, edge_index):
        import jax, jax.numpy as jnp
        import numpy as np
        N_NODES = 10000
        IN_F = 512
        OUT_F = 512
        N_EDGES = 2500
        GRID_SIZE = 5
        SPLINE_ORDER = 3
        ALPHA = 0.2

        def _grid():
            step = 2.0 / GRID_SIZE
            return jnp.arange(-SPLINE_ORDER, GRID_SIZE + SPLINE_ORDER + 1, dtype=jnp.float32) * step - 1.0

        def _b_splines(x, grid):
            x = x[..., None]
            bases = ((x >= grid[:-1]) & (x < grid[1:])).astype(x.dtype)
            for p in range(1, SPLINE_ORDER + 1):
                left = (x - grid[:-(p + 1)]) / (grid[p:-1] - grid[:-(p + 1)]) * bases[..., :-1]
                right = (grid[p + 1:] - x) / (grid[p + 1:] - grid[1:-p]) * bases[..., 1:]
                bases = left + right
            return bases
        HW = h @ W
        row, col = (edge_index[0], edge_index[1])
        s = HW @ a[:OUT_F, 0]
        t = HW @ a[OUT_F:, 0]
        e = jax.nn.leaky_relu(s[row] + t[col], negative_slope=ALPHA)
        m = jax.ops.segment_max(e, row, num_segments=N_NODES)
        ex = jnp.exp(e - m[row])
        den = jax.ops.segment_sum(ex, row, num_segments=N_NODES)
        att = ex / den[row]
        agg = jax.ops.segment_sum(att[:, None] * h[col], row, num_segments=N_NODES)
        grid = _grid()
        basis = _b_splines(agg, grid)
        out = jax.nn.silu(agg) @ base_w.T + jnp.einsum('nip,oip->no', basis, spline_w)
        return out

    def _L0_ffn_ref(x, switch_w, switch_b, expert_w, expert_b):
        import jax, jax.numpy as jnp
        import numpy as np
        CAPACITY_FACTOR = 1.2
        B, S, D = x.shape
        E = switch_w.shape[0]
        N = B * S
        xf = x.reshape(N, D)
        logits = xf @ switch_w.T + switch_b
        probs = jax.nn.softmax(logits, axis=-1)
        route_probs = jnp.max(probs, axis=-1)
        routes = jnp.argmax(probs, axis=-1)
        oh = jax.nn.one_hot(routes, E, dtype=jnp.int32)
        pos = jnp.take_along_axis(jnp.cumsum(oh, axis=0), routes[:, None], axis=1)[:, 0] - 1
        capacity = int(CAPACITY_FACTOR * N / E)
        keep = pos < capacity
        buf = jnp.zeros((E, capacity, D), dtype=xf.dtype).at[routes, pos].set(xf)
        y = jnp.einsum('ecd,efd->ecf', buf, expert_w) + expert_b[:, None, :]
        gathered = y[routes, jnp.minimum(pos, capacity - 1)]
        out = jnp.where(keep[:, None], gathered, xf) * route_probs[:, None]
        return out.reshape(B, S, D)
    edge_index = jnp.stack([src, dst])
    x = x + _L0_gnn_ref(_layernorm(x, axis=-1), L0_gnn_W, L0_gnn_a, L0_gnn_base_w, L0_gnn_spline_w, edge_index)
    x = x + _L0_ffn_ref(_layernorm(x, axis=-1)[None], L0_ffn_switch_w, L0_ffn_switch_b, L0_ffn_expert_w, L0_ffn_expert_b)[0]
    return x

_drawn_inputs = setup_inputs


def setup_inputs(seed=0):
    import zlib

    import numpy as np

    out = dict(_drawn_inputs(seed))
    spreads = {'L0_ffn_switch_b': (0.0, 0.289), 'L0_ffn_expert_b': (0.0, 0.8)}
    factors = {}
    for name, (base, spread) in spreads.items():
        noise = np.random.default_rng([zlib.crc32(name.encode()), seed]).standard_normal(out[name].shape)
        drawn = base * np.exp(spread * noise) if base else spread * noise
        out[name] = jnp.asarray(drawn.astype(out[name].dtype))
    for name, factor in factors.items():
        out[name] = (out[name] * factor).astype(out[name].dtype)
    return out
```

```python
from contextlib import ExitStack

import concourse.bass as bass
from concourse import mybir

P = 128
N_NODES, D, N_EDGES = 10000, 512, 12500
CH = D // P
NT = 80
NP = NT * P
ET = 98
EP = ET * P
PAD_ROW = NP - 1
NB = 8
NF = NB + 1
NEXP, CAP = 16, int(1.2 * N_NODES / 16)
ST = -(-CAP // P)
FT = NEXP * ST
EPS = 1e-5
BIG = 1e30
ALPHA = 0.2

F32, BF16, F16 = mybir.dt.float32, mybir.dt.bfloat16, mybir.dt.float16
I32, U32 = mybir.dt.int32, mybir.dt.uint32
ALU = mybir.AluOpType
ACT = mybir.ActivationFunctionType
AX = mybir.AxisListType


def wide(ap, shape):
    return ap.broadcast_to(shape)


class Phase:

    def __init__(self, nc, ctx, tag):
        self.nc, self.ctx, self.tag, self.sems = nc, ctx, tag, []
        ctx.callback(self.reset)

    def reset(self):
        with self.nc.Block() as block:

            @block.gpsimd
            def _(pool):
                for s in self.sems:
                    pool.sem_clear(s)

    def sb(self, name, shape, dt=F32):
        return self.ctx.enter_context(self.nc.sbuf_tensor(f"{self.tag}_{name}", shape, dt))

    def ps(self, name, shape, dt=F32):
        return self.ctx.enter_context(self.nc.psum_tensor(f"{self.tag}_{name}", shape, dt))

    def sem(self, name, n=None):
        def one(s):
            self.sems.append(self.ctx.enter_context(self.nc.semaphore(f"{self.tag}_{s}")))
            return self.sems[-1]

        return one(name) if n is None else [one(f"{name}{i}") for i in range(n)]


def swdge(c, n):
    return [c.swdge.pop() for _ in range(n)]


def constants(nc, m, c):
    with nc.Block() as block:
        ramp, cleared = m.sem("c_ramp"), m.sem("c_cleared")

        @block.gpsimd
        def _(pool):
            pool.iota(c.iota_f[:, :], [[1, P]], base=0, channel_multiplier=0,
                      allow_small_or_imprecise_dtypes=True)
            pool.iota(c.iota_p[:, :], [[0, 1]], base=0, channel_multiplier=1,
                      allow_small_or_imprecise_dtypes=True)
            pool.memset(c.ones[:, :], 1.0).then_inc(ramp, 1)
            pool.memset(c.ident[:, :], 0.0).then_inc(cleared, 1)
            pool.memset(c.tri[:, :], 0.0).then_inc(cleared, 1)
            pool.memset(c.after[:, :], 0.0).then_inc(cleared, 1)
            pool.wait_ge(cleared, 3)
            pool.affine_select(out=c.ident[:, :], in_=c.ident[:, :], compare_op=ALU.not_equal, fill=1.0,
                               base=0, pattern=[[-1, P]], channel_multiplier=1)
            pool.affine_select(out=c.tri[:, :], in_=c.tri[:, :], compare_op=ALU.is_ge, fill=1.0,
                               base=0, pattern=[[-1, P]], channel_multiplier=1)
            pool.affine_select(out=c.after[:, :], in_=c.after[:, :], compare_op=ALU.is_ge, fill=1.0,
                               base=0, pattern=[[1, P]], channel_multiplier=-1)


def node_phase(nc, m, c, x, wt, a2, h_dram):
    U = 4
    with ExitStack() as ctx, nc.Block() as block:
        m = Phase(nc, ctx, "n")
        xt = [m.sb(f"x{b}", [P, D]) for b in range(U)]
        ht = [m.sb(f"h{b}", [P, D]) for b in range(U)]
        hT = [m.sb(f"hT{b}", [P, CH, P]) for b in range(U)]
        wt_sb = m.sb("wt", [P, CH, D])
        a_sb = m.sb("a", [P, CH, 2])
        wa = m.sb("wa", [P, CH, 2])
        stats = m.sb("stats", [P, U, 6])
        mv = m.sb("mv", [P, U, 2])
        ve = m.sb("ve", [P, U])
        rstd = m.sb("rstd", [P, U])
        mhalf = m.sb("mhalf", [P, U])
        psT = [m.ps(f"psT{b}", [P, CH, P]) for b in range(2)]
        psS = [m.ps(f"psS{b}", [P, 2]) for b in range(U)]
        psW = m.ps("psW", [P, CH, 2])
        w_loaded, wa_mm, wa_ready, half = m.sem("w_loaded"), m.sem("wa_mm"), m.sem("wa_ready"), m.sem("half")
        x_loaded, h_stored = m.sem("x_loaded", U), m.sem("h_stored", U)
        bn_done, stats_ready, ve_ready, rstd_ready = (m.sem(s) for s in ("bn_done", "stats_ready", "ve_ready", "rstd_ready"))
        h_ready, hT_done = m.sem("h_ready"), m.sem("hT_done", U)
        hT_copied, st_done, st_copied = m.sem("hT_copied", U), m.sem("st_done", U), m.sem("st_copied", U)
        x_t = x.rearrange("(t p) d -> t p d", p=P)
        h_t = h_dram.rearrange("(t p) d -> t p d", p=P)
        K = NT // U

        @block.sync
        def _(sp):
            sp.dma_start(wt_sb[:, :, :], wt.rearrange("(c p) i -> p c i", p=P)).then_inc(w_loaded, 16)
            sp.dma_start(a_sb[:, :, :], a2.rearrange("(c p) k -> p c k", p=P)).then_inc(w_loaded, 16)
            for b in range(U):
                sp.dma_start(xt[b][:, :], x_t[b, :, :]).then_inc(x_loaded[b], 16)

            def turn(k, last):
                for b in range(U):
                    sp.wait_ge(h_ready, k * U + b + 1)
                    sp.dma_start(h_t[k * U + b, :, :], ht[b][:, :]).then_inc(h_stored[b], 16)
                    if not last:
                        sp.dma_start(xt[b][:, :], x_t[k * U + U + b, :, :]).then_inc(x_loaded[b], 16)

            turn(0, False)
            with sp.Fori(1, K - 1) as k:
                turn(k, False)
            turn(K - 1, True)
            for b in range(U):
                sp.wait_ge(h_stored[b], 16 * K)

        @block.vector
        def _(dve):
            def turn(k):
                for b in range(U):
                    dve.wait_ge(x_loaded[b], 16 * (k + 1))
                    dve.bn_stats(stats[:, b, :], xt[b][:, :]).then_inc(bn_done, 1)
                for b in range(U):
                    dve.wait_ge(bn_done, U * k + b + 1)
                    dve.nop(nofuse=True)
                    dve.bn_aggr(mv[:, b, :], stats[:, b, :]).then_inc(stats_ready, 1)
                for b in range(U):
                    dve.wait_ge(rstd_ready, k + 1)
                    dve.wait_ge(h_stored[b], 16 * k)
                    dve.wait_ge(hT_done[b], k)
                    dve.tensor_scalar(ht[b][:, :], xt[b][:, :], mv[:, b, 0:1], rstd[:, b:b + 1],
                                      ALU.subtract, ALU.mult).then_inc(h_ready, 1)

            turn(0)
            with dve.Fori(1, K) as k:
                turn(k)

        @block.gpsimd
        def _(pool):
            pool.memset(mhalf[:, :], -0.5).then_inc(half, 1)
            pool.wait_ge(half, 1)
            def turn(k):
                pool.wait_ge(stats_ready, U * (k + 1))
                pool.wait_ge(h_ready, U * k)
                pool.nop(nofuse=True)
                pool.tensor_scalar(ve[:, :], mv[:, :, 1], EPS, None, ALU.add).then_inc(ve_ready, 1)
                pool.wait_ge(ve_ready, k + 1)
                pool.tensor_tensor(rstd[:, :], ve[:, :], mhalf[:, :], ALU.pow).then_inc(rstd_ready, 1)

            turn(0)
            with pool.Fori(1, K) as k:
                turn(k)

        @block.tensor
        def _(pe):
            pe.wait_ge(w_loaded, 32)
            for ci in range(CH):
                for co in range(CH):
                    mm = pe.matmul(psW[:, ci, :], wt_sb[:, co, ci * P:(ci + 1) * P], a_sb[:, co, :],
                                   start=co == 0, stop=co == CH - 1)
            mm.then_inc(wa_mm, 1)
            pe.wait_ge(wa_ready, 1)

            def turn(k):
                for b in range(U + 1):
                    if b < U:
                        pe.wait_ge(h_ready, k * U + b + 1)
                        pe.wait_ge(hT_copied[(b - 2) % U], k + 1 if b >= 2 else k)
                        for ch in range(CH):
                            t = pe.transpose(psT[b % 2][:, ch, :], ht[b][:, ch * P:(ch + 1) * P], c.ident[:, :])
                        t.then_inc(hT_done[b], 1)
                    if b >= 1:
                        pe.wait_ge(hT_copied[b - 1], k + 1)
                        pe.wait_ge(st_copied[b - 1], k)
                        for ch in range(CH):
                            mm = pe.matmul(psS[b - 1][:, :], hT[b - 1][:, ch, :], wa[:, ch, :],
                                           start=ch == 0, stop=ch == CH - 1)
                        mm.then_inc(st_done[b - 1], 1)

            turn(0)
            with pe.Fori(1, K) as k:
                turn(k)

        @block.scalar
        def _(act):
            act.wait_ge(wa_mm, 1)
            act.copy(wa[:, :, :], psW[:, :, :]).then_inc(wa_ready, 1)
            def turn(k):
                for b in range(U + 1):
                    if b < U:
                        act.wait_ge(hT_done[b], k + 1)
                        act.wait_ge(st_done[b], k)
                        act.copy(hT[b][:, :, :], psT[b % 2][:, :, :]).then_inc(hT_copied[b], 1)
                    if b >= 1:
                        act.wait_ge(st_done[b - 1], k + 1)
                        act.copy(c.st[:, :, bass.ds(k * U + b - 1, 1)].rearrange("p a b -> p (a b)"),
                                 psS[b - 1][:, :]).then_inc(st_copied[b - 1], 1)

            turn(0)
            with act.Fori(1, K) as k:
                turn(k)


def sort_phase(nc, m, c, row, col):
    U = 2
    K = ET // U
    with ExitStack() as ctx:
        m = Phase(nc, ctx, "s")
        rowb = m.sb("rowb", [P, ET, P], I32)
        lowb = m.sb("lowb", [P, ET // 2, P], I32)
        row_low = m.sb("row_low", [P, ET, P], BF16)
        col_low = m.sb("col_low", [P, ET, P], BF16)
        nat = m.sb("nat", [ET, 2, P], I32)
        natf = m.sb("natf", [ET, 2, P])
        rc = m.sb("rc", [P, 2, ET])
        rci = m.sb("rci", [P, 2, ET], I32)
        lowi = m.sb("lowi", [P, 2, ET], I32)
        low = m.sb("low", [P, 2, ET])
        high = m.sb("high", [P, 2, ET])
        one_low = m.sb("one_low", [P, ET, P], BF16)
        one_high = m.sb("one_high", [P, ET, 2, NT], BF16)
        count = m.sb("count", [P, NT])
        start = m.sb("start", [P, NT])
        base = m.sb("base", [P, NT])
        zeros = m.sb("zeros", [P, NT])
        some = m.sb("some", [P, NT])
        last = m.sb("last", [P, NT])
        running = m.sb("running", [P, U, NT])
        row_hotT = m.sb("row_hotT", [P, U, P])
        col_hotT = m.sb("col_hotT", [P, U, P])
        junk = m.sb("junk", [P, U, P + 3 * NT])
        rank = m.sb("rank", [P, ET])
        first = m.sb("first", [P, ET])
        score = m.sb("score", [P, ET])
        pos = m.sb("pos", [P, ET])
        posi = m.sb("posi", [P, ET], I32)
        poshi = m.sb("poshi", [P, ET], I32)
        pos_tile = m.sb("pos_tile", [P, ET])
        pos_lane = m.sb("pos_lane", [P, ET])
        tile_hot = [m.sb(f"tile_hot{b}", [P, ET]) for b in range(U)]
        values = [m.sb(f"values{b}", [P, 3, P]) for b in range(U)]
        psC = m.ps("psC", [P, NT])
        psX = m.ps("psX", [P, 2, P])
        psH = [m.ps(f"psH{b}", [P, NT]) for b in range(U)]
        psG = [m.ps(f"psG{b}", [P, 3, NT]) for b in range(U)]
        psV = m.ps("psV", [ET, 3, P])
        step = m.sem("step")
        row_bc, col_bc, nat_loaded = m.sem("row_bc"), m.sem("col_bc"), m.sem("nat_loaded")
        low_ready, low_copied = m.sem("low_ready"), m.sem("low_copied")

        with nc.Block() as block:
            turned, counted, summed = m.sem("turned"), m.sem("counted"), m.sem("summed")

            @block.sync
            def _(sp):
                flat = lambda a: a.rearrange("(o t) p -> o (t p)", o=1).broadcast_to([P, EP])
                sp.dma_start(nat[:, 0, :], row).then_inc(nat_loaded, 16)
                sp.dma_start(nat[:, 1, :], col).then_inc(nat_loaded, 16)
                sp.dma_start(rowb[:, :, :].rearrange("p t e -> p (t e)"), flat(row)).then_inc(row_bc, 16)
                for half in range(2):
                    sp.wait_ge(low_copied, 2 + half)
                    sp.dma_start(lowb[:, :, :].rearrange("p t e -> p (t e)"),
                                 flat(col)[:, half * EP // 2:(half + 1) * EP // 2]).then_inc(col_bc, 16)

            @block.vector
            def _(dve):
                dve.wait_ge(nat_loaded, 32)
                dve.tensor_copy(natf[:, :, :], nat[:, :, :]).then_inc(step, 1)
                dve.memset(zeros[:, :], 0.0)
                dve.wait_ge(turned, 1)
                dve.tensor_copy(rc[:, :, :], psX[:, :, 0:ET]).then_inc(step, 1)
                dve.wait_ge(step, 2)
                dve.tensor_copy(rci[:, :, :], rc[:, :, :]).then_inc(step, 1)
                dve.wait_ge(step, 3)
                dve.tensor_scalar(lowi[:, :, :], rci[:, :, :], P - 1, None, ALU.bitwise_and).then_inc(step, 1)
                dve.wait_ge(step, 4)
                dve.tensor_copy(low[:, :, :], lowi[:, :, :]).then_inc(step, 1)
                dve.wait_ge(step, 5)
                dve.tensor_tensor(high[:, :, :], rc[:, :, :], low[:, :, :], ALU.subtract).then_inc(step, 1)
                dve.wait_ge(step, 6)
                dve.tensor_scalar(high[:, :, :], high[:, :, :], 1.0 / P, None, ALU.mult).then_inc(step, 1)
                dve.wait_ge(step, 7)
                dve.tensor_tensor(one_low[:, :, :], wide(c.iota_f[:, :].unsqueeze(1), [P, ET, P]),
                                  wide(low[:, 0, :].unsqueeze(2), [P, ET, P]), ALU.is_equal)
                for k in range(2):
                    dve.tensor_tensor(one_high[:, :, k, :], wide(c.iota_f[:, 0:NT].unsqueeze(1), [P, ET, NT]),
                                      wide(high[:, k, :].unsqueeze(2), [P, ET, NT]), ALU.is_equal).then_inc(step, 1)
                dve.wait_ge(row_bc, 16)
                for half in range(2):
                    dve.wait_ge(low_copied, half)
                    dve.tensor_scalar(lowb[:, :, :], rowb[:, half * ET // 2:(half + 1) * ET // 2, :], P - 1, None,
                                      ALU.bitwise_and).then_inc(low_ready, 1)
                for half in range(2):
                    dve.wait_ge(col_bc, 16 * (half + 1))
                    dve.tensor_scalar(lowb[:, :, :], lowb[:, :, :], P - 1, None, ALU.bitwise_and).then_inc(low_ready, 1)
                dve.wait_ge(counted, 1)
                dve.tensor_copy(count[:, :], psC[:, :]).then_inc(step, 1)
                dve.wait_ge(summed, 1)
                dve.tensor_tensor_scan(base[:, :], psX[:, 0, 0:NT], zeros[:, :], 0.0, ALU.add, ALU.add).then_inc(step, 1)
                dve.wait_ge(step, 11)
                dve.tensor_tensor(base[:, :], base[:, :], psX[:, 0, 0:NT], ALU.subtract).then_inc(step, 1)
                dve.wait_ge(step, 12)
                dve.tensor_tensor(start[:, :], psX[:, 1, 0:NT], base[:, :], ALU.add).then_inc(step, 1)
                dve.tensor_scalar(some[:, :], count[:, :], 0.0, None, ALU.is_gt).then_inc(step, 1)
                dve.wait_ge(step, 14)
                dve.tensor_copy(running[:, 0, :], start[:, :])
                dve.tensor_tensor(last[:, :], start[:, :], count[:, :], ALU.add).then_inc(step, 1)
                dve.wait_ge(step, 15)
                dve.scalar_tensor_tensor(last[:, :], last[:, :], -1.0 - EP, some[:, :], ALU.add, ALU.mult).then_inc(step, 1)
                dve.wait_ge(step, 16)
                dve.tensor_scalar(c.last_edge[:, :], last[:, :], float(EP), None, ALU.add)

            @block.scalar
            def _(act):
                for n in range(4):
                    half = n % 2
                    act.wait_ge(low_ready, n + 1)
                    act.copy((row_low, col_low)[n // 2][:, half * ET // 2:(half + 1) * ET // 2, :],
                             lowb[:, :, :]).then_inc(low_copied, 1)

            @block.tensor
            def _(pe):
                pe.wait_ge(step, 1)
                pe.transpose(psX[:, 0, 0:ET], natf[:, 0, :], c.ident[0:ET, 0:ET])
                pe.transpose(psX[:, 1, 0:ET], natf[:, 1, :], c.ident[0:ET, 0:ET]).then_inc(turned, 1)
                pe.wait_ge(step, 9)
                pe.matmul(psC[:, :], one_low[:, 0, :], one_high[:, 0, 0, :], start=True, stop=False)
                with pe.Fori(1, ET - 1) as t:
                    pe.matmul(psC[:, :], one_low[:, bass.ds(t, 1), :].squeeze(1),
                              one_high[:, bass.ds(t, 1), 0, :].squeeze(1), start=False, stop=False)
                pe.matmul(psC[:, :], one_low[:, ET - 1, :], one_high[:, ET - 1, 0, :], start=False, stop=True).then_inc(counted, 1)
                pe.wait_ge(step, 10)
                pe.matmul(psX[:, 0, 0:NT], c.ones[:, :], count[:, :], start=True, stop=True)
                pe.matmul(psX[:, 1, 0:NT], c.tri[:, :], count[:, :], start=True, stop=True).then_inc(summed, 1)

        with nc.Block() as block:
            hist_done, hist_added, hots_ready = m.sem("hist_done", U), m.sem("hist_added", U), m.sem("hots_ready", U)
            looked_up, picked = m.sem("looked_up", U), m.sem("picked", U)

            @block.tensor
            def _(pe):
                def turn(k):
                    for b in range(U):
                        t = k * U + b
                        pe.wait_ge(hist_added[b], k)
                        pe.matmul(psH[b][:, :], one_low[:, bass.ds(t, 1), :].squeeze(1),
                                  one_high[:, bass.ds(t, 1), 0, :].squeeze(1), start=True, stop=True).then_inc(hist_done[b], 1)
                        pe.wait_ge(hots_ready[b], k + 1)
                        pe.wait_ge(picked[b], k)
                        pe.matmul(psG[b][:, 0, :], row_hotT[:, b, :], running[:, b, :], start=True, stop=True)
                        pe.matmul(psG[b][:, 1, :], row_hotT[:, b, :], c.st[:, 0, :], start=True, stop=True)
                        pe.matmul(psG[b][:, 2, :], col_hotT[:, b, :], c.st[:, 1, :], start=True, stop=True).then_inc(looked_up[b], 1)

                turn(0)
                with pe.Fori(1, K) as k:
                    turn(k)

            @block.vector
            def _(dve):
                def turn(k):
                    for b in range(U):
                        t = k * U + b
                        at = bass.ds(t, 1)
                        dve.wait_ge(looked_up[b], k)
                        dve.tensor_scalar(row_hotT[:, b, :], row_low[:, at, :].squeeze(1), c.iota_p[:, :], None, ALU.is_equal)
                        dve.tensor_scalar(col_hotT[:, b, :], col_low[:, at, :].squeeze(1), c.iota_p[:, :], None,
                                          ALU.is_equal).then_inc(hots_ready[b], 1)
                        dve.wait_ge(hist_done[b], k + 1)
                        dve.scalar_tensor_tensor(junk[:, b, 0:P], rowb[:, at, :].squeeze(1), rc[:, 0, at], c.after[:, :],
                                                 ALU.is_equal, ALU.mult, accum_out=rank[:, at])
                        dve.wait_ge(looked_up[1 - b], k + b)
                        dve.wait_ge(hist_added[1 - b], k + b)
                        dve.tensor_tensor(running[:, 1 - b, :], running[:, b, :], psH[b][:, :], ALU.add).then_inc(hist_added[b], 1)
                        dve.wait_ge(looked_up[b], k + 1)
                        dve.scalar_tensor_tensor(junk[:, b, P:P + NT], psG[b][:, 0, :], 1.0, one_high[:, at, 0, :].squeeze(1),
                                                 ALU.mult, ALU.mult, accum_out=first[:, at])
                        dve.scalar_tensor_tensor(junk[:, b, P + NT:].rearrange("p (a n) -> p a n", a=2), psG[b][:, 1:3, :], 1.0,
                                                 one_high[:, at, :, :].squeeze(1), ALU.mult, ALU.mult,
                                                 accum_out=score[:, at]).then_inc(picked[b], 1)

                turn(0)
                with dve.Fori(1, K) as k:
                    turn(k)

        with nc.Block() as block:
            hot_ready, moved, all_moved = m.sem("hot_ready", U), m.sem("moved", U), m.sem("all_moved")
            s3 = m.sem("s3")

            @block.vector
            def _(dve):
                dve.tensor_tensor(pos[:, :], first[:, :], rank[:, :], ALU.add).then_inc(s3, 1)
                dve.wait_ge(s3, 1)
                dve.tensor_copy(posi[:, :], pos[:, :]).then_inc(s3, 1)
                dve.wait_ge(s3, 2)
                dve.tensor_scalar(poshi[:, :], posi[:, :], 7, None, ALU.logical_shift_right).then_inc(s3, 1)
                dve.wait_ge(s3, 3)
                dve.tensor_copy(pos_tile[:, :], poshi[:, :]).then_inc(s3, 1)
                dve.wait_ge(s3, 4)
                dve.scalar_tensor_tensor(pos_lane[:, :], pos_tile[:, :], -float(P), pos[:, :], ALU.mult, ALU.add).then_inc(s3, 1)
                dve.wait_ge(s3, 5)
                def turn(k):
                    for b in range(U):
                        at = bass.ds(k * U + b, 1)
                        dve.wait_ge(moved[b], k)
                        dve.tensor_scalar(tile_hot[b][:, :], c.iota_f[:, 0:ET], pos_tile[:, at], None, ALU.is_equal)
                        for v, value in enumerate((rc[:, 0, at], rc[:, 1, at], score[:, at])):
                            done = dve.tensor_scalar(values[b][:, v, :], c.iota_f[:, :], pos_lane[:, at], value,
                                                     ALU.is_equal, ALU.mult)
                        done.then_inc(hot_ready[b], 1)

                turn(0)
                with dve.Fori(1, K) as k:
                    turn(k)
                dve.wait_ge(all_moved, 1)
                dve.tensor_copy(c.sorted[:, :, :], psV[:, :, :])

            @block.tensor
            def _(pe):
                pe.matmul(psV[:, :, :], zeros_row(c)[:, 0:ET], zeros_row(c)[:, :], start=True, stop=False)
                def turn(k):
                    for b in range(U):
                        pe.wait_ge(hot_ready[b], k + 1)
                        pe.matmul(psV[:, :, :], tile_hot[b][:, :], values[b][:, :, :], start=False, stop=False).then_inc(moved[b], 1)

                turn(0)
                with pe.Fori(1, K) as k:
                    turn(k)
                pe.matmul(psV[:, :, :], zeros_row(c)[:, 0:ET], zeros_row(c)[:, :], start=False, stop=True).then_inc(all_moved, 1)


def zeros_row(c):
    return c.zrow[:, :]


def softmax_phase(nc, m, c, row_dram):
    with ExitStack() as ctx:
        m = Phase(nc, ctx, "a")
        row, col, score = c.sorted[:, 0, :], c.sorted[:, 1, :], c.sorted[:, 2, :]
        e, ex, tot = (m.sb(s, [ET, P]) for s in ("e", "ex", "tot"))
        row1 = m.sb("row1", [ET, P])
        near = m.sb("near", [ET, 2, P])
        same = m.sb("same", [ET, 2, P])
        wall = m.sb("wall", [ET, 2, P])
        through = m.sb("through", [ET, 2, 2])
        scan = m.sb("scan", [ET, 2, P])
        ends = m.sb("ends", [1, 4, ET])
        carried = m.sb("carried", [1, 2, P])
        carry = m.sb("carry", [ET, 2])
        shift = m.sb("shift", [ET, 2, ET])
        ps = m.ps("ps", [P, 4, P])
        ps1 = m.ps("ps1", [1, 4, P])
        psc = m.ps("psc", [ET, 2])
        with nc.Block() as block:
            v, t, landed = m.sem("v"), m.sem("t"), m.sem("landed")
            done = {"v": 0, "t": 0}

            def vec(dve, ins):
                done["v"] += 1
                ins.then_inc(v, 1)
                return done["v"]

            @block.vector
            def _(dve):
                n = 0

                def step(ins):
                    nonlocal n
                    ins.then_inc(v, 1)
                    n += 1
                    dve.wait_ge(v, n)

                dve.memset(shift[:, :, :], 0.0).then_inc(v, 1)
                n += 1
                dve.wait_ge(v, n)
                dve.tensor_copy(shift[:, 0, 1:ET], c.ident[0:ET, 0:ET - 1])
                step(dve.tensor_copy(shift[:, 1, 0:ET - 1], c.ident[0:ET, 1:ET]))
                step(dve.tensor_scalar(row1[:, :], row, 1.0, None, ALU.add))
                dve.wait_ge(t, 1)
                dve.tensor_copy(near[:, 0, 1:P], row[:, 0:P - 1])
                dve.tensor_copy(near[:, 1, 0:P - 1], row[:, 1:P])
                dve.tensor_scalar(near[:, 0, 0:1], psc[:, 0:1], -1.0, None, ALU.add)
                step(dve.tensor_scalar(near[:, 1, P - 1:P], psc[:, 1:2], -1.0, None, ALU.add))
                dve.tensor_tensor(same[:, 0, :], near[:, 0, :], row, ALU.is_equal)
                step(dve.tensor_tensor(same[:, 1, :], near[:, 1, :], row, ALU.is_equal))
                step(dve.tensor_scalar(wall[:, :, :], same[:, :, :], -1.0, BIG, ALU.add, ALU.mult))
                dve.tensor_reduce(through[:, :, 0], wall[:, :, :], AX.X, ALU.min)
                dve.tensor_reduce(through[:, :, 1], same[:, :, :], AX.X, ALU.min)
                step(dve.scalar_tensor_tensor(e[:, :], score, ALPHA, score, ALU.mult, ALU.max))
                turn = 1
                for what, (value, gate, k, op0, op1, low) in enumerate((
                        (e, wall, 0, ALU.add, ALU.max, -BIG), (ex, same, 1, ALU.mult, ALU.add, 0.0))):
                    def scans(initial):
                        f = dve.tensor_tensor_scan(scan[:, 0, :], gate[:, 0, :], value[:, :], initial(0), op0, op1)
                        step(dve.tensor_tensor_scan(scan[:, 1, ::-1], gate[:, 1, ::-1], value[:, ::-1], initial(1), op0, op1))

                    scans(lambda d: low)
                    turn += 1
                    dve.wait_ge(t, turn)
                    step(dve.tensor_copy(ends[:, :, :], ps1[:, :, 0:ET]))
                    dve.tensor_tensor_scan(carried[:, 0, 0:ET], ends[:, 2, 0:ET], ends[:, 0, 0:ET], low, op0, op1)
                    step(dve.tensor_tensor_scan(carried[:, 1, 0:ET][:, ::-1], ends[:, 3, 0:ET][:, ::-1],
                                                ends[:, 1, 0:ET][:, ::-1], low, op0, op1))
                    turn += 1
                    dve.wait_ge(t, turn)
                    step(dve.tensor_copy(carry[:, :], psc[:, :]))
                    turn += 1
                    dve.wait_ge(t, turn)
                    step(dve.tensor_copy(carry[:, :], psc[:, :]))
                    scans(lambda d: carry[:, d:d + 1])
                    if what == 0:
                        step(dve.tensor_tensor(tot[:, :], scan[:, 0, :], scan[:, 1, :], ALU.max))
                        step(dve.tensor_tensor(tot[:, :], e[:, :], tot[:, :], ALU.subtract))
                        turn += 1
                        dve.wait_ge(t, turn)
                    else:
                        step(dve.tensor_tensor(tot[:, :], scan[:, 0, :], scan[:, 1, :], ALU.add))
                        step(dve.tensor_tensor(tot[:, :], tot[:, :], ex[:, :], ALU.subtract))
                        step(dve.reciprocal(tot[:, :], tot[:, :]))
                        step(dve.tensor_tensor(ex[:, :], ex[:, :], tot[:, :], ALU.mult))
                step(dve.tensor_tensor(carry[:, 0:1], row1[:, P - 1:P], same[:, 1, P - 1:P], ALU.mult))
                step(dve.tensor_scalar(c.run_on[:, :], carry[:, 0:1], -1.0, None, ALU.add))
                turn += 1
                dve.wait_ge(t, turn)
                dve.tensor_copy(c.row_l[:, :], ps[:, 0, 0:ET])
                dve.tensor_copy(c.col_l[:, :], ps[:, 1, 0:ET])
                dve.tensor_copy(c.att_l[:, :], ps[:, 2, 0:ET])
                done["v"] = n

            @block.tensor
            def _(pe):
                pe.wait_ge(v, 3)
                pe.matmul(psc[:, 0:1], shift[:, 0, :], row1[:, P - 1:P], start=True, stop=True)
                pe.matmul(psc[:, 1:2], shift[:, 1, :], row1[:, 0:1], start=True, stop=True).then_inc(t, 1)
                at = 7
                for k in range(2):
                    at += 1
                    pe.wait_ge(v, at)
                    for d, end in ((0, P - 1), (1, 0)):
                        pe.matmul(ps1[:, d, 0:ET], scan[:, d, end:end + 1], c.ident[0:ET, 0:ET], start=True, stop=True)
                        g = pe.matmul(ps1[:, 2 + d, 0:ET], through[:, d, k:k + 1], c.ident[0:ET, 0:ET], start=True, stop=True)
                    g.then_inc(t, 1)
                    at += 2
                    pe.wait_ge(v, at)
                    for d in range(2):
                        g = pe.matmul(psc[:, d:d + 1], carried[:, d, 0:ET], c.ones[0:1, 0:1], start=True, stop=True)
                    g.then_inc(t, 1)
                    at += 1
                    pe.wait_ge(v, at)
                    for d in range(2):
                        g = pe.matmul(psc[:, d:d + 1], shift[:, d, :], carry[:, d:d + 1], start=True, stop=True)
                    g.then_inc(t, 1)
                    at += 2 + 2
                    if k == 1:
                        at += 2
                at += 2
                pe.wait_ge(v, at)
                for j, a in enumerate((row, col, ex[:, :])):
                    g = pe.transpose(ps[:, j, 0:ET], a, c.ident[0:ET, 0:ET])
                g.then_inc(t, 1)

            @block.scalar
            def _(act):
                act.wait_ge(v, 7 + 8)
                act.activation(ex[:, :], tot[:, :], ACT.Exp).then_inc(t, 1)

            @block.sync
            def _(sp):
                sp.dma_start(row_dram, row).then_inc(landed, 16)
                sp.wait_ge(landed, 16)

def edge_phase(nc, m, c, h_dram, row_dram, part_dram):
    U = 7
    K = ET // U
    V = 2
    with ExitStack() as ctx, nc.Block() as block:
        m = Phase(nc, ctx, "e")
        rowb = m.sb("rowb", [P, ET, P])
        index = [m.sb(f"index{b}", [P, 1], U32) for b in range(U)]
        got = [m.sb(f"got{b}", [P, D]) for b in range(U)]
        weight = [m.sb(f"weight{b}", [P, P]) for b in range(U)]
        part = [m.sb(f"part{b}", [P, D]) for b in range(U)]
        none = m.sb("none", [P, D])
        ps = [m.ps(f"ps{b}", [P, D]) for b in range(U)]
        rows_loaded, zeroed, zero_stored = m.sem("rows_loaded"), m.sem("zeroed"), m.sem("zero_stored")
        index_ready, gathered, weight_ready = m.sem("index_ready", U), swdge(c, U), m.sem("weight_ready", U)
        summed, copied, stored, ends_loaded = m.sem("summed", U), m.sem("copied", U), m.sem("stored", U), m.sem("ends_loaded")
        part_t = part_dram.rearrange("(t p) d -> t p d", p=P)

        @block.gpsimd
        def _(pool):
            pool.memset(none[:, :], 0.0).then_inc(zeroed, 1)
            def turn(k):
                for b in range(U):
                    pool.wait_ge(summed[b], k)
                    pool.tensor_copy(index[b][:, :], c.col_l[:, bass.ds(k * U + b, 1)]).then_inc(index_ready[b], 1)
                for b in range(U):
                    pool.wait_ge(index_ready[b], k + 1)
                    pool.nop(nofuse=True)
                    pool.indirect_dma_start(got[b][:, :], None, h_dram,
                                            bass.IndirectOffsetOnAxis(index[b][:, :], 0)).then_inc(gathered[b], 16)

            turn(0)
            with pool.Fori(1, K) as k:
                turn(k)

        @block.vector
        def _(dve):
            dve.wait_ge(rows_loaded, 16)
            def turn(k):
                for b in range(U):
                    at = bass.ds(k * U + b, 1)
                    dve.wait_ge(summed[b], k)
                    dve.tensor_scalar(weight[b][:, :], rowb[:, at, :].squeeze(1), c.row_l[:, at], c.att_l[:, at],
                                      ALU.is_equal, ALU.mult).then_inc(weight_ready[b], 1)

            turn(0)
            with dve.Fori(1, K) as k:
                turn(k)

        @block.tensor
        def _(pe):
            def turn(k):
                for b in range(U):
                    pe.wait_ge(weight_ready[b], k + 1)
                    pe.wait_ge(gathered[b], 16 * (k + 1))
                    pe.wait_ge(copied[b], k)
                    pe.matmul(ps[b][:, :], weight[b][:, :], got[b][:, :], start=True, stop=True).then_inc(summed[b], 1)

            turn(0)
            with pe.Fori(1, K) as k:
                turn(k)

        @block.scalar
        def _(act):
            def turn(k):
                for b in range(U):
                    act.wait_ge(summed[b], k + 1)
                    act.wait_ge(stored[b], 16 * k)
                    act.copy(part[b][:, :], ps[b][:, :]).then_inc(copied[b], 1)

            turn(0)
            with act.Fori(1, K) as k:
                turn(k)

        @block.sync
        def _(sp):
            sp.dma_start(rowb[:, :, :].rearrange("p t e -> p (t e)"),
                         row_dram.rearrange("(o t) p -> o (t p)", o=1).broadcast_to([P, EP])).then_inc(rows_loaded, 16)
            sp.wait_ge(zeroed, 1)
            sp.dma_start(part_t[ET, :, :], none[:, :]).then_inc(zero_stored, 16)
            def turn(k):
                for b in range(U):
                    sp.wait_ge(copied[b], k + 1)
                    sp.dma_start(part_t[k * U + b, :, :], part[b][:, :]).then_inc(stored[b], 16)

            turn(0)
            with sp.Fori(1, K) as k:
                turn(k)
            for b in range(U):
                sp.wait_ge(stored[b], 16 * K)
            sp.wait_ge(zero_stored, 16)
            sp.dma_start(c.ends[:, :], part_t[0:ET, P - 1, :]).then_inc(ends_loaded, 16)
            sp.wait_ge(ends_loaded, 16)


def weight_phase(nc, m, c, base_w, spline_w):
    with ExitStack() as ctx, nc.Block() as block:
        m = Phase(nc, ctx, "w")
        U = 3
        w = [m.sb(f"w{b}", [P, 4, D]) for b in range(U)]
        tops = m.sb("tops", [P, 18])
        top = m.sb("top", [P, 1])
        topT = m.sb("topT", [1, 1])
        bits = m.sb("bits", [P, 1])
        third = m.sb("third", [P, 1])
        ps = m.ps("ps", [P, P])
        loaded, used, v, t = m.sem("loaded", U), m.sem("used", U), m.sem("v"), m.sem("t")
        scaled, high, low = m.sem("scaled"), m.sem("high"), m.sem("low")
        base_v = base_w.rearrange("(c p) o -> p c o", p=P)
        spline_v = spline_w.rearrange("(c p) k o -> c p k o", p=P)
        pieces = [(base_v, 0, None)] + [(spline_v[ch, :, 4 * g:4 * g + 4, :], ch, g) for ch in range(CH) for g in range(2)]
        NPC = len(pieces)

        @block.sync
        def _(sp):
            for n in range(2 * NPC):
                if n >= U:
                    sp.wait_ge(used[n % U], n // U)
                sp.dma_start(w[n % U][:, :, :], pieces[n % NPC][0]).then_inc(loaded[n % U], 16)

        @block.vector
        def _(dve):
            for n in range(NPC):
                dve.wait_ge(loaded[n % U], 16 * (n // U + 1))
                dve.tensor_reduce(tops[:, n:n + 1], w[n % U][:, :, :], AX.XY, ALU.max, apply_absolute_value=True).then_inc(used[n % U], 1)
            for b in range(U):
                dve.wait_ge(used[b], len(range(b, NPC, U)))
            dve.tensor_reduce(top[:, :], tops[:, 0:NPC], AX.X, ALU.max).then_inc(v, 1)
            dve.wait_ge(t, 1)
            dve.tensor_reduce(topT[:, :], ps[0:1, 0:P], AX.X, ALU.max).then_inc(v, 1)
            dve.wait_ge(t, 2)
            dve.tensor_scalar(bits[:, :], ps[:, 0:1], 1e-30, None, ALU.max).then_inc(v, 1)
            dve.wait_ge(v, 3)
            dve.tensor_scalar(bits[:, :].bitcast(I32), bits[:, :].bitcast(I32), 0x7F800000, None, ALU.bitwise_and).then_inc(v, 1)
            dve.wait_ge(v, 4)
            dve.tensor_scalar(c.unscale[:, :], bits[:, :], 2.0 ** -23, None, ALU.mult)
            dve.reciprocal(c.scale[:, :], bits[:, :]).then_inc(v, 1)
            dve.wait_ge(v, 5)
            dve.tensor_scalar(c.scale[:, :], c.scale[:, :], 2.0 ** 13, None, ALU.mult).then_inc(v, 1)
            dve.wait_ge(v, 6)
            dve.tensor_scalar(third[:, :], c.scale[:, :], 1.0 / 3.0, None, ALU.mult).then_inc(scaled, 1)
            dve.wait_ge(scaled, 1)
            for n in range(NPC):
                q = n + NPC
                _, ch, g = pieces[n]
                fac = c.scale if g is None else third
                hi, lo = target(c, ch, g)
                dve.wait_ge(high, n + 1)
                dve.scalar_tensor_tensor(lo, w[q % U][:, :, :], fac[:, :], hi, ALU.mult, ALU.subtract).then_inc(used[q % U], 1)

        @block.scalar
        def _(act):
            act.wait_ge(scaled, 1)
            for n in range(NPC):
                q = n + NPC
                _, ch, g = pieces[n]
                fac = c.scale if g is None else third
                hi, lo = target(c, ch, g)
                act.wait_ge(loaded[q % U], 16 * (q // U + 1))
                act.activation(hi, w[q % U][:, :, :], ACT.Copy, scale=fac[:, :]).then_inc(high, 1)

        @block.tensor
        def _(pe):
            pe.wait_ge(v, 1)
            pe.transpose(ps[0:1, 0:P], top[:, :], c.ident[:, :]).then_inc(t, 1)
            pe.wait_ge(v, 2)
            pe.matmul(ps[:, 0:1], c.ones[0:1, :], topT[:, :], start=True, stop=True).then_inc(t, 1)


def target(c, ch, g):
    if g is None:
        return c.w_hi[:, :, NB, :], c.w_lo[:, :, NB, :]
    return c.w_hi[:, ch, 4 * g:4 * g + 4, :], c.w_lo[:, ch, 4 * g:4 * g + 4, :]


def layer_phase(nc, m, c, x, part_dram, both_dram, out):
    with ExitStack() as ctx, nc.Block() as block:
        m = Phase(nc, ctx, "l")
        pair = lambda name, shape, dt=F32: [m.sb(f"{name}{b}", shape, dt) for b in range(2)]
        index, agg, xt = pair("index", [P, 1], U32), pair("agg", [P, D]), pair("xt", [P, D])
        both, out0 = pair("both", [P, 2, D]), pair("out0", [P, D])
        carry_hot = pair("carry_hot", [ET, P])
        f_hi, f_lo = pair("f_hi", [P, NF, D], F16), pair("f_lo", [P, NF, D], F16)
        G = 4
        y, a, b1, a2, b2, nn = (pair(s, [P, 2, D]) for s in ("y", "a", "b1", "a2", "b2", "nn"))
        aggT, th, zz = m.sb("aggT", [P, D]), m.sb("th", [P, D]), m.sb("zz", [P, D])
        h2T = m.sb("h2T", [P, CH, P])
        stats, mv, ve, rstd = pair("stats", [P, 6]), pair("mv", [P, 2]), pair("ve", [P, 1]), pair("rstd", [P, 1])
        mhalf = m.sb("mhalf", [P, 1])
        logit, ntop, ex, tot, prob = (pair("logit", [P, NEXP]), pair("ntop", [P, 1]), pair("ex", [P, NEXP]),
                                      pair("tot", [P, 1]), pair("prob", [P, 1]))
        run_on_t = m.sb("run_on_t", [ET, NT])
        ps_agg = [m.ps(f"ps_agg{b}", [P, CH, P]) for b in range(2)]
        ps_out = [m.ps(f"ps_out{b}", [P, D]) for b in range(2)]
        ps_h2 = m.ps("ps_h2", [P, CH, P])
        ps_logit = [m.ps(f"ps_logit{b}", [P, NEXP]) for b in range(2)]
        gathered = swdge(c, 2)
        x_loaded, both_stored, out_stored = (m.sem(s, 2) for s in ("x_loaded", "both_stored", "out_stored"))
        run_on_ready, half = m.sem("run_on_ready"), m.sem("half")
        index_ready, hot_ready, aggT_ready = m.sem("index_ready", 2), m.sem("hot_ready", 2), m.sem("aggT_ready", 2)
        y_ready, ab_ready, sq_ready, b3_ready, n_ready, a3_ready, hi_ready, lo_ready = (
            m.sem(s) for s in ("y_ready", "ab_ready", "sq_ready", "b3_ready", "n_ready", "a3_ready", "hi_ready", "lo_ready"))
        th_ready, z_ready, zhi_ready, zlo_ready = (m.sem(s, 2) for s in ("th_ready", "z_ready", "zhi_ready", "zlo_ready"))
        out_ready, x1_ready, bn_done, mv_ready, ve_ready, rstd_ready, h2_ready = (
            m.sem(s, 2) for s in ("out_ready", "x1_ready", "bn_done", "mv_ready", "ve_ready", "rstd_ready", "h2_ready"))
        h2T_ready, h2T_copied, logit_done, logit_ready, ntop_ready, ex_ready, prob_ready, out0_ready = (
            m.sem(s, 2) for s in ("h2T_ready", "h2T_copied", "logit_done", "logit_ready", "ntop_ready", "ex_ready", "prob_ready", "out0_ready"))
        x_t = x.rearrange("(t p) d -> t p d", p=P)
        out_t = out.rearrange("(t p) d -> t p d", p=P)
        both_t = both_dram.rearrange("(t p) d -> t p d", p=P)

        def steps(eng, step):
            for i in range(-1, 4):
                step(i, i // 2, i % 2, lambda o, i=i: 0 <= i + o < NT)
            with eng.Fori(2, NT // 2 - 1) as k:
                for b in range(2):
                    step(k * 2 + b, k, b, lambda o: True)
            for i in range(NT - 2, NT + 2):
                step(i, i // 2, i % 2, lambda o, i=i: 0 <= i + o < NT)

        def slot(k, b, o):
            return (b + o) % 2, k + (b + o) // 2

        @block.gpsimd
        def _(pool):
            pool.iota(run_on_t[:, :], [[-P, NT]], base=0, channel_multiplier=0, allow_small_or_imprecise_dtypes=True).then_inc(run_on_ready, 1)
            pool.memset(mhalf[:, :], -0.5).then_inc(half, 1)
            pool.wait_ge(half, 1)

            def gather(i, b, k):
                pool.wait_ge(aggT_ready[b], k)
                pool.tensor_copy(index[b][:, :], c.last_edge[:, bass.ds(i, 1)]).then_inc(index_ready[b], 1)
                pool.wait_ge(index_ready[b], k + 1)
                pool.nop(nofuse=True)
                pool.indirect_dma_start(agg[b][:, :], None, part_dram,
                                        bass.IndirectOffsetOnAxis(index[b][:, :], 0)).then_inc(gathered[b], 16)

            def cubes(k, b, i, g):
                n = 4 * (i + 1) + g
                pool.wait_ge(sq_ready, n + 1)
                pool.tensor_tensor(b2[g % 2][:, :, :], b1[g % 2][:, :, :], b2[g % 2][:, :, :], ALU.mult).then_inc(b3_ready, 1)

            def step(i, k, b, ok):
                if ok(2):
                    b2_, k2 = slot(k, b, 2)
                    gather(i + 2, b2_, k2)
                if ok(1):
                    cubes(k, b, i, 0)
                    cubes(k, b, i, 1)
                if ok(-1):
                    bb, kk = slot(k, b, -1)
                    pool.wait_ge(mv_ready[bb], kk + 1)
                    pool.wait_ge(h2_ready[bb], kk)
                    pool.nop(nofuse=True)
                    pool.tensor_scalar(ve[bb][:, :], mv[bb][:, 1:2], EPS, None, ALU.add).then_inc(ve_ready[bb], 1)
                    pool.wait_ge(ve_ready[bb], kk + 1)
                    pool.tensor_tensor(rstd[bb][:, :], ve[bb][:, :], mhalf[:, :], ALU.pow).then_inc(rstd_ready[bb], 1)
                if ok(1):
                    cubes(k, b, i, 2)
                    cubes(k, b, i, 3)

            gather(0, 0, 0)
            steps(pool, step)

        @block.sync
        def _(sp):
            def step(i, k, b, ok):
                if ok(0):
                    sp.wait_ge(x1_ready[b], k)
                    sp.dma_start(xt[b][:, :], x_t[i, :, :] if isinstance(i, int) else x_t[bass.ds(i, 1), :, :].squeeze(0)).then_inc(x_loaded[b], 16)
                if ok(-1):
                    bb, kk = slot(k, b, -1)
                    sp.wait_ge(h2_ready[bb], kk + 1)
                    sp.dma_start(both_t[bass.ds(i - 1, 1), :, :].squeeze(0), both[bb][:, :, :].rearrange("p a d -> p (a d)")).then_inc(both_stored[bb], 16)
                if ok(-2):
                    sp.wait_ge(out0_ready[b], k)
                    sp.dma_start(out_t[bass.ds(i - 2, 1), :, :].squeeze(0), out0[b][:, :]).then_inc(out_stored[b], 16)

            steps(sp, step)
            for b in range(2):
                sp.wait_ge(both_stored[b], 16 * (NT // 2))
                sp.wait_ge(out_stored[b], 16 * (NT // 2))

        @block.tensor
        def _(pe):
            def agg_t(tile, b, k):
                pe.wait_ge(gathered[b], 16 * (k + 1))
                pe.wait_ge(hot_ready[b], k + 1)
                if not (isinstance(tile, int) and tile < 1):
                    pe.wait_ge(y_ready, 4 * tile - 4)
                for ch in range(CH):
                    pe.matmul(ps_agg[b][:, ch, :], agg[b][:, ch * P:(ch + 1) * P], c.ident[:, :], start=True, stop=False)
                    g = pe.matmul(ps_agg[b][:, ch, :], c.ends[:, ch * P:(ch + 1) * P], carry_hot[b][:, :], start=False, stop=True)
                g.then_inc(aggT_ready[b], 1)

            def products(b, k, i, fs, first, last):
                for f in fs:
                    for ch in range(CH):
                        cols = slice(ch * P, (ch + 1) * P)
                        for part, (lhs, rhs) in enumerate(((f_hi, c.w_hi), (f_hi, c.w_lo), (f_lo, c.w_hi))):
                            mm = pe.matmul(ps_out[b][:, :], lhs[b][:, f, cols], rhs[:, ch, f, :],
                                           start=first and f == fs[0] and ch == 0 and part == 0,
                                           stop=last and f == fs[-1] and ch == CH - 1 and part == 2)
                return mm

            def step(i, k, b, ok):
                if ok(1):
                    agg_t(i + 1, *slot(k, b, 1))
                if ok(0):
                    pe.wait_ge(x1_ready[b], k)
                    for g in range(2):
                        pe.wait_ge(lo_ready, 4 * i + g + 1)
                        products(b, k, i, (2 * g, 2 * g + 1), g == 0, False)
                bb, kk = slot(k, b, -1)
                if ok(-1):
                    pe.wait_ge(h2_ready[bb], kk + 1)
                    for ch in range(CH):
                        g = pe.transpose(ps_h2[:, ch, :], both[bb][:, 1, ch * P:(ch + 1) * P], c.ident[:, :])
                    g.then_inc(h2T_ready[bb], 1)
                if ok(0):
                    for g in range(2, 4):
                        pe.wait_ge(lo_ready, 4 * i + g + 1)
                        products(b, k, i, (2 * g, 2 * g + 1), False, False)
                if ok(-1):
                    pe.wait_ge(h2T_copied[bb], kk + 1)
                    pe.wait_ge(logit_ready[bb], kk)
                    for ch in range(CH):
                        g = pe.matmul(ps_logit[bb][:, :], h2T[:, ch, :], c.gate_w[:, ch, :], start=ch == 0, stop=ch == CH - 1)
                    g.then_inc(logit_done[bb], 1)
                if ok(0):
                    pe.wait_ge(zlo_ready[b], k + 1)
                    products(b, k, i, (NB,), False, True).then_inc(out_ready[b], 1)

            steps(pe, step)

        @block.scalar
        def _(act):
            def bases(b, k, i, g):
                n = 4 * (i + 1) + g
                if g == 0:
                    act.wait_ge(aggT_ready[b], k + 1)
                if not (isinstance(n, int) and n < 2):
                    act.wait_ge(ab_ready, n - 1)
                for j in range(2):
                    done = act.activation(y[g % 2][:, j, :], ps_agg[b][:, :, :].rearrange("p c n -> p (c n)"), ACT.Abs,
                                          bias=c.mid[:, 2 * g + j:2 * g + j + 1], scale=20.0)
                done.then_inc(y_ready, 1)

            def squares(i, g):
                n = 4 * (i + 1) + g
                act.wait_ge(ab_ready, n + 1)
                if not (isinstance(n, int) and n < 2):
                    act.wait_ge(n_ready, n - 1)
                act.activation(a2[g % 2][:, :, :], a[g % 2][:, :, :], ACT.Square)
                act.activation(b2[g % 2][:, :, :], b1[g % 2][:, :, :], ACT.Square, scale=2.0).then_inc(sq_ready, 1)

            def high(b, k, i, g):
                n = 4 * (i + 1) + g
                act.wait_ge(n_ready, n + 1)
                if g == 0:
                    act.wait_ge(out_ready[b], k)
                act.copy(f_hi[b][:, 2 * g:2 * g + 2, :], nn[g % 2][:, :, :]).then_inc(hi_ready, 1)

            def step(i, k, b, ok):
                if ok(1):
                    b_, k_ = slot(k, b, 1)
                    bases(b_, k_, i, 0)
                    bases(b_, k_, i, 1)
                    squares(i, 0)
                    act.wait_ge(z_ready[1 - b_], k_ + b_)
                    act.copy(aggT[:, :], ps_agg[b_][:, :, :].rearrange("p c n -> p (c n)"))
                    act.activation(th[:, :], ps_agg[b_][:, :, :].rearrange("p c n -> p (c n)"), ACT.Tanh, scale=0.5).then_inc(th_ready[b_], 1)
                    bases(b_, k_, i, 2)
                    squares(i, 1)
                    high(b_, k_, i, 0)
                    bases(b_, k_, i, 3)
                if ok(-1):
                    bb, kk = slot(k, b, -1)
                    act.wait_ge(h2T_ready[bb], kk + 1)
                    act.wait_ge(logit_done[1 - bb], kk + bb)
                    act.copy(h2T[:, :, :], ps_h2[:, :, :]).then_inc(h2T_copied[bb], 1)
                if ok(1):
                    squares(i, 2)
                    high(b_, k_, i, 1)
                    act.wait_ge(z_ready[b_], k_ + 1)
                    act.wait_ge(out_ready[b_], k_)
                    act.activation(f_hi[b_][:, NB, :], zz[:, :], ACT.Copy, scale=512.0).then_inc(zhi_ready[b_], 1)
                    squares(i, 3)
                    high(b_, k_, i, 2)
                    high(b_, k_, i, 3)
                if ok(-1):
                    act.wait_ge(ntop_ready[bb], kk + 1)
                    act.wait_ge(prob_ready[bb], kk)
                    act.activation(ex[bb][:, :], logit[bb][:, :], ACT.Exp, bias=ntop[bb][:, :], accum_out=tot[bb][:, :]).then_inc(ex_ready[bb], 1)

            steps(act, step)

        @block.vector
        def _(dve):
            dve.wait_ge(run_on_ready, 1)
            dve.tensor_scalar(run_on_t[:, :], run_on_t[:, :], c.run_on[:, :], None, ALU.add).then_inc(run_on_ready, 1)
            dve.wait_ge(run_on_ready, 2)

            def hot(i, b, k):
                dve.wait_ge(aggT_ready[b], k)
                dve.tensor_scalar(carry_hot[b][:, :], c.iota_f[0:ET, :], run_on_t[:, bass.ds(i, 1)], None, ALU.is_equal).then_inc(hot_ready[b], 1)

            def sides(i, g):
                n = 4 * (i + 1) + g
                dve.wait_ge(y_ready, n + 1)
                if not (isinstance(n, int) and n < 2):
                    dve.wait_ge(b3_ready, n - 1)
                    dve.wait_ge(n_ready, n - 1)
                dve.tensor_scalar(a[g % 2][:, :, :], y[g % 2][:, :, :], -16.0, 0.0, ALU.add, ALU.min)
                dve.tensor_scalar(b1[g % 2][:, :, :], y[g % 2][:, :, :], -8.0, 0.0, ALU.add, ALU.min).then_inc(ab_ready, 1)

            def basis(i, g):
                n = 4 * (i + 1) + g
                dve.wait_ge(sq_ready, n + 1)
                dve.tensor_tensor(a2[g % 2][:, :, :], a[g % 2][:, :, :], a2[g % 2][:, :, :], ALU.mult).then_inc(a3_ready, 1)
                dve.wait_ge(b3_ready, n + 1)
                dve.wait_ge(a3_ready, n + 1)
                if not (isinstance(n, int) and n < 2):
                    dve.wait_ge(lo_ready, n - 1)
                    dve.wait_ge(hi_ready, n - 1)
                dve.tensor_tensor(nn[g % 2][:, :, :], b2[g % 2][:, :, :], a2[g % 2][:, :, :], ALU.subtract).then_inc(n_ready, 1)

            def low(b, k, i, g):
                n = 4 * (i + 1) + g
                dve.wait_ge(hi_ready, n + 1)
                dve.tensor_tensor(f_lo[b][:, 2 * g:2 * g + 2, :], nn[g % 2][:, :, :], f_hi[b][:, 2 * g:2 * g + 2, :],
                                  ALU.subtract).then_inc(lo_ready, 1)

            def step(i, k, b, ok):
                bb, kk = slot(k, b, -1)
                if ok(2):
                    b2_, k2 = slot(k, b, 2)
                    hot(i + 2, b2_, k2)
                if ok(1):
                    b_, k_ = slot(k, b, 1)
                    sides(i, 0)
                    sides(i, 1)
                if ok(-1):
                    dve.wait_ge(out_ready[bb], kk + 1)
                    dve.wait_ge(x_loaded[bb], 16 * (kk + 1))
                    dve.wait_ge(both_stored[bb], 16 * kk)
                    dve.wait_ge(out0_ready[bb], kk)
                    dve.scalar_tensor_tensor(both[bb][:, 0, :], ps_out[bb][:, :], c.unscale[:, :], xt[bb][:, :],
                                             ALU.mult, ALU.add).then_inc(x1_ready[bb], 1)
                    dve.wait_ge(x1_ready[bb], kk + 1)
                    dve.bn_stats(stats[bb][:, :], both[bb][:, 0, :]).then_inc(bn_done[bb], 1)
                if ok(1):
                    basis(i, 0)
                if ok(-1):
                    dve.wait_ge(bn_done[bb], kk + 1)
                    dve.nop(nofuse=True)
                    dve.bn_aggr(mv[bb][:, :], stats[bb][:, :]).then_inc(mv_ready[bb], 1)
                if ok(1):
                    dve.wait_ge(th_ready[b_], k_ + 1)
                    dve.wait_ge(zlo_ready[1 - b_], k_ + b_)
                    dve.scalar_tensor_tensor(zz[:, :], th[:, :], 1.0, aggT[:, :], ALU.add, ALU.mult).then_inc(z_ready[b_], 1)
                    sides(i, 2)
                    basis(i, 1)
                    low(b_, k_, i, 0)
                if ok(-1):
                    dve.wait_ge(rstd_ready[bb], kk + 1)
                    dve.tensor_scalar(both[bb][:, 1, :], both[bb][:, 0, :], mv[bb][:, 0:1], rstd[bb][:, :],
                                      ALU.subtract, ALU.mult).then_inc(h2_ready[bb], 1)
                if ok(1):
                    sides(i, 3)
                    basis(i, 2)
                    low(b_, k_, i, 1)
                    dve.wait_ge(zhi_ready[b_], k_ + 1)
                    dve.scalar_tensor_tensor(f_lo[b_][:, NB, :], zz[:, :], 512.0, f_hi[b_][:, NB, :], ALU.mult, ALU.subtract).then_inc(zlo_ready[b_], 1)
                    basis(i, 3)
                    low(b_, k_, i, 2)
                if ok(-2):
                    dve.wait_ge(ex_ready[b], k)
                    dve.reciprocal(prob[b][:, :], tot[b][:, :]).then_inc(prob_ready[b], 1)
                if ok(1):
                    low(b_, k_, i, 3)
                if ok(-2):
                    dve.wait_ge(prob_ready[b], k)
                    dve.wait_ge(out_stored[b], 16 * (k - 1))
                    dve.tensor_copy(c.prob[:, bass.ds(i - 2, 1)], prob[b][:, :])
                    dve.scalar_tensor_tensor(out0[b][:, :], both[b][:, 1, :], prob[b][:, :], both[b][:, 0, :],
                                             ALU.mult, ALU.add).then_inc(out0_ready[b], 1)
                if ok(-1):
                    dve.wait_ge(logit_done[bb], kk + 1)
                    dve.wait_ge(ex_ready[bb], kk)
                    dve.tensor_tensor(logit[bb][:, :], ps_logit[bb][:, :], c.gate_b[:, :], ALU.add).then_inc(logit_ready[bb], 1)
                    dve.wait_ge(logit_ready[bb], kk + 1)
                    dve.tensor_copy(c.logits[:, bass.ds(i - 1, 1), :].squeeze(1), logit[bb][:, :])
                    dve.tensor_reduce(ntop[bb][:, :], logit[bb][:, :], AX.X, ALU.max, negate=True).then_inc(ntop_ready[bb], 1)

            hot(0, 0, 0)
            steps(dve, step)

def route_phase(nc, m, c):
    with ExitStack() as ctx:
        m = Phase(nc, ctx, "r")
        te = lambda ap: wide(ap.unsqueeze(2), [P, NT, NEXP])
        best = m.sb("best", [P, NT])
        countdown = m.sb("countdown", [P, NEXP])
        points = m.sb("points", [P, NT, NEXP])
        first = m.sb("first", [P, NT])
        route = m.sb("route", [P, NEXP, NT], BF16)
        tri, ones = m.sb("tri", [P, P], BF16), m.sb("ones", [P, P], BF16)
        keep_on = m.sb("keep_on", [P, NEXP, NT])
        totals = m.sb("totals", [P, NEXP, NT])
        upto = m.sb("upto", [P, NEXP, NT])
        before = m.sb("before", [P, NEXP, NT])
        mine = m.sb("mine", [P, NEXP, NT])
        pos, over, expert, place = (m.sb(s, [P, NT]) for s in ("pos", "over", "expert", "place"))
        placei, tilei = m.sb("placei", [P, NT], I32), m.sb("tilei", [P, NT], I32)
        place_tile, place_lane = m.sb("place_tile", [P, NT]), m.sb("place_lane", [P, NT])
        token = m.sb("token", [P, NT])
        lane_hot = [m.sb(f"lane_hot{b}", [P, P]) for b in range(2)]
        values = [m.sb(f"values{b}", [P, 2, FT]) for b in range(2)]
        slots = m.sb("slots", [P, 2, FT])
        empty = m.sb("empty", [P, FT])
        PIECE = 6
        pieces = [(e, min(e + PIECE, NEXP)) for e in range(0, NEXP, PIECE)]
        ps_in = [m.ps(f"ps_in{n}", [P, PIECE, NT]) for n in range(len(pieces))]
        ps_all = [m.ps(f"ps_all{n}", [P, PIECE, NT]) for n in range(len(pieces))]
        ps_slots = m.ps("ps_slots", [P, 2, FT])
        v, made, counted, hot_ready, moved, all_moved = (m.sem("v"), m.sem("made"), m.sem("counted"),
                                                         m.sem("hot_ready", 2), m.sem("moved", 2), m.sem("all_moved"))
        with nc.Block() as block:

            @block.gpsimd
            def _(pool):
                pool.iota(countdown[:, :], [[-1, NEXP]], base=NEXP, channel_multiplier=0, allow_small_or_imprecise_dtypes=True)
                pool.iota(token[:, :], [[P, NT]], base=1, channel_multiplier=1, allow_small_or_imprecise_dtypes=True).then_inc(made, 1)

            @block.vector
            def _(dve):
                n = 0

                def step(ins):
                    nonlocal n
                    ins.then_inc(v, 1)
                    n += 1
                    dve.wait_ge(v, n)

                dve.memset(keep_on[:, :, :], 1.0)
                dve.tensor_copy(tri[:, :], c.tri[:, :])
                dve.tensor_copy(ones[:, :], c.ones[:, :])
                step(dve.tensor_reduce(best[:, :], c.logits[:, :, :], AX.X, ALU.max))
                dve.memset(keep_on[:, :, 0], 0.0)
                step(dve.tensor_tensor(points[:, :, :], c.logits[:, :, :], te(best[:, :]), ALU.is_equal))
                dve.wait_ge(made, 1)
                step(dve.tensor_tensor(points[:, :, :], points[:, :, :], wide(countdown[:, :].unsqueeze(1), [P, NT, NEXP]), ALU.mult))
                step(dve.tensor_reduce(first[:, :], points[:, :, :], AX.X, ALU.max))
                step(dve.tensor_tensor(route[:, :, :].rearrange("p e t -> p t e"), wide(countdown[:, :].unsqueeze(1), [P, NT, NEXP]),
                                       te(first[:, :]), ALU.is_equal))
                dve.wait_ge(counted, 1)
                for q, (e0, e1) in enumerate(pieces):
                    done = dve.tensor_copy(totals[:, e0:e1, :], ps_all[q][:, 0:e1 - e0, :])
                step(done)
                flat = lambda a: a[:, :, :].rearrange("p e t -> p (e t)")
                step(dve.tensor_tensor_scan(flat(upto), flat(keep_on), flat(totals), 0.0, ALU.mult, ALU.add))
                step(dve.tensor_tensor(before[:, :, :], upto[:, :, :], totals[:, :, :], ALU.subtract))
                for q, (e0, e1) in enumerate(pieces):
                    done = dve.tensor_tensor(mine[:, e0:e1, :], ps_in[q][:, 0:e1 - e0, :], before[:, e0:e1, :], ALU.add)
                step(done)
                step(dve.tensor_tensor(mine[:, :, :], mine[:, :, :], route[:, :, :], ALU.mult))
                step(dve.tensor_reduce(pos[:, :], mine[:, :, :].rearrange("p e t -> p t e"), AX.X, ALU.add))
                step(dve.tensor_scalar(over[:, :], pos[:, :], float(CAP), 32768.0, ALU.is_ge, ALU.mult))
                step(dve.tensor_scalar(expert[:, :], first[:, :], -float(ST * P), float(NEXP * ST * P), ALU.mult, ALU.add))
                step(dve.tensor_tensor(place[:, :], pos[:, :], over[:, :], ALU.add))
                step(dve.tensor_tensor(place[:, :], place[:, :], expert[:, :], ALU.add))
                step(dve.tensor_copy(placei[:, :], place[:, :]))
                step(dve.tensor_scalar(tilei[:, :], placei[:, :], 7, None, ALU.logical_shift_right))
                step(dve.tensor_copy(place_tile[:, :], tilei[:, :]))
                step(dve.scalar_tensor_tensor(place_lane[:, :], place_tile[:, :], -float(P), place[:, :], ALU.mult, ALU.add))
                def turn(k):
                    for b in range(2):
                        at = bass.ds(k * 2 + b, 1)
                        dve.wait_ge(moved[b], k)
                        dve.tensor_scalar(lane_hot[b][:, :], c.iota_f[:, :], place_lane[:, at], None, ALU.is_equal)
                        dve.tensor_scalar(values[b][:, 0, :], c.iota_f[:, 0:FT], place_tile[:, at], token[:, at], ALU.is_equal, ALU.mult)
                        dve.tensor_scalar(values[b][:, 1, :], c.iota_f[:, 0:FT], place_tile[:, at], c.prob[:, at],
                                          ALU.is_equal, ALU.mult).then_inc(hot_ready[b], 1)

                turn(0)
                with dve.Fori(1, NT // 2) as k:
                    turn(k)
                dve.wait_ge(all_moved, 1)
                step(dve.tensor_copy(slots[:, :, :], ps_slots[:, :, :]))
                dve.tensor_copy(c.slot_prob[:, :], slots[:, 1, :])
                dve.tensor_scalar(c.slot_read[:, :], slots[:, 0, :], -1.0, 0.0, ALU.add, ALU.max)
                step(dve.tensor_scalar(empty[:, :], slots[:, 0, :], 0.0, float(NP + 1), ALU.is_equal, ALU.mult))
                step(dve.scalar_tensor_tensor(empty[:, :], slots[:, 0, :], -1.0, empty[:, :], ALU.add, ALU.add))
                dve.tensor_copy(c.slot_write[:, :], empty[:, :])

            @block.tensor
            def _(pe):
                pe.wait_ge(v, 5)
                for q, (e0, e1) in enumerate(pieces):
                    pe.matmul(ps_in[q][:, 0:e1 - e0, :], tri[:, :], route[:, e0:e1, :], start=True, stop=True)
                    g = pe.matmul(ps_all[q][:, 0:e1 - e0, :], ones[:, :], route[:, e0:e1, :], start=True, stop=True)
                g.then_inc(counted, 1)
                pe.matmul(ps_slots[:, :, :], c.zrow[:, 0:P], c.zrow[:, 0:2 * FT], start=True, stop=False)
                def turn(k):
                    for b in range(2):
                        pe.wait_ge(hot_ready[b], k + 1)
                        pe.matmul(ps_slots[:, :, :], lane_hot[b][:, :], values[b][:, :, :], start=False, stop=False).then_inc(moved[b], 1)

                turn(0)
                with pe.Fori(1, NT // 2) as k:
                    turn(k)
                pe.matmul(ps_slots[:, :, :], c.zrow[:, 0:P], c.zrow[:, 0:2 * FT], start=False, stop=True).then_inc(all_moved, 1)


def expert_phase(nc, m, c, expert_w, expert_b, both_dram, out):
    U = ST
    with ExitStack() as ctx, nc.Block() as block:
        m = Phase(nc, ctx, "x")
        w = [m.sb(f"w{b}", [P, CH, D]) for b in range(2)]
        w_hi, w_lo = m.sb("w_hi", [P, CH, D], F16), m.sb("w_lo", [P, CH, D], F16)
        bias = m.sb("bias", [P, NEXP, D])
        read = [m.sb(f"read{b}", [P, 1], U32) for b in range(U)]
        write = [m.sb(f"write{b}", [P, 1], U32) for b in range(U)]
        both = [m.sb(f"both{b}", [P, 2 * D]) for b in range(U)]
        hT_hi = [m.sb(f"hT_hi{b}", [P, D], F16) for b in range(2)]
        hT_lo = [m.sb(f"hT_lo{b}", [P, D], F16) for b in range(2)]
        y = [m.sb(f"y{b}", [P, D]) for b in range(2)]
        o = [m.sb(f"o{b}", [P, D]) for b in range(U)]
        tops, topT, bits, scale, unscale = m.sb("tops", [P, 1]), m.sb("topT", [1, 1]), m.sb("bits", [P, 1]), m.sb("scale", [P, 1]), m.sb("unscale", [P, 1])
        ps_t = [m.ps(f"ps_t{b}", [P, D]) for b in range(2)]
        ps_y = [m.ps(f"ps_y{b}", [P, D]) for b in range(2)]
        ps_top = m.ps("ps_top", [P, P])
        bias_loaded, w_loaded = m.sem("bias_loaded"), m.sem("w_loaded")
        index_ready, gathered, stored = m.sem("index_ready", U), swdge(c, U), swdge(c, U)
        top_ready, top_row, topT_ready, top_all, max_ready, bits_ready, recip_ready, scale_ready = (
            m.sem(s) for s in ("top_ready", "top_row", "topT_ready", "top_all", "max_ready", "bits_ready", "recip_ready", "scale_ready"))
        w_high, w_ready = m.sem("w_high"), m.sem("w_ready")
        turned, t_high, t_low, multiplied = m.sem("turned", U), m.sem("t_high", U), m.sem("t_low", U), m.sem("multiplied", U)
        y_ready, o_ready = m.sem("y_ready", U), m.sem("o_ready", U)

        @block.sync
        def _(sp):
            sp.dma_start(bias[:, :, :].rearrange("p e d -> p (e d)"),
                         expert_b.rearrange("(o e) d -> o (e d)", o=1).broadcast_to([P, NEXP * D])).then_inc(bias_loaded, 16)
            w_v = expert_w.rearrange("e (c p) f -> p e c f", p=P)
            sp.dma_start(w[0][:, :, :], w_v[:, 0, :, :]).then_inc(w_loaded, 16)
            def turn(e):
                sp.wait_ge(w_ready, e + 1)
                sp.dma_start(w[0][:, :, :], w_v[:, bass.ds(e + 1, 1), :, :].squeeze(1)).then_inc(w_loaded, 16)

            turn(0)
            with sp.Fori(1, NEXP - 1) as e:
                turn(e)

        @block.gpsimd
        def _(pool):
            def turn(e):
                for b in range(U):
                    pool.wait_ge(o_ready[b], e)
                    pool.wait_ge(stored[b], 16 * e)
                    pool.tensor_copy(read[b][:, :], c.slot_read[:, bass.ds(e * ST + b, 1)])
                    pool.tensor_copy(write[b][:, :], c.slot_write[:, bass.ds(e * ST + b, 1)]).then_inc(index_ready[b], 1)
                for b in range(U):
                    pool.wait_ge(index_ready[b], e + 1)
                    pool.nop(nofuse=True)
                    pool.indirect_dma_start(both[b][:, :], None, both_dram,
                                            bass.IndirectOffsetOnAxis(read[b][:, :], 0)).then_inc(gathered[b], 16)
                for b in range(U):
                    pool.wait_ge(o_ready[b], e + 1)
                    pool.nop(nofuse=True)
                    pool.indirect_dma_start(out, bass.IndirectOffsetOnAxis(write[b][:, :], 0), o[b][:, :], None,
                                            bounds_check=NP - 1, oob_is_err=False).then_inc(stored[b], 16)

            turn(0)
            with pool.Fori(1, NEXP) as e:
                turn(e)
            for b in range(U):
                pool.wait_ge(stored[b], 16 * NEXP)

        @block.tensor
        def _(pe):
            def turn(e):
                pe.wait_ge(top_ready, e + 1)
                pe.transpose(ps_top[0:1, 0:P], tops[:, :], c.ident[:, :]).then_inc(top_row, 1)
                pe.wait_ge(topT_ready, e + 1)
                pe.matmul(ps_top[:, 0:1], c.ones[0:1, :], topT[:, :], start=True, stop=True).then_inc(top_all, 1)
                for b in range(U + 1):
                    if b < U:
                        pe.wait_ge(gathered[b], 16 * (e + 1))
                        pe.wait_ge(t_low[(b - 2) % U], e + 1 if b >= 2 else e)
                        for ch in range(CH):
                            g = pe.transpose(ps_t[b % 2][:, ch * P:(ch + 1) * P], both[b][:, D + ch * P:D + (ch + 1) * P], c.ident[:, :])
                        g.then_inc(turned[b], 1)
                    if b >= 1:
                        q = b - 1
                        pe.wait_ge(w_ready, e + 1)
                        pe.wait_ge(t_low[q], e + 1)
                        pe.wait_ge(y_ready[(q - 2) % U], e + 1 if q >= 2 else e)
                        for ch in range(CH):
                            for part, (lhs, rhs) in enumerate(((hT_hi, w_hi), (hT_hi, w_lo), (hT_lo, w_hi))):
                                g = pe.matmul(ps_y[q % 2][:, :], lhs[q % 2][:, ch * P:(ch + 1) * P], rhs[:, ch, :],
                                              start=ch == 0 and part == 0, stop=ch == CH - 1 and part == 2)
                        g.then_inc(multiplied[q], 1)

            turn(0)
            with pe.Fori(1, NEXP) as e:
                turn(e)

        @block.scalar
        def _(act):
            def turn(e):
                act.wait_ge(scale_ready, e + 1)
                act.wait_ge(multiplied[U - 1], e)
                act.activation(w_hi[:, :, :], w[0][:, :, :], ACT.Copy, scale=scale[:, :]).then_inc(w_high, 1)
                for b in range(U):
                    act.wait_ge(turned[b], e + 1)
                    act.wait_ge(multiplied[(b - 2) % U], e + 1 if b >= 2 else e)
                    act.activation(hT_hi[b % 2][:, :], ps_t[b % 2][:, :], ACT.Copy, scale=1024.0).then_inc(t_high[b], 1)

            turn(0)
            with act.Fori(1, NEXP) as e:
                turn(e)

        @block.vector
        def _(dve):
            dve.wait_ge(bias_loaded, 16)
            def turn(e):
                dve.wait_ge(w_loaded, 16 * (e + 1))
                dve.tensor_reduce(tops[:, :], w[0][:, :, :], AX.XY, ALU.max, apply_absolute_value=True).then_inc(top_ready, 1)
                dve.wait_ge(top_row, e + 1)
                dve.tensor_reduce(topT[:, :], ps_top[0:1, 0:P], AX.X, ALU.max).then_inc(topT_ready, 1)
                dve.wait_ge(top_all, e + 1)
                dve.tensor_scalar(bits[:, :], ps_top[:, 0:1], 1e-30, None, ALU.max).then_inc(max_ready, 1)
                dve.wait_ge(max_ready, e + 1)
                dve.tensor_scalar(bits[:, :].bitcast(I32), bits[:, :].bitcast(I32), 0x7F800000, None, ALU.bitwise_and).then_inc(bits_ready, 1)
                dve.wait_ge(bits_ready, e + 1)
                dve.tensor_scalar(unscale[:, :], bits[:, :], 2.0 ** -23, None, ALU.mult)
                dve.reciprocal(scale[:, :], bits[:, :]).then_inc(recip_ready, 1)
                dve.wait_ge(recip_ready, e + 1)
                dve.tensor_scalar(scale[:, :], scale[:, :], 2.0 ** 13, None, ALU.mult).then_inc(scale_ready, 1)
                dve.wait_ge(w_high, e + 1)
                dve.scalar_tensor_tensor(w_lo[:, :, :], w[0][:, :, :], scale[:, :], w_hi[:, :, :], ALU.mult, ALU.subtract).then_inc(w_ready, 1)
                for b in range(U + 2):
                    if b < U:
                        dve.wait_ge(t_high[b], e + 1)
                        dve.scalar_tensor_tensor(hT_lo[b % 2][:, :], ps_t[b % 2][:, :], 1024.0, hT_hi[b % 2][:, :],
                                                 ALU.mult, ALU.subtract).then_inc(t_low[b], 1)
                    if 1 <= b <= U:
                        q = b - 1
                        dve.wait_ge(multiplied[q], e + 1)
                        dve.wait_ge(o_ready[(q - 2) % U], e + 1 if q >= 2 else e)
                        dve.scalar_tensor_tensor(y[q % 2][:, :], ps_y[q % 2][:, :], unscale[:, :], bias[:, bass.ds(e, 1), :].squeeze(1),
                                                 ALU.mult, ALU.add).then_inc(y_ready[q], 1)
                    if b >= 2:
                        q = b - 2
                        dve.wait_ge(y_ready[q], e + 1)
                        dve.wait_ge(stored[q], 16 * e)
                        dve.scalar_tensor_tensor(o[q][:, :], y[q % 2][:, :], c.slot_prob[:, bass.ds(e * ST + q, 1)], both[q][:, 0:D],
                                                 ALU.mult, ALU.add).then_inc(o_ready[q], 1)

            turn(0)
            with dve.Fori(1, NEXP) as e:
                turn(e)


class Consts:
    pass


def build(nc, x, row, col, wt, a2, base_w, spline_w, switch_w, switch_b, expert_w, expert_b, out):
    with ExitStack() as ctx:
        m = Phase(nc, ctx, "g")
        c = Consts()
        c.iota_f, c.iota_p = m.sb("iota_f", [P, P]), m.sb("iota_p", [P, 1])
        c.ones, c.ident, c.tri, c.after = (m.sb(s, [P, P]) for s in ("ones", "ident", "tri", "after"))
        c.swdge = m.sem("swdge", 7 + 2 + 2 * ST)
        c.st = m.sb("st", [P, 2, NT])
        h_dram = nc.dram_tensor("h_dram", [NP, D], F32, kind="Internal").ap()
        constants(nc, m, c)
        node_phase(nc, m, c, x, wt, a2, h_dram)
        if True:
            row_dram = nc.dram_tensor("row_dram", [ET, P], F32, kind="Internal").ap()
            c.zrow = m.sb("zrow", [1, 3 * P])
            c.last_edge = m.sb("last_edge", [P, NT], U32)
            c.sorted = m.sb("sorted", [ET, 3, P])
            c.row_l, c.att_l, c.col_l = m.sb("row_l", [P, ET]), m.sb("att_l", [P, ET]), m.sb("col_l", [P, ET], U32)
            c.run_on = m.sb("run_on", [ET, 1])
            with nc.Block() as block:
                @block.gpsimd
                def _(pool):
                    pool.memset(c.zrow[:, :], 0.0)
            sort_phase(nc, m, c, row, col)
            softmax_phase(nc, m, c, row_dram)
        if True:
            part_dram = nc.dram_tensor("part_dram", [EP + P, D], F32, kind="Internal").ap()
            c.ends = m.sb("ends", [ET, D])
            edge_phase(nc, m, c, h_dram, row_dram, part_dram)
        if True:
            both_dram = nc.dram_tensor("both_dram", [NP, 2 * D], F32, kind="Internal").ap()
            c.logits, c.prob = m.sb("logits", [P, NT, NEXP]), m.sb("prob", [P, NT])
            c.gate_w, c.gate_b, c.mid = m.sb("gate_w", [P, CH, NEXP]), m.sb("gate_b", [P, NEXP]), m.sb("mid", [P, NB])
            c.scale, c.unscale = m.sb("scale", [P, 1]), m.sb("unscale", [P, 1])
            with ExitStack() as wctx:
                mw = Phase(nc, wctx, "ww")
                c.w_hi, c.w_lo = mw.sb("w_hi", [P, CH, NF, D], F16), mw.sb("w_lo", [P, CH, NF, D], F16)
                with nc.Block() as block:
                    s = m.sem("gate_loaded")

                    @block.sync
                    def _(sp):
                        sp.dma_start(c.gate_w[:, :, :], switch_w.rearrange("(c p) e -> p c e", p=P)).then_inc(s, 16)
                        sp.dma_start(c.gate_b[:, :], switch_b.broadcast_to([P, NEXP])).then_inc(s, 16)
                        sp.wait_ge(s, 32)

                    @block.gpsimd
                    def _(pool):
                        pool.iota(c.mid[:, :], [[-8, NB]], base=28, channel_multiplier=0, allow_small_or_imprecise_dtypes=True)
                weight_phase(nc, m, c, base_w, spline_w)
                layer_phase(nc, m, c, x, part_dram, both_dram, out)
            if True:
                c.slot_read, c.slot_write, c.slot_prob = m.sb("slot_read", [P, FT], U32), m.sb("slot_write", [P, FT], U32), m.sb("slot_prob", [P, FT])
                route_phase(nc, m, c)
                expert_phase(nc, m, c, expert_w, expert_b, both_dram, out)


def kernel(x, src, dst, L0_gnn_W, L0_gnn_a, L0_gnn_base_w, L0_gnn_spline_w, L0_ffn_switch_w,
           L0_ffn_switch_b, L0_ffn_expert_w, L0_ffn_expert_b):
    import numpy as np
    import concourse.bacc as bacc
    from concourse.bass_utils import run_bass_kernel_spmd as run

    lay = np.ascontiguousarray
    pad = EP - N_EDGES
    arrays = {
        "x": np.concatenate([x, np.zeros((NP - N_NODES, D), np.float32)]),
        "row": np.concatenate([src, np.full((pad,), PAD_ROW, np.int32)]).reshape(ET, P),
        "col": np.concatenate([dst, np.zeros((pad,), np.int32)]).reshape(ET, P),
        "wt": lay(np.transpose(L0_gnn_W)),
        "a2": lay(np.transpose(np.reshape(L0_gnn_a, (2, D)))),
        "base_w": lay(np.transpose(L0_gnn_base_w)),
        "spline_w": lay(np.transpose(L0_gnn_spline_w, (1, 2, 0))),
        "switch_w": lay(np.transpose(L0_ffn_switch_w)),
        "switch_b": np.reshape(L0_ffn_switch_b, (1, NEXP)),
        "expert_w": lay(np.transpose(L0_ffn_expert_w, (0, 2, 1))),
        "expert_b": lay(L0_ffn_expert_b),
    }
    nc = bacc.Bacc("TRN2", target_bir_lowering=False, num_devices=1)
    args = [nc.dram_tensor(f"in_{k}", a.shape, mybir.dt.from_np(a.dtype), kind="ExternalInput").ap()
            for k, a in arrays.items()]
    out = nc.dram_tensor("out_0", (NP, D), F32, kind="ExternalOutput").ap()
    build(nc, *args, out)
    r = run(nc, [{f"in_{k}": a for k, a in arrays.items()}], core_ids=[0])
    return r.results[0]["out_0"][:N_NODES]
```

```python
from contextlib import ExitStack

import concourse.bass as bass
from concourse import mybir

P = 128
N_NODES, D, N_EDGES = 10000, 512, 12500
CH = D // P
NT = 80
NP = NT * P
LT = -(-N_NODES // P)
ET = 98
EP = ET * P
PAD_ROW = NP - 1
NB = 8
NF = NB + 1
NEXP, CAP = 16, int(1.2 * N_NODES / 16)
ST = -(-CAP // P)
FT = NEXP * ST
EPS = 1e-5
BIG = 1e30
ALPHA = 0.2

F32, BF16, F16 = mybir.dt.float32, mybir.dt.bfloat16, mybir.dt.float16
I32, U32 = mybir.dt.int32, mybir.dt.uint32
ALU = mybir.AluOpType
ACT = mybir.ActivationFunctionType
AX = mybir.AxisListType


def wide(ap, shape):
    return ap.broadcast_to(shape)


class Phase:

    def __init__(self, nc, ctx, tag):
        self.nc, self.ctx, self.tag, self.sems = nc, ctx, tag, []
        ctx.callback(self.reset)

    def reset(self):
        with self.nc.Block() as block:

            @block.gpsimd
            def _(pool):
                for s in self.sems:
                    pool.sem_clear(s)

    def sb(self, name, shape, dt=F32):
        return self.ctx.enter_context(self.nc.sbuf_tensor(f"{self.tag}_{name}", shape, dt))

    def ps(self, name, shape, dt=F32):
        return self.ctx.enter_context(self.nc.psum_tensor(f"{self.tag}_{name}", shape, dt))

    def sem(self, name, n=None):
        def one(s):
            self.sems.append(self.ctx.enter_context(self.nc.semaphore(f"{self.tag}_{s}")))
            return self.sems[-1]

        return one(name) if n is None else [one(f"{name}{i}") for i in range(n)]


def swdge(c, n):
    return [c.swdge.pop() for _ in range(n)]


def constants(nc, m, c):
    with nc.Block() as block:
        ramp, cleared = m.sem("c_ramp"), m.sem("c_cleared")

        @block.gpsimd
        def _(pool):
            pool.iota(c.iota_f[:, :], [[1, P]], base=0, channel_multiplier=0,
                      allow_small_or_imprecise_dtypes=True)
            pool.iota(c.iota_p[:, :], [[0, 1]], base=0, channel_multiplier=1,
                      allow_small_or_imprecise_dtypes=True)
            pool.memset(c.ones[:, :], 1.0).then_inc(ramp, 1)
            pool.memset(c.ident[:, :], 0.0).then_inc(cleared, 1)
            pool.memset(c.tri[:, :], 0.0).then_inc(cleared, 1)
            pool.memset(c.after[:, :], 0.0).then_inc(cleared, 1)
            pool.wait_ge(cleared, 3)
            pool.affine_select(out=c.ident[:, :], in_=c.ident[:, :], compare_op=ALU.not_equal, fill=1.0,
                               base=0, pattern=[[-1, P]], channel_multiplier=1)
            pool.affine_select(out=c.tri[:, :], in_=c.tri[:, :], compare_op=ALU.is_ge, fill=1.0,
                               base=0, pattern=[[-1, P]], channel_multiplier=1)
            pool.affine_select(out=c.after[:, :], in_=c.after[:, :], compare_op=ALU.is_ge, fill=1.0,
                               base=0, pattern=[[1, P]], channel_multiplier=-1)


def node_phase(nc, m, c, x, wt, a2, h_dram):
    U = 4
    with ExitStack() as ctx, nc.Block() as block:
        m = Phase(nc, ctx, "n")
        xt = [m.sb(f"x{b}", [P, D]) for b in range(U)]
        ht = [m.sb(f"h{b}", [P, D]) for b in range(U)]
        hT = [m.sb(f"hT{b}", [P, CH, P]) for b in range(U)]
        wt_sb = m.sb("wt", [P, CH, D])
        a_sb = m.sb("a", [P, CH, 2])
        wa = m.sb("wa", [P, CH, 2])
        stats = m.sb("stats", [P, U, 6])
        mv = m.sb("mv", [P, U, 2])
        ve = m.sb("ve", [P, U])
        rstd = m.sb("rstd", [P, U])
        mhalf = m.sb("mhalf", [P, U])
        psT = [m.ps(f"psT{b}", [P, CH, P]) for b in range(2)]
        psS = [m.ps(f"psS{b}", [P, 2]) for b in range(U)]
        psW = m.ps("psW", [P, CH, 2])
        w_loaded, wa_mm, wa_ready, half = m.sem("w_loaded"), m.sem("wa_mm"), m.sem("wa_ready"), m.sem("half")
        x_loaded, h_stored = m.sem("x_loaded", U), m.sem("h_stored", U)
        bn_done, stats_ready, ve_ready, rstd_ready = (m.sem(s) for s in ("bn_done", "stats_ready", "ve_ready", "rstd_ready"))
        h_ready, hT_done = m.sem("h_ready"), m.sem("hT_done", U)
        hT_copied, st_done, st_copied = m.sem("hT_copied", U), m.sem("st_done", U), m.sem("st_copied", U)
        x_t = x.rearrange("(t p) d -> t p d", p=P)
        h_t = h_dram.rearrange("(t p) d -> t p d", p=P)
        K = NT // U

        @block.sync
        def _(sp):
            sp.dma_start(wt_sb[:, :, :], wt.rearrange("(c p) i -> p c i", p=P)).then_inc(w_loaded, 16)
            sp.dma_start(a_sb[:, :, :], a2.rearrange("(c p) k -> p c k", p=P)).then_inc(w_loaded, 16)
            for b in range(U):
                sp.dma_start(xt[b][:, :], x_t[b, :, :]).then_inc(x_loaded[b], 16)

            def turn(k, last):
                for b in range(U):
                    sp.wait_ge(h_ready, k * U + b + 1)
                    sp.dma_start(h_t[k * U + b, :, :], ht[b][:, :]).then_inc(h_stored[b], 16)
                    if not last:
                        sp.dma_start(xt[b][:, :], x_t[k * U + U + b, :, :]).then_inc(x_loaded[b], 16)

            turn(0, False)
            with sp.Fori(1, K - 1) as k:
                turn(k, False)
            turn(K - 1, True)
            for b in range(U):
                sp.wait_ge(h_stored[b], 16 * K)

        @block.vector
        def _(dve):
            def turn(k):
                for b in range(U):
                    dve.wait_ge(x_loaded[b], 16 * (k + 1))
                    dve.bn_stats(stats[:, b, :], xt[b][:, :]).then_inc(bn_done, 1)
                for b in range(U):
                    dve.wait_ge(bn_done, U * k + b + 1)
                    dve.nop(nofuse=True)
                    dve.bn_aggr(mv[:, b, :], stats[:, b, :]).then_inc(stats_ready, 1)
                for b in range(U):
                    dve.wait_ge(rstd_ready, k + 1)
                    dve.wait_ge(h_stored[b], 16 * k)
                    dve.wait_ge(hT_done[b], k)
                    dve.tensor_scalar(ht[b][:, :], xt[b][:, :], mv[:, b, 0:1], rstd[:, b:b + 1],
                                      ALU.subtract, ALU.mult).then_inc(h_ready, 1)

            turn(0)
            with dve.Fori(1, K) as k:
                turn(k)

        @block.gpsimd
        def _(pool):
            pool.memset(mhalf[:, :], -0.5).then_inc(half, 1)
            pool.wait_ge(half, 1)
            def turn(k):
                pool.wait_ge(stats_ready, U * (k + 1))
                pool.wait_ge(h_ready, U * k)
                pool.nop(nofuse=True)
                pool.tensor_scalar(ve[:, :], mv[:, :, 1], EPS, None, ALU.add).then_inc(ve_ready, 1)
                pool.wait_ge(ve_ready, k + 1)
                pool.tensor_tensor(rstd[:, :], ve[:, :], mhalf[:, :], ALU.pow).then_inc(rstd_ready, 1)

            turn(0)
            with pool.Fori(1, K) as k:
                turn(k)

        @block.tensor
        def _(pe):
            pe.wait_ge(w_loaded, 32)
            for ci in range(CH):
                for co in range(CH):
                    mm = pe.matmul(psW[:, ci, :], wt_sb[:, co, ci * P:(ci + 1) * P], a_sb[:, co, :],
                                   start=co == 0, stop=co == CH - 1)
            mm.then_inc(wa_mm, 1)
            pe.wait_ge(wa_ready, 1)

            def turn(k):
                for b in range(U + 1):
                    if b < U:
                        pe.wait_ge(h_ready, k * U + b + 1)
                        pe.wait_ge(hT_copied[(b - 2) % U], k + 1 if b >= 2 else k)
                        for ch in range(CH):
                            t = pe.transpose(psT[b % 2][:, ch, :], ht[b][:, ch * P:(ch + 1) * P], c.ident[:, :])
                        t.then_inc(hT_done[b], 1)
                    if b >= 1:
                        pe.wait_ge(hT_copied[b - 1], k + 1)
                        pe.wait_ge(st_copied[b - 1], k)
                        for ch in range(CH):
                            mm = pe.matmul(psS[b - 1][:, :], hT[b - 1][:, ch, :], wa[:, ch, :],
                                           start=ch == 0, stop=ch == CH - 1)
                        mm.then_inc(st_done[b - 1], 1)

            turn(0)
            with pe.Fori(1, K) as k:
                turn(k)

        @block.scalar
        def _(act):
            act.wait_ge(wa_mm, 1)
            act.copy(wa[:, :, :], psW[:, :, :]).then_inc(wa_ready, 1)
            def turn(k):
                for b in range(U + 1):
                    if b < U:
                        act.wait_ge(hT_done[b], k + 1)
                        act.wait_ge(st_done[b], k)
                        act.copy(hT[b][:, :, :], psT[b % 2][:, :, :]).then_inc(hT_copied[b], 1)
                    if b >= 1:
                        act.wait_ge(st_done[b - 1], k + 1)
                        act.copy(c.st[:, :, bass.ds(k * U + b - 1, 1)].rearrange("p a b -> p (a b)"),
                                 psS[b - 1][:, :]).then_inc(st_copied[b - 1], 1)

            turn(0)
            with act.Fori(1, K) as k:
                turn(k)


def sort_phase(nc, m, c, row, col):
    U = 2
    K = ET // U
    with ExitStack() as ctx:
        m = Phase(nc, ctx, "s")
        rowb = m.sb("rowb", [P, ET, P], I32)
        lowb = m.sb("lowb", [P, ET // 2, P], I32)
        row_low = m.sb("row_low", [P, ET, P], BF16)
        col_low = m.sb("col_low", [P, ET, P], BF16)
        nat = m.sb("nat", [ET, 2, P], I32)
        natf = m.sb("natf", [ET, 2, P])
        rc = m.sb("rc", [P, 2, ET])
        rci = m.sb("rci", [P, 2, ET], I32)
        lowi = m.sb("lowi", [P, 2, ET], I32)
        low = m.sb("low", [P, 2, ET])
        high = m.sb("high", [P, 2, ET])
        one_low = m.sb("one_low", [P, ET, P], BF16)
        one_high = m.sb("one_high", [P, ET, 2, NT], BF16)
        count = m.sb("count", [P, NT])
        start = m.sb("start", [P, NT])
        base = m.sb("base", [P, NT])
        zeros = m.sb("zeros", [P, NT])
        some = m.sb("some", [P, NT])
        last = m.sb("last", [P, NT])
        running = m.sb("running", [P, U, NT])
        row_hotT = m.sb("row_hotT", [P, U, P])
        col_hotT = m.sb("col_hotT", [P, U, P])
        junk = m.sb("junk", [P, U, P + 3 * NT])
        rank = m.sb("rank", [P, ET])
        first = m.sb("first", [P, ET])
        score = m.sb("score", [P, ET])
        pos = m.sb("pos", [P, ET])
        posi = m.sb("posi", [P, ET], I32)
        poshi = m.sb("poshi", [P, ET], I32)
        pos_tile = m.sb("pos_tile", [P, ET])
        pos_lane = m.sb("pos_lane", [P, ET])
        tile_hot = [m.sb(f"tile_hot{b}", [P, ET]) for b in range(U)]
        values = [m.sb(f"values{b}", [P, 3, P]) for b in range(U)]
        psC = m.ps("psC", [P, NT])
        psX = m.ps("psX", [P, 2, P])
        psH = [m.ps(f"psH{b}", [P, NT]) for b in range(U)]
        psG = [m.ps(f"psG{b}", [P, 3, NT]) for b in range(U)]
        psV = m.ps("psV", [ET, 3, P])
        step = m.sem("step")
        row_bc, col_bc, nat_loaded = m.sem("row_bc"), m.sem("col_bc"), m.sem("nat_loaded")
        low_ready, low_copied = m.sem("low_ready"), m.sem("low_copied")

        with nc.Block() as block:
            turned, counted, summed = m.sem("turned"), m.sem("counted"), m.sem("summed")

            @block.sync
            def _(sp):
                flat = lambda a: a.rearrange("(o t) p -> o (t p)", o=1).broadcast_to([P, EP])
                sp.dma_start(nat[:, 0, :], row).then_inc(nat_loaded, 16)
                sp.dma_start(nat[:, 1, :], col).then_inc(nat_loaded, 16)
                sp.dma_start(rowb[:, :, :].rearrange("p t e -> p (t e)"), flat(row)).then_inc(row_bc, 16)
                for half in range(2):
                    sp.wait_ge(low_copied, 2 + half)
                    sp.dma_start(lowb[:, :, :].rearrange("p t e -> p (t e)"),
                                 flat(col)[:, half * EP // 2:(half + 1) * EP // 2]).then_inc(col_bc, 16)

            @block.vector
            def _(dve):
                dve.wait_ge(nat_loaded, 32)
                dve.tensor_copy(natf[:, :, :], nat[:, :, :]).then_inc(step, 1)
                dve.memset(zeros[:, :], 0.0)
                dve.wait_ge(turned, 1)
                dve.tensor_copy(rc[:, :, :], psX[:, :, 0:ET]).then_inc(step, 1)
                dve.wait_ge(step, 2)
                dve.tensor_copy(rci[:, :, :], rc[:, :, :]).then_inc(step, 1)
                dve.wait_ge(step, 3)
                dve.tensor_scalar(lowi[:, :, :], rci[:, :, :], P - 1, None, ALU.bitwise_and).then_inc(step, 1)
                dve.wait_ge(step, 4)
                dve.tensor_copy(low[:, :, :], lowi[:, :, :]).then_inc(step, 1)
                dve.wait_ge(step, 5)
                dve.tensor_tensor(high[:, :, :], rc[:, :, :], low[:, :, :], ALU.subtract).then_inc(step, 1)
                dve.wait_ge(step, 6)
                dve.tensor_scalar(high[:, :, :], high[:, :, :], 1.0 / P, None, ALU.mult).then_inc(step, 1)
                dve.wait_ge(step, 7)
                dve.tensor_tensor(one_low[:, :, :], wide(c.iota_f[:, :].unsqueeze(1), [P, ET, P]),
                                  wide(low[:, 0, :].unsqueeze(2), [P, ET, P]), ALU.is_equal)
                for k in range(2):
                    dve.tensor_tensor(one_high[:, :, k, :], wide(c.iota_f[:, 0:NT].unsqueeze(1), [P, ET, NT]),
                                      wide(high[:, k, :].unsqueeze(2), [P, ET, NT]), ALU.is_equal).then_inc(step, 1)
                dve.wait_ge(row_bc, 16)
                for half in range(2):
                    dve.wait_ge(low_copied, half)
                    dve.tensor_scalar(lowb[:, :, :], rowb[:, half * ET // 2:(half + 1) * ET // 2, :], P - 1, None,
                                      ALU.bitwise_and).then_inc(low_ready, 1)
                for half in range(2):
                    dve.wait_ge(col_bc, 16 * (half + 1))
                    dve.tensor_scalar(lowb[:, :, :], lowb[:, :, :], P - 1, None, ALU.bitwise_and).then_inc(low_ready, 1)
                dve.wait_ge(counted, 1)
                dve.tensor_copy(count[:, :], psC[:, :]).then_inc(step, 1)
                dve.wait_ge(summed, 1)
                dve.tensor_tensor_scan(base[:, :], psX[:, 0, 0:NT], zeros[:, :], 0.0, ALU.add, ALU.add).then_inc(step, 1)
                dve.wait_ge(step, 11)
                dve.tensor_tensor(base[:, :], base[:, :], psX[:, 0, 0:NT], ALU.subtract).then_inc(step, 1)
                dve.wait_ge(step, 12)
                dve.tensor_tensor(start[:, :], psX[:, 1, 0:NT], base[:, :], ALU.add).then_inc(step, 1)
                dve.tensor_scalar(some[:, :], count[:, :], 0.0, None, ALU.is_gt).then_inc(step, 1)
                dve.wait_ge(step, 14)
                dve.tensor_copy(running[:, 0, :], start[:, :])
                dve.tensor_tensor(last[:, :], start[:, :], count[:, :], ALU.add).then_inc(step, 1)
                dve.wait_ge(step, 15)
                dve.scalar_tensor_tensor(last[:, :], last[:, :], -1.0 - EP, some[:, :], ALU.add, ALU.mult).then_inc(step, 1)
                dve.wait_ge(step, 16)
                dve.tensor_scalar(c.last_edge[:, :], last[:, :], float(EP), None, ALU.add)

            @block.scalar
            def _(act):
                for n in range(4):
                    half = n % 2
                    act.wait_ge(low_ready, n + 1)
                    act.copy((row_low, col_low)[n // 2][:, half * ET // 2:(half + 1) * ET // 2, :],
                             lowb[:, :, :]).then_inc(low_copied, 1)

            @block.tensor
            def _(pe):
                pe.wait_ge(step, 1)
                pe.transpose(psX[:, 0, 0:ET], natf[:, 0, :], c.ident[0:ET, 0:ET])
                pe.transpose(psX[:, 1, 0:ET], natf[:, 1, :], c.ident[0:ET, 0:ET]).then_inc(turned, 1)
                pe.wait_ge(step, 9)
                pe.matmul(psC[:, :], one_low[:, 0, :], one_high[:, 0, 0, :], start=True, stop=False)
                with pe.Fori(1, ET - 1) as t:
                    pe.matmul(psC[:, :], one_low[:, bass.ds(t, 1), :].squeeze(1),
                              one_high[:, bass.ds(t, 1), 0, :].squeeze(1), start=False, stop=False)
                pe.matmul(psC[:, :], one_low[:, ET - 1, :], one_high[:, ET - 1, 0, :], start=False, stop=True).then_inc(counted, 1)
                pe.wait_ge(step, 10)
                pe.matmul(psX[:, 0, 0:NT], c.ones[:, :], count[:, :], start=True, stop=True)
                pe.matmul(psX[:, 1, 0:NT], c.tri[:, :], count[:, :], start=True, stop=True).then_inc(summed, 1)

        with nc.Block() as block:
            hist_done, hist_added, hots_ready = m.sem("hist_done", U), m.sem("hist_added", U), m.sem("hots_ready", U)
            looked_up, picked = m.sem("looked_up", U), m.sem("picked", U)

            @block.tensor
            def _(pe):
                def turn(k):
                    for b in range(U):
                        t = k * U + b
                        pe.wait_ge(hist_added[b], k)
                        pe.matmul(psH[b][:, :], one_low[:, bass.ds(t, 1), :].squeeze(1),
                                  one_high[:, bass.ds(t, 1), 0, :].squeeze(1), start=True, stop=True).then_inc(hist_done[b], 1)
                        pe.wait_ge(hots_ready[b], k + 1)
                        pe.wait_ge(picked[b], k)
                        pe.matmul(psG[b][:, 0, :], row_hotT[:, b, :], running[:, b, :], start=True, stop=True)
                        pe.matmul(psG[b][:, 1, :], row_hotT[:, b, :], c.st[:, 0, :], start=True, stop=True)
                        pe.matmul(psG[b][:, 2, :], col_hotT[:, b, :], c.st[:, 1, :], start=True, stop=True).then_inc(looked_up[b], 1)

                turn(0)
                with pe.Fori(1, K) as k:
                    turn(k)

            @block.vector
            def _(dve):
                def turn(k):
                    for b in range(U):
                        t = k * U + b
                        at = bass.ds(t, 1)
                        dve.wait_ge(looked_up[b], k)
                        dve.tensor_scalar(row_hotT[:, b, :], row_low[:, at, :].squeeze(1), c.iota_p[:, :], None, ALU.is_equal)
                        dve.tensor_scalar(col_hotT[:, b, :], col_low[:, at, :].squeeze(1), c.iota_p[:, :], None,
                                          ALU.is_equal).then_inc(hots_ready[b], 1)
                        dve.wait_ge(hist_done[b], k + 1)
                        dve.scalar_tensor_tensor(junk[:, b, 0:P], rowb[:, at, :].squeeze(1), rc[:, 0, at], c.after[:, :],
                                                 ALU.is_equal, ALU.mult, accum_out=rank[:, at])
                        dve.wait_ge(looked_up[1 - b], k + b)
                        dve.wait_ge(hist_added[1 - b], k + b)
                        dve.tensor_tensor(running[:, 1 - b, :], running[:, b, :], psH[b][:, :], ALU.add).then_inc(hist_added[b], 1)
                        dve.wait_ge(looked_up[b], k + 1)
                        dve.scalar_tensor_tensor(junk[:, b, P:P + NT], psG[b][:, 0, :], 1.0, one_high[:, at, 0, :].squeeze(1),
                                                 ALU.mult, ALU.mult, accum_out=first[:, at])
                        dve.scalar_tensor_tensor(junk[:, b, P + NT:].rearrange("p (a n) -> p a n", a=2), psG[b][:, 1:3, :], 1.0,
                                                 one_high[:, at, :, :].squeeze(1), ALU.mult, ALU.mult,
                                                 accum_out=score[:, at]).then_inc(picked[b], 1)

                turn(0)
                with dve.Fori(1, K) as k:
                    turn(k)

        with nc.Block() as block:
            hot_ready, moved, all_moved = m.sem("hot_ready", U), m.sem("moved", U), m.sem("all_moved")
            s3 = m.sem("s3")

            @block.vector
            def _(dve):
                dve.tensor_tensor(pos[:, :], first[:, :], rank[:, :], ALU.add).then_inc(s3, 1)
                dve.wait_ge(s3, 1)
                dve.tensor_copy(posi[:, :], pos[:, :]).then_inc(s3, 1)
                dve.wait_ge(s3, 2)
                dve.tensor_scalar(poshi[:, :], posi[:, :], 7, None, ALU.logical_shift_right).then_inc(s3, 1)
                dve.wait_ge(s3, 3)
                dve.tensor_copy(pos_tile[:, :], poshi[:, :]).then_inc(s3, 1)
                dve.wait_ge(s3, 4)
                dve.scalar_tensor_tensor(pos_lane[:, :], pos_tile[:, :], -float(P), pos[:, :], ALU.mult, ALU.add).then_inc(s3, 1)
                dve.wait_ge(s3, 5)
                def turn(k):
                    for b in range(U):
                        at = bass.ds(k * U + b, 1)
                        dve.wait_ge(moved[b], k)
                        dve.tensor_scalar(tile_hot[b][:, :], c.iota_f[:, 0:ET], pos_tile[:, at], None, ALU.is_equal)
                        for v, value in enumerate((rc[:, 0, at], rc[:, 1, at], score[:, at])):
                            done = dve.tensor_scalar(values[b][:, v, :], c.iota_f[:, :], pos_lane[:, at], value,
                                                     ALU.is_equal, ALU.mult)
                        done.then_inc(hot_ready[b], 1)

                turn(0)
                with dve.Fori(1, K) as k:
                    turn(k)
                dve.wait_ge(all_moved, 1)
                dve.tensor_copy(c.sorted[:, :, :], psV[:, :, :])

            @block.tensor
            def _(pe):
                pe.matmul(psV[:, :, :], zeros_row(c)[:, 0:ET], zeros_row(c)[:, :], start=True, stop=False)
                def turn(k):
                    for b in range(U):
                        pe.wait_ge(hot_ready[b], k + 1)
                        pe.matmul(psV[:, :, :], tile_hot[b][:, :], values[b][:, :, :], start=False, stop=False).then_inc(moved[b], 1)

                turn(0)
                with pe.Fori(1, K) as k:
                    turn(k)
                pe.matmul(psV[:, :, :], zeros_row(c)[:, 0:ET], zeros_row(c)[:, :], start=False, stop=True).then_inc(all_moved, 1)


def zeros_row(c):
    return c.zrow[:, :]


def softmax_phase(nc, m, c, row_dram):
    with ExitStack() as ctx:
        m = Phase(nc, ctx, "a")
        row, col, score = c.sorted[:, 0, :], c.sorted[:, 1, :], c.sorted[:, 2, :]
        e, ex, tot = (m.sb(s, [ET, P]) for s in ("e", "ex", "tot"))
        row1 = m.sb("row1", [ET, P])
        near = m.sb("near", [ET, 2, P])
        same = m.sb("same", [ET, 2, P])
        wall = m.sb("wall", [ET, 2, P])
        through = m.sb("through", [ET, 2, 2])
        scan = m.sb("scan", [ET, 2, P])
        ends = m.sb("ends", [1, 4, ET])
        carried = m.sb("carried", [1, 2, P])
        carry = m.sb("carry", [ET, 2])
        shift = m.sb("shift", [ET, 2, ET])
        ps = m.ps("ps", [P, 4, P])
        ps1 = m.ps("ps1", [1, 4, P])
        psc = m.ps("psc", [ET, 2])
        with nc.Block() as block:
            v, t, landed = m.sem("v"), m.sem("t"), m.sem("landed")
            done = {"v": 0, "t": 0}

            def vec(dve, ins):
                done["v"] += 1
                ins.then_inc(v, 1)
                return done["v"]

            @block.vector
            def _(dve):
                n = 0

                def step(ins):
                    nonlocal n
                    ins.then_inc(v, 1)
                    n += 1
                    dve.wait_ge(v, n)

                dve.memset(shift[:, :, :], 0.0).then_inc(v, 1)
                n += 1
                dve.wait_ge(v, n)
                dve.tensor_copy(shift[:, 0, 1:ET], c.ident[0:ET, 0:ET - 1])
                step(dve.tensor_copy(shift[:, 1, 0:ET - 1], c.ident[0:ET, 1:ET]))
                step(dve.tensor_scalar(row1[:, :], row, 1.0, None, ALU.add))
                dve.wait_ge(t, 1)
                dve.tensor_copy(near[:, 0, 1:P], row[:, 0:P - 1])
                dve.tensor_copy(near[:, 1, 0:P - 1], row[:, 1:P])
                dve.tensor_scalar(near[:, 0, 0:1], psc[:, 0:1], -1.0, None, ALU.add)
                step(dve.tensor_scalar(near[:, 1, P - 1:P], psc[:, 1:2], -1.0, None, ALU.add))
                dve.tensor_tensor(same[:, 0, :], near[:, 0, :], row, ALU.is_equal)
                step(dve.tensor_tensor(same[:, 1, :], near[:, 1, :], row, ALU.is_equal))
                step(dve.tensor_scalar(wall[:, :, :], same[:, :, :], -1.0, BIG, ALU.add, ALU.mult))
                dve.tensor_reduce(through[:, :, 0], wall[:, :, :], AX.X, ALU.min)
                dve.tensor_reduce(through[:, :, 1], same[:, :, :], AX.X, ALU.min)
                step(dve.scalar_tensor_tensor(e[:, :], score, ALPHA, score, ALU.mult, ALU.max))
                turn = 1
                for what, (value, gate, k, op0, op1, low) in enumerate((
                        (e, wall, 0, ALU.add, ALU.max, -BIG), (ex, same, 1, ALU.mult, ALU.add, 0.0))):
                    def scans(initial):
                        f = dve.tensor_tensor_scan(scan[:, 0, :], gate[:, 0, :], value[:, :], initial(0), op0, op1)
                        step(dve.tensor_tensor_scan(scan[:, 1, ::-1], gate[:, 1, ::-1], value[:, ::-1], initial(1), op0, op1))

                    scans(lambda d: low)
                    turn += 1
                    dve.wait_ge(t, turn)
                    step(dve.tensor_copy(ends[:, :, :], ps1[:, :, 0:ET]))
                    dve.tensor_tensor_scan(carried[:, 0, 0:ET], ends[:, 2, 0:ET], ends[:, 0, 0:ET], low, op0, op1)
                    step(dve.tensor_tensor_scan(carried[:, 1, 0:ET][:, ::-1], ends[:, 3, 0:ET][:, ::-1],
                                                ends[:, 1, 0:ET][:, ::-1], low, op0, op1))
                    turn += 1
                    dve.wait_ge(t, turn)
                    step(dve.tensor_copy(carry[:, :], psc[:, :]))
                    turn += 1
                    dve.wait_ge(t, turn)
                    step(dve.tensor_copy(carry[:, :], psc[:, :]))
                    scans(lambda d: carry[:, d:d + 1])
                    if what == 0:
                        step(dve.tensor_tensor(tot[:, :], scan[:, 0, :], scan[:, 1, :], ALU.max))
                        step(dve.tensor_tensor(tot[:, :], e[:, :], tot[:, :], ALU.subtract))
                        turn += 1
                        dve.wait_ge(t, turn)
                    else:
                        step(dve.tensor_tensor(tot[:, :], scan[:, 0, :], scan[:, 1, :], ALU.add))
                        step(dve.tensor_tensor(tot[:, :], tot[:, :], ex[:, :], ALU.subtract))
                        step(dve.reciprocal(tot[:, :], tot[:, :]))
                        step(dve.tensor_tensor(ex[:, :], ex[:, :], tot[:, :], ALU.mult))
                step(dve.tensor_tensor(carry[:, 0:1], row1[:, P - 1:P], same[:, 1, P - 1:P], ALU.mult))
                step(dve.tensor_scalar(c.run_on[:, :], carry[:, 0:1], -1.0, None, ALU.add))
                turn += 1
                dve.wait_ge(t, turn)
                dve.tensor_copy(c.row_l[:, :], ps[:, 0, 0:ET])
                dve.tensor_copy(c.col_l[:, :], ps[:, 1, 0:ET])
                dve.tensor_copy(c.att_l[:, :], ps[:, 2, 0:ET])
                done["v"] = n

            @block.tensor
            def _(pe):
                pe.wait_ge(v, 3)
                pe.matmul(psc[:, 0:1], shift[:, 0, :], row1[:, P - 1:P], start=True, stop=True)
                pe.matmul(psc[:, 1:2], shift[:, 1, :], row1[:, 0:1], start=True, stop=True).then_inc(t, 1)
                at = 7
                for k in range(2):
                    at += 1
                    pe.wait_ge(v, at)
                    for d, end in ((0, P - 1), (1, 0)):
                        pe.matmul(ps1[:, d, 0:ET], scan[:, d, end:end + 1], c.ident[0:ET, 0:ET], start=True, stop=True)
                        g = pe.matmul(ps1[:, 2 + d, 0:ET], through[:, d, k:k + 1], c.ident[0:ET, 0:ET], start=True, stop=True)
                    g.then_inc(t, 1)
                    at += 2
                    pe.wait_ge(v, at)
                    for d in range(2):
                        g = pe.matmul(psc[:, d:d + 1], carried[:, d, 0:ET], c.ones[0:1, 0:1], start=True, stop=True)
                    g.then_inc(t, 1)
                    at += 1
                    pe.wait_ge(v, at)
                    for d in range(2):
                        g = pe.matmul(psc[:, d:d + 1], shift[:, d, :], carry[:, d:d + 1], start=True, stop=True)
                    g.then_inc(t, 1)
                    at += 2 + 2
                    if k == 1:
                        at += 2
                at += 2
                pe.wait_ge(v, at)
                for j, a in enumerate((row, col, ex[:, :])):
                    g = pe.transpose(ps[:, j, 0:ET], a, c.ident[0:ET, 0:ET])
                g.then_inc(t, 1)

            @block.scalar
            def _(act):
                act.wait_ge(v, 7 + 8)
                act.activation(ex[:, :], tot[:, :], ACT.Exp).then_inc(t, 1)

            @block.sync
            def _(sp):
                sp.dma_start(row_dram, row).then_inc(landed, 16)
                sp.wait_ge(landed, 16)

def edge_phase(nc, m, c, h_dram, row_dram, part_dram):
    U = 7
    K = ET // U
    V = 2
    with ExitStack() as ctx, nc.Block() as block:
        m = Phase(nc, ctx, "e")
        rowb = m.sb("rowb", [P, ET, P])
        index = [m.sb(f"index{b}", [P, 1], U32) for b in range(U)]
        got = [m.sb(f"got{b}", [P, D]) for b in range(U)]
        weight = [m.sb(f"weight{b}", [P, P]) for b in range(U)]
        part = [m.sb(f"part{b}", [P, D]) for b in range(U)]
        none = m.sb("none", [P, D])
        ps = [m.ps(f"ps{b}", [P, D]) for b in range(U)]
        rows_loaded, zeroed, zero_stored = m.sem("rows_loaded"), m.sem("zeroed"), m.sem("zero_stored")
        index_ready, gathered, weight_ready = m.sem("index_ready", U), swdge(c, U), m.sem("weight_ready", U)
        summed, copied, stored = m.sem("summed", U), m.sem("copied", U), m.sem("stored", U)
        part_t = part_dram.rearrange("(t p) d -> t p d", p=P)

        @block.gpsimd
        def _(pool):
            pool.memset(none[:, :], 0.0).then_inc(zeroed, 1)
            def turn(k):
                for b in range(U):
                    pool.wait_ge(summed[b], k)
                    pool.tensor_copy(index[b][:, :], c.col_l[:, bass.ds(k * U + b, 1)]).then_inc(index_ready[b], 1)
                for b in range(U):
                    pool.wait_ge(index_ready[b], k + 1)
                    pool.nop(nofuse=True)
                    pool.indirect_dma_start(got[b][:, :], None, h_dram,
                                            bass.IndirectOffsetOnAxis(index[b][:, :], 0)).then_inc(gathered[b], 16)

            turn(0)
            with pool.Fori(1, K) as k:
                turn(k)

        @block.vector
        def _(dve):
            dve.wait_ge(rows_loaded, 16)
            def turn(k):
                for b in range(U):
                    at = bass.ds(k * U + b, 1)
                    dve.wait_ge(summed[b], k)
                    dve.tensor_scalar(weight[b][:, :], rowb[:, at, :].squeeze(1), c.row_l[:, at], c.att_l[:, at],
                                      ALU.is_equal, ALU.mult).then_inc(weight_ready[b], 1)

            turn(0)
            with dve.Fori(1, K) as k:
                turn(k)

        @block.tensor
        def _(pe):
            def turn(k):
                for b in range(U):
                    pe.wait_ge(weight_ready[b], k + 1)
                    pe.wait_ge(gathered[b], 16 * (k + 1))
                    pe.wait_ge(copied[b], k)
                    pe.matmul(ps[b][:, :], weight[b][:, :], got[b][:, :], start=True, stop=True).then_inc(summed[b], 1)

            turn(0)
            with pe.Fori(1, K) as k:
                turn(k)

        @block.scalar
        def _(act):
            def turn(k):
                for b in range(U):
                    act.wait_ge(summed[b], k + 1)
                    act.wait_ge(stored[b], 16 * k)
                    act.copy(part[b][:, :], ps[b][:, :]).then_inc(copied[b], 1)

            turn(0)
            with act.Fori(1, K) as k:
                turn(k)

        @block.sync
        def _(sp):
            sp.dma_start(rowb[:, :, :].rearrange("p t e -> p (t e)"),
                         row_dram.rearrange("(o t) p -> o (t p)", o=1).broadcast_to([P, EP])).then_inc(rows_loaded, 16)
            sp.wait_ge(zeroed, 1)
            sp.dma_start(part_t[ET, :, :], none[:, :]).then_inc(zero_stored, 16)
            def turn(k):
                for b in range(U):
                    sp.wait_ge(copied[b], k + 1)
                    sp.dma_start(part_t[k * U + b, :, :], part[b][:, :]).then_inc(stored[b], 16)

            turn(0)
            with sp.Fori(1, K) as k:
                turn(k)
            for b in range(U):
                sp.wait_ge(stored[b], 16 * K)
            sp.wait_ge(zero_stored, 16)


def carry_phase(nc, m, c, part_dram):
    with ExitStack() as ctx, nc.Block() as block:
        m = Phase(nc, ctx, "y")
        row = c.sorted[:, 0, :]
        equal = m.sb("equal", [ET, P])
        count, onward, wanted, other, last = (m.sb(s, [ET, 1]) for s in ("count", "onward", "wanted", "other", "last"))
        index = m.sb("index", [ET, 1], U32)
        spread, began = m.sb("spread", [ET, ET]), m.sb("began", [ET, ET])
        ends, got, total = (m.sb(s, [ET, D]) for s in ("ends", "got", "total"))
        ps_wanted, ps_carry = m.ps("ps_wanted", [ET, ET]), m.ps("ps_carry", [ET, D])
        v, ends_loaded, index_ready = m.sem("v"), m.sem("ends_loaded"), m.sem("index_ready")
        spread_done, carried, summed = m.sem("spread_done"), m.sem("carried"), m.sem("summed")
        gathered, stored = swdge(c, 2)

        @block.sync
        def _(sp):
            sp.dma_start(ends[:, :], part_dram.rearrange("(t p) d -> t p d", p=P)[0:ET, P - 1, :]).then_inc(ends_loaded, 16)

        @block.vector
        def _(dve):
            dve.scalar_tensor_tensor(equal[:, :], row, row[:, 0:1], c.ones[0:ET, :], ALU.is_equal, ALU.mult, accum_out=count[:, :])
            dve.tensor_tensor(onward[:, :], row[:, 0:1], c.run_on[:, :], ALU.is_equal).then_inc(v, 1)
            dve.wait_ge(v, 1)
            dve.scalar_tensor_tensor(wanted[:, :], onward[:, :], 65536.0, row[:, 0:1], ALU.mult, ALU.add)
            dve.scalar_tensor_tensor(last[:, :], c.iota_p[0:ET, :], float(P), count[:, :], ALU.mult, ALU.add).then_inc(v, 1)
            dve.wait_ge(v, 2)
            dve.tensor_scalar(other[:, :], c.iota_p[0:ET, :], float(EP + 1), None, ALU.add)
            dve.tensor_scalar(last[:, :], last[:, :], -1.0, None, ALU.add)
            dve.tensor_scalar(spread[:, :], c.ident[0:ET, 0:ET], wanted[:, :], None, ALU.mult).then_inc(v, 1)
            dve.wait_ge(v, 3)
            dve.tensor_tensor(other[:, :], other[:, :], last[:, :], ALU.subtract).then_inc(v, 1)
            dve.wait_ge(v, 4)
            dve.scalar_tensor_tensor(index[:, :], other[:, :], onward[:, :], last[:, :], ALU.mult, ALU.add).then_inc(index_ready, 1)
            dve.wait_ge(spread_done, 1)
            dve.tensor_scalar(began[:, :], ps_wanted[:, :], c.run_on[:, :], None, ALU.is_equal).then_inc(v, 1)
            dve.wait_ge(carried, 1)
            dve.wait_ge(gathered, 16)
            dve.tensor_tensor(total[:, :], got[:, :], ps_carry[:, :], ALU.add).then_inc(summed, 1)

        @block.tensor
        def _(pe):
            pe.wait_ge(v, 3)
            pe.matmul(ps_wanted[:, :], c.ones[0:ET, 0:ET], spread[:, :], start=True, stop=True).then_inc(spread_done, 1)
            pe.wait_ge(v, 5)
            pe.wait_ge(ends_loaded, 16)
            pe.matmul(ps_carry[:, :], began[:, :], ends[:, :], start=True, stop=True).then_inc(carried, 1)

        @block.gpsimd
        def _(pool):
            pool.wait_ge(index_ready, 1)
            pool.nop(nofuse=True)
            pool.indirect_dma_start(got[:, :], None, part_dram, bass.IndirectOffsetOnAxis(index[:, :], 0)).then_inc(gathered, 16)
            pool.wait_ge(summed, 1)
            pool.nop(nofuse=True)
            pool.indirect_dma_start(part_dram, bass.IndirectOffsetOnAxis(index[:, :], 0), total[:, :], None,
                                    bounds_check=EP + P - 1, oob_is_err=False).then_inc(stored, 16)
            pool.wait_ge(stored, 16)


def weight_phase(nc, m, c, base_w, spline_w):
    with ExitStack() as ctx, nc.Block() as block:
        m = Phase(nc, ctx, "w")
        U = 3
        w = [m.sb(f"w{b}", [P, 4, D]) for b in range(U)]
        tops = m.sb("tops", [P, 18])
        top = m.sb("top", [P, 1])
        topT = m.sb("topT", [1, 1])
        bits = m.sb("bits", [P, 1])
        third = m.sb("third", [P, 1])
        ps = m.ps("ps", [P, P])
        loaded, used, v, t = m.sem("loaded", U), m.sem("used", U), m.sem("v"), m.sem("t")
        scaled, high, low = m.sem("scaled"), m.sem("high"), m.sem("low")
        base_v = base_w.rearrange("(c p) o -> p c o", p=P)
        spline_v = spline_w.rearrange("(c p) k o -> c p k o", p=P)
        pieces = [(base_v, 0, None)] + [(spline_v[ch, :, 4 * g:4 * g + 4, :], ch, g) for ch in range(CH) for g in range(2)]
        NPC = len(pieces)

        @block.sync
        def _(sp):
            for n in range(2 * NPC):
                if n >= U:
                    sp.wait_ge(used[n % U], n // U)
                sp.dma_start(w[n % U][:, :, :], pieces[n % NPC][0]).then_inc(loaded[n % U], 16)

        @block.vector
        def _(dve):
            for n in range(NPC):
                dve.wait_ge(loaded[n % U], 16 * (n // U + 1))
                dve.tensor_reduce(tops[:, n:n + 1], w[n % U][:, :, :], AX.XY, ALU.max, apply_absolute_value=True).then_inc(used[n % U], 1)
            for b in range(U):
                dve.wait_ge(used[b], len(range(b, NPC, U)))
            dve.tensor_reduce(top[:, :], tops[:, 0:NPC], AX.X, ALU.max).then_inc(v, 1)
            dve.wait_ge(t, 1)
            dve.tensor_reduce(topT[:, :], ps[0:1, 0:P], AX.X, ALU.max).then_inc(v, 1)
            dve.wait_ge(t, 2)
            dve.tensor_scalar(bits[:, :], ps[:, 0:1], 1e-30, None, ALU.max).then_inc(v, 1)
            dve.wait_ge(v, 3)
            dve.tensor_scalar(bits[:, :].bitcast(I32), bits[:, :].bitcast(I32), 0x7F800000, None, ALU.bitwise_and).then_inc(v, 1)
            dve.wait_ge(v, 4)
            dve.tensor_scalar(c.unscale[:, :], bits[:, :], 2.0 ** -23, None, ALU.mult)
            dve.reciprocal(c.scale[:, :], bits[:, :]).then_inc(v, 1)
            dve.wait_ge(v, 5)
            dve.tensor_scalar(c.scale[:, :], c.scale[:, :], 2.0 ** 13, None, ALU.mult).then_inc(v, 1)
            dve.wait_ge(v, 6)
            dve.tensor_scalar(third[:, :], c.scale[:, :], 1.0 / 3.0, None, ALU.mult).then_inc(scaled, 1)
            dve.wait_ge(scaled, 1)
            for n in range(NPC):
                q = n + NPC
                _, ch, g = pieces[n]
                fac = c.scale if g is None else third
                hi, lo = target(c, ch, g)
                dve.wait_ge(high, n + 1)
                dve.scalar_tensor_tensor(lo, w[q % U][:, :, :], fac[:, :], hi, ALU.mult, ALU.subtract).then_inc(used[q % U], 1)

        @block.scalar
        def _(act):
            act.wait_ge(scaled, 1)
            for n in range(NPC):
                q = n + NPC
                _, ch, g = pieces[n]
                fac = c.scale if g is None else third
                hi, lo = target(c, ch, g)
                act.wait_ge(loaded[q % U], 16 * (q // U + 1))
                act.activation(hi, w[q % U][:, :, :], ACT.Copy, scale=fac[:, :]).then_inc(high, 1)

        @block.tensor
        def _(pe):
            pe.wait_ge(v, 1)
            pe.transpose(ps[0:1, 0:P], top[:, :], c.ident[:, :]).then_inc(t, 1)
            pe.wait_ge(v, 2)
            pe.matmul(ps[:, 0:1], c.ones[0:1, :], topT[:, :], start=True, stop=True).then_inc(t, 1)


def target(c, ch, g):
    if g is None:
        return c.w_hi[:, :, NB, :], c.w_lo[:, :, NB, :]
    return c.w_hi[:, ch, 4 * g:4 * g + 4, :], c.w_lo[:, ch, 4 * g:4 * g + 4, :]


def layer_phase(nc, m, c, x, part_dram, both_dram, out):
    with ExitStack() as ctx, nc.Block() as block:
        m = Phase(nc, ctx, "l")
        pair = lambda name, shape, dt=F32: [m.sb(f"{name}{b}", shape, dt) for b in range(2)]
        index, agg, xt = pair("index", [P, 1], U32), pair("agg", [P, D]), pair("xt", [P, D])
        both, out0 = pair("both", [P, 2, D]), pair("out0", [P, D])
        f_hi, f_lo = pair("f_hi", [P, NF, D], F16), pair("f_lo", [P, NF, D], F16)
        G = 4
        y, a, b1, a2, b2, nn = (pair(s, [P, 2, D]) for s in ("y", "a", "b1", "a2", "b2", "nn"))
        th, zz = m.sb("th", [P, D]), m.sb("zz", [P, D])
        h2T = m.sb("h2T", [P, CH, P])
        stats, mv, ve, rstd = pair("stats", [P, 6]), pair("mv", [P, 2]), pair("ve", [P, 1]), pair("rstd", [P, 1])
        mhalf, nothing = m.sb("mhalf", [P, 1]), m.sb("nothing", [P, 2 * D])
        logit, ntop, ex, tot, prob = (pair("logit", [P, NEXP]), pair("ntop", [P, 1]), pair("ex", [P, NEXP]),
                                      pair("tot", [P, 1]), pair("prob", [P, 1]))
        ps_agg = [m.ps(f"ps_agg{b}", [P, CH, P]) for b in range(2)]
        ps_out = [m.ps(f"ps_out{b}", [P, D]) for b in range(2)]
        ps_h2 = m.ps("ps_h2", [P, CH, P])
        ps_logit = [m.ps(f"ps_logit{b}", [P, NEXP]) for b in range(2)]
        gathered = swdge(c, 2)
        x_loaded, both_stored, out_stored = (m.sem(s, 2) for s in ("x_loaded", "both_stored", "out_stored"))
        half, rest_stored = m.sem("half"), m.sem("rest_stored")
        y_ready, ab_ready, sq_ready, b3_ready, n_ready, a3_ready, hi_ready, lo_ready = (
            m.sem(s) for s in ("y_ready", "ab_ready", "sq_ready", "b3_ready", "n_ready", "a3_ready", "hi_ready", "lo_ready"))
        f_used = m.sem("f_used")
        (index_ready, aggT_ready, th_ready, z_ready, zhi_ready, zlo_ready, x1_ready, bn_done, mv_ready, ve_ready,
         rstd_ready, h2_ready, h2T_ready, h2T_copied, logit_done, logit_ready, ntop_ready, ex_ready, prob_ready, out0_ready) = (
            m.sem(s) for s in ("index_ready", "aggT_ready", "th_ready", "z_ready", "zhi_ready", "zlo_ready", "x1_ready",
                               "bn_done", "mv_ready", "ve_ready", "rstd_ready", "h2_ready", "h2T_ready", "h2T_copied",
                               "logit_done", "logit_ready", "ntop_ready", "ex_ready", "prob_ready", "out0_ready"))
        x_t = x.rearrange("(t p) d -> t p d", p=P)
        out_t = out.rearrange("(t p) d -> t p d", p=P)
        both_t = both_dram.rearrange("(t p) d -> t p d", p=P)
        row_of = lambda v, i: v[bass.ds(i, 1), :, :].squeeze(0)

        def steps(eng, step):
            def peeled(i):
                step(i, i // 2, i % 2, lambda o: 0 <= i + o < LT)

            for i in range(-2, 6):
                peeled(i)
            with eng.Fori(3, (LT - 3) // 2) as k:
                for b in range(2):
                    step(k * 2 + b, k, b, lambda o: True)
            for i in range((LT - 3) // 2 * 2, LT + 3):
                peeled(i)

        def slot(k, b, o):
            return (b + o) % 2, k + (b + o) // 2

        def past(v):
            return max(v, 0) if isinstance(v, int) else v

        @block.gpsimd
        def _(pool):
            pool.memset(mhalf[:, :], -0.5).then_inc(half, 1)
            pool.memset(c.logits[:, LT:NT, :], 0.0)
            pool.memset(c.prob[:, LT:NT], 0.0)
            pool.memset(nothing[:, :], 0.0).then_inc(half, 1)
            pool.wait_ge(half, 1)

            def gather(t, b):
                pool.wait_ge(aggT_ready, past(t - 1))
                pool.tensor_copy(index[b][:, :], c.last_edge[:, bass.ds(t, 1)]).then_inc(index_ready, 1)
                pool.wait_ge(index_ready, t + 1)
                pool.nop(nofuse=True)
                pool.indirect_dma_start(agg[b][:, :], None, part_dram,
                                        bass.IndirectOffsetOnAxis(index[b][:, :], 0)).then_inc(gathered[b], 16)

            def cubes(n, q):
                pool.wait_ge(sq_ready, n + 1)
                pool.tensor_tensor(b2[q][:, :, :], b1[q][:, :, :], b2[q][:, :, :], ALU.mult).then_inc(b3_ready, 1)

            def step(i, k, b, ok):
                for g in range(G):
                    if ok(1 + (g + 1) // G):
                        cubes(4 * i + 4 + g + 1, (g + 1) % 2)
                    if g == 0 and ok(3):
                        gather(i + 3, (b + 3) % 2)
                    if g == 2 and ok(-1):
                        q = (b - 1) % 2
                        pool.wait_ge(mv_ready, i)
                        pool.wait_ge(h2_ready, past(i - 2))
                        pool.nop(nofuse=True)
                        pool.tensor_scalar(ve[q][:, :], mv[q][:, 1:2], EPS, None, ALU.add).then_inc(ve_ready, 1)
                        pool.wait_ge(ve_ready, i)
                        pool.tensor_tensor(rstd[q][:, :], ve[q][:, :], mhalf[:, :], ALU.pow).then_inc(rstd_ready, 1)

            gather(0, 0)
            steps(pool, step)

        @block.sync
        def _(sp):
            def step(i, k, b, ok):
                if ok(0):
                    sp.wait_ge(x1_ready, past(i - 1))
                    sp.dma_start(xt[b][:, :], row_of(x_t, i)).then_inc(x_loaded[b], 16)
                if ok(-3):
                    q = (b - 3) % 2
                    sp.wait_ge(out0_ready, i - 2)
                    sp.dma_start(row_of(out_t, i - 3), out0[q][:, :]).then_inc(out_stored[q], 16)
                if ok(-1):
                    q = (b - 1) % 2
                    sp.wait_ge(h2_ready, i)
                    sp.dma_start(row_of(both_t, i - 1), both[q][:, :, :].rearrange("p a d -> p (a d)")).then_inc(both_stored[q], 16)

            sp.wait_ge(half, 2)
            for t in range(LT, NT):
                sp.dma_start(both_t[t, :, :], nothing[:, :]).then_inc(rest_stored, 16)
            steps(sp, step)
            sp.wait_ge(rest_stored, 16 * (NT - LT))
            for b in range(2):
                sp.wait_ge(both_stored[b], 16 * ((LT + 1 - b) // 2))
                sp.wait_ge(out_stored[b], 16 * ((LT + 1 - b) // 2))

        @block.tensor
        def _(pe):
            def agg_t(t, b, turn):
                pe.wait_ge(gathered[b], 16 * (turn + 1))
                pe.wait_ge(y_ready, past(4 * t - 4))
                pe.wait_ge(z_ready, past(t - 1))
                for ch in range(CH):
                    g = pe.transpose(ps_agg[b][:, ch, :], agg[b][:, ch * P:(ch + 1) * P], c.ident[:, :])
                g.then_inc(aggT_ready, 1)

            def products(b, fs, first, last):
                for f in fs:
                    for ch in range(CH):
                        cols = slice(ch * P, (ch + 1) * P)
                        for part, (lhs, rhs) in enumerate(((f_hi, c.w_hi), (f_hi, c.w_lo), (f_lo, c.w_hi))):
                            mm = pe.matmul(ps_out[b][:, :], lhs[b][:, f, cols], rhs[:, ch, f, :],
                                           start=first and f == fs[0] and ch == 0 and part == 0,
                                           stop=last and f == fs[-1] and ch == CH - 1 and part == 2)
                mm.then_inc(f_used, 1)

            def step(i, k, b, ok):
                if ok(2):
                    agg_t(i + 2, *slot(k, b, 2))
                for g in range(G):
                    if ok(0):
                        if g == 0:
                            pe.wait_ge(x1_ready, past(i - 1))
                        pe.wait_ge(lo_ready, 4 * i + g + 1)
                        products(b, (2 * g, 2 * g + 1), g == 0, False)
                    if g == 0 and ok(-2):
                        pe.wait_ge(h2_ready, i - 1)
                        pe.wait_ge(h2T_copied, past(i - 2))
                        for ch in range(CH):
                            t = pe.transpose(ps_h2[:, ch, :], both[b][:, 1, ch * P:(ch + 1) * P], c.ident[:, :])
                        t.then_inc(h2T_ready, 1)
                    if g == 2 and ok(-2):
                        pe.wait_ge(h2T_copied, i - 1)
                        pe.wait_ge(logit_ready, past(i - 3))
                        for ch in range(CH):
                            t = pe.matmul(ps_logit[b][:, :], h2T[:, ch, :], c.gate_w[:, ch, :], start=ch == 0, stop=ch == CH - 1)
                        t.then_inc(logit_done, 1)
                if ok(0):
                    pe.wait_ge(zlo_ready, i + 1)
                    products(b, (NB,), False, True)

            steps(pe, step)

        @block.scalar
        def _(act):
            def squares(n, q):
                act.wait_ge(ab_ready, n + 1)
                act.wait_ge(n_ready, past(n - 1))
                act.activation(a2[q][:, :, :], a[q][:, :, :], ACT.Square)
                act.activation(b2[q][:, :, :], b1[q][:, :, :], ACT.Square, scale=2.0).then_inc(sq_ready, 1)

            def high(t, b, g):
                act.wait_ge(n_ready, 4 * t + g + 1)
                act.wait_ge(f_used, past(5 * t - 10 + g + 1))
                act.copy(f_hi[b][:, 2 * g:2 * g + 2, :], nn[g % 2][:, :, :]).then_inc(hi_ready, 1)

            def bases(t, b, g):
                n = 4 * t + g
                act.wait_ge(aggT_ready, t + 1)
                act.wait_ge(ab_ready, past(n - 1))
                for j in range(2):
                    done = act.activation(y[g % 2][:, j, :], ps_agg[b][:, :, :].rearrange("p c n -> p (c n)"), ACT.Abs,
                                          bias=c.mid[:, 2 * g + j:2 * g + j + 1], scale=20.0)
                done.then_inc(y_ready, 1)

            def step(i, k, b, ok):
                q = (b + 1) % 2
                for g in range(G):
                    if ok(1 + (g + 1) // G):
                        squares(4 * i + 4 + g + 1, (g + 1) % 2)
                    if ok(1):
                        high(i + 1, q, g)
                    if ok(1 + (g + 3) // G):
                        bases(i + 1 + (g + 3) // G, (b + 1 + (g + 3) // G) % 2, (g + 3) % G)
                    if g == 0 and ok(1):
                        act.wait_ge(z_ready, i + 1)
                        act.activation(th[:, :], ps_agg[q][:, :, :].rearrange("p c n -> p (c n)"), ACT.Tanh, scale=0.5).then_inc(th_ready, 1)
                    if g == 0 and ok(-3):
                        act.wait_ge(ntop_ready, i - 2)
                        act.wait_ge(prob_ready, past(i - 4))
                        act.activation(ex[q][:, :], logit[q][:, :], ACT.Exp, bias=ntop[q][:, :], accum_out=tot[q][:, :]).then_inc(ex_ready, 1)
                    if g == 1 and ok(-2):
                        act.wait_ge(h2T_ready, i - 1)
                        act.wait_ge(logit_done, past(i - 2))
                        act.copy(h2T[:, :, :], ps_h2[:, :, :]).then_inc(h2T_copied, 1)
                    if g == 2 and ok(1):
                        act.wait_ge(z_ready, i + 2)
                        act.wait_ge(f_used, past(5 * i))
                        act.activation(f_hi[q][:, NB, :], zz[:, :], ACT.Copy, scale=512.0).then_inc(zhi_ready, 1)

            steps(act, step)

        @block.vector
        def _(dve):
            def sides(n, q):
                dve.wait_ge(y_ready, n + 1)
                dve.wait_ge(b3_ready, past(n - 1))
                dve.wait_ge(a3_ready, past(n - 1))
                dve.tensor_scalar(a[q][:, :, :], y[q][:, :, :], -16.0, 0.0, ALU.add, ALU.min)
                dve.tensor_scalar(b1[q][:, :, :], y[q][:, :, :], -8.0, 0.0, ALU.add, ALU.min).then_inc(ab_ready, 1)

            def cubes(n, q):
                dve.wait_ge(sq_ready, n + 1)
                dve.tensor_tensor(a2[q][:, :, :], a[q][:, :, :], a2[q][:, :, :], ALU.mult).then_inc(a3_ready, 1)

            def basis(n, q):
                dve.wait_ge(b3_ready, n + 1)
                dve.wait_ge(a3_ready, n + 1)
                dve.wait_ge(lo_ready, past(n - 1))
                dve.tensor_tensor(nn[q][:, :, :], b2[q][:, :, :], a2[q][:, :, :], ALU.subtract).then_inc(n_ready, 1)

            def low(t, b, g):
                dve.wait_ge(hi_ready, 4 * t + g + 1)
                dve.tensor_tensor(f_lo[b][:, 2 * g:2 * g + 2, :], nn[g % 2][:, :, :], f_hi[b][:, 2 * g:2 * g + 2, :],
                                  ALU.subtract).then_inc(lo_ready, 1)

            def step(i, k, b, ok):
                q, turn = slot(k, b, -1)
                for g in range(G):
                    if ok(1 + (g + 2) // G):
                        sides(4 * i + 4 + g + 2, g % 2)
                    if g == 0 and ok(-3):
                        dve.wait_ge(logit_done, i - 2)
                        dve.wait_ge(ex_ready, past(i - 4))
                        dve.tensor_tensor(logit[q][:, :], ps_logit[q][:, :], c.gate_b[:, :], ALU.add).then_inc(logit_ready, 1)
                        dve.wait_ge(logit_ready, i - 2)
                        dve.tensor_copy(c.logits[:, bass.ds(i - 3, 1), :].squeeze(1), logit[q][:, :])
                        dve.tensor_reduce(ntop[q][:, :], logit[q][:, :], AX.X, ALU.max, negate=True).then_inc(ntop_ready, 1)
                    if g == 1 and ok(-3):
                        dve.wait_ge(ex_ready, i - 2)
                        dve.reciprocal(prob[q][:, :], tot[q][:, :]).then_inc(prob_ready, 1)
                    if g == 1 and ok(1):
                        dve.wait_ge(th_ready, i + 2)
                        dve.wait_ge(zlo_ready, i + 1)
                        dve.scalar_tensor_tensor(zz[:, :], th[:, :], 1.0, ps_agg[q][:, :, :].rearrange("p c n -> p (c n)"),
                                                 ALU.add, ALU.mult).then_inc(z_ready, 1)
                    if g == 2 and ok(-1):
                        dve.wait_ge(x1_ready, i)
                        dve.bn_stats(stats[q][:, :], both[q][:, 0, :]).then_inc(bn_done, 1)
                    if ok(1 + (g + 1) // G):
                        cubes(4 * i + 4 + g + 1, (g + 1) % 2)
                    if g == 1 and ok(-3):
                        dve.wait_ge(prob_ready, i - 2)
                        dve.wait_ge(out_stored[q], 16 * past(turn - 1))
                        dve.tensor_copy(c.prob[:, bass.ds(i - 3, 1)], prob[q][:, :])
                        dve.scalar_tensor_tensor(out0[q][:, :], both[q][:, 1, :], prob[q][:, :], both[q][:, 0, :],
                                                 ALU.mult, ALU.add).then_inc(out0_ready, 1)
                    if g == 2 and ok(-1):
                        dve.wait_ge(bn_done, i)
                        dve.nop(nofuse=True)
                        dve.bn_aggr(mv[q][:, :], stats[q][:, :]).then_inc(mv_ready, 1)
                    if g == 3 and ok(1):
                        dve.wait_ge(zhi_ready, i + 2)
                        dve.scalar_tensor_tensor(f_lo[q][:, NB, :], zz[:, :], 512.0, f_hi[q][:, NB, :], ALU.mult, ALU.subtract).then_inc(zlo_ready, 1)
                    if ok(1):
                        low(i + 1, q, g)
                    if g == 1 and ok(-1):
                        dve.wait_ge(f_used, 5 * i)
                        dve.wait_ge(x_loaded[q], 16 * (turn + 1))
                        dve.wait_ge(both_stored[q], 16 * turn)
                        dve.wait_ge(out0_ready, past(i - 2))
                        dve.scalar_tensor_tensor(both[q][:, 0, :], ps_out[q][:, :], c.unscale[:, :], xt[q][:, :],
                                                 ALU.mult, ALU.add).then_inc(x1_ready, 1)
                    if g == 3 and ok(-1):
                        dve.wait_ge(rstd_ready, i)
                        dve.tensor_scalar(both[q][:, 1, :], both[q][:, 0, :], mv[q][:, 0:1], rstd[q][:, :],
                                          ALU.subtract, ALU.mult).then_inc(h2_ready, 1)
                    if ok(1 + (g + 1) // G):
                        basis(4 * i + 4 + g + 1, (g + 1) % 2)

            steps(dve, step)


def route_phase(nc, m, c):
    with ExitStack() as ctx:
        m = Phase(nc, ctx, "r")
        te = lambda ap: wide(ap.unsqueeze(2), [P, NT, NEXP])
        best = m.sb("best", [P, NT])
        countdown = m.sb("countdown", [P, NEXP])
        points = m.sb("points", [P, NT, NEXP])
        first = m.sb("first", [P, NT])
        route = m.sb("route", [P, NEXP, NT], BF16)
        tri, ones = m.sb("tri", [P, P], BF16), m.sb("ones", [P, P], BF16)
        keep_on = m.sb("keep_on", [P, NEXP, NT])
        totals = m.sb("totals", [P, NEXP, NT])
        upto = m.sb("upto", [P, NEXP, NT])
        before = m.sb("before", [P, NEXP, NT])
        mine = m.sb("mine", [P, NEXP, NT])
        pos, over, expert, place = (m.sb(s, [P, NT]) for s in ("pos", "over", "expert", "place"))
        placei, tilei = m.sb("placei", [P, NT], I32), m.sb("tilei", [P, NT], I32)
        place_tile, place_lane = m.sb("place_tile", [P, NT]), m.sb("place_lane", [P, NT])
        token = m.sb("token", [P, NT])
        lane_hot = [m.sb(f"lane_hot{b}", [P, P]) for b in range(2)]
        values = [m.sb(f"values{b}", [P, 2, FT]) for b in range(2)]
        slots = m.sb("slots", [P, 2, FT])
        empty = m.sb("empty", [P, FT])
        PIECE = 6
        pieces = [(e, min(e + PIECE, NEXP)) for e in range(0, NEXP, PIECE)]
        ps_in = [m.ps(f"ps_in{n}", [P, PIECE, NT]) for n in range(len(pieces))]
        ps_all = [m.ps(f"ps_all{n}", [P, PIECE, NT]) for n in range(len(pieces))]
        ps_slots = m.ps("ps_slots", [P, 2, FT])
        v, made, counted, hot_ready, moved, all_moved = (m.sem("v"), m.sem("made"), m.sem("counted"),
                                                         m.sem("hot_ready", 2), m.sem("moved", 2), m.sem("all_moved"))
        with nc.Block() as block:

            @block.gpsimd
            def _(pool):
                pool.iota(countdown[:, :], [[-1, NEXP]], base=NEXP, channel_multiplier=0, allow_small_or_imprecise_dtypes=True)
                pool.iota(token[:, :], [[P, NT]], base=1, channel_multiplier=1, allow_small_or_imprecise_dtypes=True).then_inc(made, 1)

            @block.vector
            def _(dve):
                n = 0

                def step(ins):
                    nonlocal n
                    ins.then_inc(v, 1)
                    n += 1
                    dve.wait_ge(v, n)

                dve.memset(keep_on[:, :, :], 1.0)
                dve.tensor_copy(tri[:, :], c.tri[:, :])
                dve.tensor_copy(ones[:, :], c.ones[:, :])
                step(dve.tensor_reduce(best[:, :], c.logits[:, :, :], AX.X, ALU.max))
                dve.memset(keep_on[:, :, 0], 0.0)
                step(dve.tensor_tensor(points[:, :, :], c.logits[:, :, :], te(best[:, :]), ALU.is_equal))
                dve.wait_ge(made, 1)
                step(dve.tensor_tensor(points[:, :, :], points[:, :, :], wide(countdown[:, :].unsqueeze(1), [P, NT, NEXP]), ALU.mult))
                step(dve.tensor_reduce(first[:, :], points[:, :, :], AX.X, ALU.max))
                step(dve.tensor_tensor(route[:, :, :].rearrange("p e t -> p t e"), wide(countdown[:, :].unsqueeze(1), [P, NT, NEXP]),
                                       te(first[:, :]), ALU.is_equal))
                dve.wait_ge(counted, 1)
                for q, (e0, e1) in enumerate(pieces):
                    done = dve.tensor_copy(totals[:, e0:e1, :], ps_all[q][:, 0:e1 - e0, :])
                step(done)
                flat = lambda a: a[:, :, :].rearrange("p e t -> p (e t)")
                step(dve.tensor_tensor_scan(flat(upto), flat(keep_on), flat(totals), 0.0, ALU.mult, ALU.add))
                step(dve.tensor_tensor(before[:, :, :], upto[:, :, :], totals[:, :, :], ALU.subtract))
                for q, (e0, e1) in enumerate(pieces):
                    done = dve.tensor_tensor(mine[:, e0:e1, :], ps_in[q][:, 0:e1 - e0, :], before[:, e0:e1, :], ALU.add)
                step(done)
                step(dve.tensor_tensor(mine[:, :, :], mine[:, :, :], route[:, :, :], ALU.mult))
                step(dve.tensor_reduce(pos[:, :], mine[:, :, :].rearrange("p e t -> p t e"), AX.X, ALU.add))
                step(dve.tensor_scalar(over[:, :], pos[:, :], float(CAP), 32768.0, ALU.is_ge, ALU.mult))
                step(dve.tensor_scalar(expert[:, :], first[:, :], -float(ST * P), float(NEXP * ST * P), ALU.mult, ALU.add))
                step(dve.tensor_tensor(place[:, :], pos[:, :], over[:, :], ALU.add))
                step(dve.tensor_tensor(place[:, :], place[:, :], expert[:, :], ALU.add))
                step(dve.tensor_copy(placei[:, :], place[:, :]))
                step(dve.tensor_scalar(tilei[:, :], placei[:, :], 7, None, ALU.logical_shift_right))
                step(dve.tensor_copy(place_tile[:, :], tilei[:, :]))
                step(dve.scalar_tensor_tensor(place_lane[:, :], place_tile[:, :], -float(P), place[:, :], ALU.mult, ALU.add))
                def turn(k):
                    for b in range(2):
                        at = bass.ds(k * 2 + b, 1)
                        dve.wait_ge(moved[b], k)
                        dve.tensor_scalar(lane_hot[b][:, :], c.iota_f[:, :], place_lane[:, at], None, ALU.is_equal)
                        dve.tensor_scalar(values[b][:, 0, :], c.iota_f[:, 0:FT], place_tile[:, at], token[:, at], ALU.is_equal, ALU.mult)
                        dve.tensor_scalar(values[b][:, 1, :], c.iota_f[:, 0:FT], place_tile[:, at], c.prob[:, at],
                                          ALU.is_equal, ALU.mult).then_inc(hot_ready[b], 1)

                turn(0)
                with dve.Fori(1, NT // 2) as k:
                    turn(k)
                dve.wait_ge(all_moved, 1)
                step(dve.tensor_copy(slots[:, :, :], ps_slots[:, :, :]))
                dve.tensor_copy(c.slot_prob[:, :], slots[:, 1, :])
                dve.tensor_scalar(c.slot_read[:, :], slots[:, 0, :], -1.0, 0.0, ALU.add, ALU.max)
                step(dve.tensor_scalar(empty[:, :], slots[:, 0, :], 0.0, float(NP + 1), ALU.is_equal, ALU.mult))
                step(dve.scalar_tensor_tensor(empty[:, :], slots[:, 0, :], -1.0, empty[:, :], ALU.add, ALU.add))
                dve.tensor_copy(c.slot_write[:, :], empty[:, :])

            @block.tensor
            def _(pe):
                pe.wait_ge(v, 5)
                for q, (e0, e1) in enumerate(pieces):
                    pe.matmul(ps_in[q][:, 0:e1 - e0, :], tri[:, :], route[:, e0:e1, :], start=True, stop=True)
                    g = pe.matmul(ps_all[q][:, 0:e1 - e0, :], ones[:, :], route[:, e0:e1, :], start=True, stop=True)
                g.then_inc(counted, 1)
                pe.matmul(ps_slots[:, :, :], c.zrow[:, 0:P], c.zrow[:, 0:2 * FT], start=True, stop=False)
                def turn(k):
                    for b in range(2):
                        pe.wait_ge(hot_ready[b], k + 1)
                        pe.matmul(ps_slots[:, :, :], lane_hot[b][:, :], values[b][:, :, :], start=False, stop=False).then_inc(moved[b], 1)

                turn(0)
                with pe.Fori(1, NT // 2) as k:
                    turn(k)
                pe.matmul(ps_slots[:, :, :], c.zrow[:, 0:P], c.zrow[:, 0:2 * FT], start=False, stop=True).then_inc(all_moved, 1)


def expert_phase(nc, m, c, expert_w, expert_b, both_dram, out):
    U = ST
    with ExitStack() as ctx, nc.Block() as block:
        m = Phase(nc, ctx, "x")
        pair = lambda name, shape, dt=F32: [m.sb(f"{name}{b}", shape, dt) for b in range(2)]
        w, w_hi, w_lo = pair("w", [P, CH, D]), pair("w_hi", [P, CH, D], F16), pair("w_lo", [P, CH, D], F16)
        bias = m.sb("bias", [P, NEXP, D])
        read = [m.sb(f"read{b}", [P, 1], U32) for b in range(U)]
        write = [m.sb(f"write{b}", [P, 1], U32) for b in range(U)]
        both = [m.sb(f"both{b}", [P, 2 * D]) for b in range(U)]
        hT_hi = [m.sb(f"hT_hi{b}", [P, D], F16) for b in range(3)]
        hT_lo = [m.sb(f"hT_lo{b}", [P, D], F16) for b in range(3)]
        y = pair("y", [P, D])
        o = [m.sb(f"o{b}", [P, D]) for b in range(U)]
        tops, topT, bits, scale, unscale = m.sb("tops", [P, 1]), m.sb("topT", [1, 1]), m.sb("bits", [P, 1]), m.sb("scale", [P, 1]), pair("unscale", [P, 1])
        ps_t = [m.ps(f"ps_t{b}", [P, D]) for b in range(2)]
        ps_y = [m.ps(f"ps_y{b}", [P, D]) for b in range(2)]
        ps_top = m.ps("ps_top", [P, P])
        bias_loaded, w_loaded = m.sem("bias_loaded"), m.sem("w_loaded", 2)
        gathered, stored = swdge(c, U), swdge(c, U)
        top_ready, top_row, topT_ready, top_all, max_ready, bits_ready, recip_ready, scale_ready, w_high, w_ready = (
            m.sem(s) for s in ("top_ready", "top_row", "topT_ready", "top_all", "max_ready", "bits_ready", "recip_ready",
                               "scale_ready", "w_high", "w_ready"))
        read_ready, write_ready, turned, t_high, t_low, multiplied, y_ready, o_ready = (
            m.sem(s) for s in ("read_ready", "write_ready", "turned", "t_high", "t_low", "multiplied", "y_ready", "o_ready"))

        def turns(eng, slot):
            def pair_of_experts(k, ok):
                for j in range(2 * U):
                    slot(k * (2 * U) + j, j, k, k * 2 + j // U, j % U, ok)

            for j in range(-4, 0):
                slot(j, j, 0, -1, j % U, lambda n: 0 <= n < FT)
            pair_of_experts(0, lambda n: 0 <= n < FT)
            with eng.Fori(1, NEXP // 2 - 1) as k:
                pair_of_experts(k, lambda n: True)
            pair_of_experts(NEXP // 2 - 1, lambda n: 0 <= n < FT)
            for j in range(2):
                slot(FT + j, j, NEXP // 2, NEXP, j, lambda n: 0 <= n < FT)

        def past(v):
            return max(v, 0) if isinstance(v, int) else v

        @block.sync
        def _(sp):
            w_v = expert_w.rearrange("e (c p) f -> p e c f", p=P)
            for h in range(2):
                sp.dma_start(w[h][:, :, :], w_v[:, h, :, :]).then_inc(w_loaded[h], 16)
            sp.dma_start(bias[:, :, :].rearrange("p e d -> p (e d)"),
                         expert_b.rearrange("(o e) d -> o (e d)", o=1).broadcast_to([P, NEXP * D])).then_inc(bias_loaded, 16)
            with sp.Fori(0, NEXP // 2 - 1) as k:
                for h in range(2):
                    sp.wait_ge(w_ready, k * 2 + h + 1)
                    sp.dma_start(w[h][:, :, :], w_v[:, bass.ds(k * 2 + h + 2, 1), :, :].squeeze(1)).then_inc(w_loaded[h], 16)

        @block.gpsimd
        def _(pool):
            def slot(n, j, k, e, q, ok):
                if ok(n + 4):
                    r, t = (q + 4) % U, e + (q + 4) // U
                    pool.wait_ge(o_ready, past(n - 1))
                    pool.wait_ge(read_ready, n + 5)
                    pool.nop(nofuse=True)
                    pool.indirect_dma_start(both[r][:, :], None, both_dram,
                                            bass.IndirectOffsetOnAxis(read[r][:, :], 0)).then_inc(gathered[r], 16)
                if ok(n + 5):
                    r, t = (q + 5) % U, e + (q + 5) // U
                    pool.wait_ge(gathered[r], 16 * t)
                    pool.tensor_copy(read[r][:, :], c.slot_read[:, bass.ds(n + 5, 1)]).then_inc(read_ready, 1)
                if ok(n - 2):
                    r = (q - 2) % U
                    pool.wait_ge(o_ready, n - 1)
                    pool.wait_ge(write_ready, n - 1)
                    pool.nop(nofuse=True)
                    pool.indirect_dma_start(out, bass.IndirectOffsetOnAxis(write[r][:, :], 0), o[r][:, :], None,
                                            bounds_check=NP - 1, oob_is_err=False).then_inc(stored[r], 16)
                if ok(n - 1):
                    r, t = (q - 1) % U, e + (q - 1) // U
                    pool.wait_ge(stored[r], 16 * t)
                    pool.tensor_copy(write[r][:, :], c.slot_write[:, bass.ds(n - 1, 1)]).then_inc(write_ready, 1)

            pool.tensor_copy(read[0][:, :], c.slot_read[:, 0:1]).then_inc(read_ready, 1)
            turns(pool, slot)
            for r in range(U):
                pool.wait_ge(stored[r], 16 * NEXP)

        @block.tensor
        def _(pe):
            def top_to_row(e):
                pe.wait_ge(top_ready, e + 1)
                pe.transpose(ps_top[0:1, 0:P], tops[:, :], c.ident[:, :]).then_inc(top_row, 1)

            def top_to_all(e):
                pe.wait_ge(topT_ready, e + 1)
                pe.matmul(ps_top[:, 0:1], c.ones[0:1, :], topT[:, :], start=True, stop=True).then_inc(top_all, 1)

            def slot(n, j, k, e, q, ok):
                if ok(n + 2):
                    r, t, b = (q + 2) % U, e + (q + 2) // U, (j + 2) % 2
                    pe.wait_ge(gathered[r], 16 * (t + 1))
                    pe.wait_ge(t_low, past(n + 1))
                    for ch in range(CH):
                        g = pe.transpose(ps_t[b][:, ch * P:(ch + 1) * P], both[r][:, D + ch * P:D + (ch + 1) * P], c.ident[:, :])
                    g.then_inc(turned, 1)
                if ok(n):
                    h = (j // U) % 2
                    if q == 0:
                        pe.wait_ge(w_ready, e + 1)
                    pe.wait_ge(t_low, n + 1)
                    pe.wait_ge(y_ready, past(n - 1))
                    for ch in range(CH):
                        for part, (lhs, rhs) in enumerate(((hT_hi, w_hi), (hT_hi, w_lo), (hT_lo, w_hi))):
                            g = pe.matmul(ps_y[j % 2][:, :], lhs[j % 3][:, ch * P:(ch + 1) * P], rhs[h][:, ch, :],
                                          start=ch == 0 and part == 0, stop=ch == CH - 1 and part == 2)
                    g.then_inc(multiplied, 1)
                    if q == 1 and ok(n + U):
                        top_to_row(e + 1)
                    if q == 2 and ok(n + U):
                        top_to_all(e + 1)

            top_to_row(0)
            top_to_all(0)
            turns(pe, slot)

        @block.scalar
        def _(act):
            def weights_high(e, h, half):
                act.wait_ge(scale_ready, e + 1)
                act.activation(w_hi[h][:, 2 * half:2 * half + 2, :], w[h][:, 2 * half:2 * half + 2, :], ACT.Copy,
                               scale=scale[:, :]).then_inc(w_high, 1)

            def slot(n, j, k, e, q, ok):
                if ok(n + 2):
                    b, d = (j + 2) % 2, (j + 2) % 3
                    act.wait_ge(turned, n + 3)
                    act.wait_ge(multiplied, past(n))
                    act.activation(hT_hi[d][:, :], ps_t[b][:, :], ACT.Copy, scale=1024.0).then_inc(t_high, 1)
                if q in (3, 4) and ok(n) and ok(n + U):
                    act.wait_ge(multiplied, past(n - q))
                    weights_high(e + 1, 1 - (j // U) % 2, q - 3)

            weights_high(0, 0, 0)
            weights_high(0, 0, 1)
            turns(act, slot)

        @block.vector
        def _(dve):
            def largest(e, h, turn):
                dve.wait_ge(w_loaded[h], 16 * (turn + 1))
                dve.tensor_reduce(tops[:, :], w[h][:, :, :], AX.XY, ALU.max, apply_absolute_value=True).then_inc(top_ready, 1)

            def largest_of_row(e):
                dve.wait_ge(top_row, e + 1)
                dve.tensor_reduce(topT[:, :], ps_top[0:1, 0:P], AX.X, ALU.max).then_inc(topT_ready, 1)

            def scales(e, h):
                dve.wait_ge(top_all, e + 1)
                dve.tensor_scalar(bits[:, :], ps_top[:, 0:1], 1e-30, None, ALU.max).then_inc(max_ready, 1)
                dve.wait_ge(max_ready, e + 1)
                dve.tensor_scalar(bits[:, :].bitcast(I32), bits[:, :].bitcast(I32), 0x7F800000, None, ALU.bitwise_and).then_inc(bits_ready, 1)
                dve.wait_ge(bits_ready, e + 1)
                dve.tensor_scalar(unscale[h][:, :], bits[:, :], 2.0 ** -23, None, ALU.mult)
                dve.wait_ge(w_ready, past(e))
                dve.reciprocal(scale[:, :], bits[:, :]).then_inc(recip_ready, 1)
                dve.wait_ge(recip_ready, e + 1)
                dve.tensor_scalar(scale[:, :], scale[:, :], 2.0 ** 13, None, ALU.mult).then_inc(scale_ready, 1)

            def weights_low(e, h, half):
                at = slice(2 * half, 2 * half + 2)
                dve.wait_ge(w_high, e * 2 + half + 1)
                done = dve.scalar_tensor_tensor(w_lo[h][:, at, :], w[h][:, at, :], scale[:, :], w_hi[h][:, at, :], ALU.mult, ALU.subtract)
                if half == 1:
                    done.then_inc(w_ready, 1)

            def slot(n, j, k, e, q, ok):
                h = (j // U) % 2
                if ok(n - 1):
                    he = h if q >= 1 else 1 - h
                    dve.wait_ge(multiplied, n)
                    dve.wait_ge(o_ready, past(n - 2))
                    dve.scalar_tensor_tensor(y[(j - 1) % 2][:, :], ps_y[(j - 1) % 2][:, :], unscale[he][:, :],
                                             bias[:, bass.ds(e if q >= 1 else e - 1, 1), :].squeeze(1), ALU.mult, ALU.add).then_inc(y_ready, 1)
                if ok(n + 2):
                    b, d = (j + 2) % 2, (j + 2) % 3
                    dve.wait_ge(t_high, n + 3)
                    dve.scalar_tensor_tensor(hT_lo[d][:, :], ps_t[b][:, :], 1024.0, hT_hi[d][:, :], ALU.mult, ALU.subtract).then_inc(t_low, 1)
                if ok(n - 1):
                    r, t = (q - 1) % U, e + (q - 1) // U
                    dve.wait_ge(y_ready, n)
                    dve.wait_ge(stored[r], 16 * t)
                    dve.scalar_tensor_tensor(o[r][:, :], y[(j - 1) % 2][:, :], c.slot_prob[:, bass.ds(n - 1, 1)], both[r][:, 0:D],
                                             ALU.mult, ALU.add).then_inc(o_ready, 1)
                if ok(n) and ok(n + U):
                    if q == 0:
                        largest(e + 1, 1 - h, k + h)
                    if q == 1:
                        largest_of_row(e + 1)
                    if q == 2:
                        scales(e + 1, 1 - h)
                    if q in (4, 5):
                        weights_low(e + 1, 1 - h, q - 4)

            largest(0, 0, 0)
            largest_of_row(0)
            scales(0, 0)
            weights_low(0, 0, 0)
            weights_low(0, 0, 1)
            dve.wait_ge(bias_loaded, 16)
            turns(dve, slot)


class Consts:
    pass


def build(nc, x, row, col, wt, a2, base_w, spline_w, switch_w, switch_b, expert_w, expert_b, out):
    with ExitStack() as ctx:
        m = Phase(nc, ctx, "g")
        c = Consts()
        c.iota_f, c.iota_p = m.sb("iota_f", [P, P]), m.sb("iota_p", [P, 1])
        c.ones, c.ident, c.tri, c.after = (m.sb(s, [P, P]) for s in ("ones", "ident", "tri", "after"))
        c.swdge = m.sem("swdge", 7 + 2 + 2 + 2 * ST)
        c.st = m.sb("st", [P, 2, NT])
        h_dram = nc.dram_tensor("h_dram", [NP, D], F32, kind="Internal").ap()
        constants(nc, m, c)
        node_phase(nc, m, c, x, wt, a2, h_dram)
        if True:
            row_dram = nc.dram_tensor("row_dram", [ET, P], F32, kind="Internal").ap()
            c.zrow = m.sb("zrow", [1, 3 * P])
            c.last_edge = m.sb("last_edge", [P, NT], U32)
            c.sorted = m.sb("sorted", [ET, 3, P])
            c.row_l, c.att_l, c.col_l = m.sb("row_l", [P, ET]), m.sb("att_l", [P, ET]), m.sb("col_l", [P, ET], U32)
            c.run_on = m.sb("run_on", [ET, 1])
            with nc.Block() as block:
                @block.gpsimd
                def _(pool):
                    pool.memset(c.zrow[:, :], 0.0)
            sort_phase(nc, m, c, row, col)
            softmax_phase(nc, m, c, row_dram)
        if True:
            part_dram = nc.dram_tensor("part_dram", [EP + P, D], F32, kind="Internal").ap()
            edge_phase(nc, m, c, h_dram, row_dram, part_dram)
            carry_phase(nc, m, c, part_dram)
        if True:
            both_dram = nc.dram_tensor("both_dram", [NP, 2 * D], F32, kind="Internal").ap()
            c.logits, c.prob = m.sb("logits", [P, NT, NEXP]), m.sb("prob", [P, NT])
            c.gate_w, c.gate_b, c.mid = m.sb("gate_w", [P, CH, NEXP]), m.sb("gate_b", [P, NEXP]), m.sb("mid", [P, NB])
            c.scale, c.unscale = m.sb("scale", [P, 1]), m.sb("unscale", [P, 1])
            with ExitStack() as wctx:
                mw = Phase(nc, wctx, "ww")
                c.w_hi, c.w_lo = mw.sb("w_hi", [P, CH, NF, D], F16), mw.sb("w_lo", [P, CH, NF, D], F16)
                with nc.Block() as block:
                    s = m.sem("gate_loaded")

                    @block.sync
                    def _(sp):
                        sp.dma_start(c.gate_w[:, :, :], switch_w.rearrange("(c p) e -> p c e", p=P)).then_inc(s, 16)
                        sp.dma_start(c.gate_b[:, :], switch_b.broadcast_to([P, NEXP])).then_inc(s, 16)
                        sp.wait_ge(s, 32)

                    @block.gpsimd
                    def _(pool):
                        pool.iota(c.mid[:, :], [[-8, NB]], base=28, channel_multiplier=0, allow_small_or_imprecise_dtypes=True)
                weight_phase(nc, m, c, base_w, spline_w)
                layer_phase(nc, m, c, x, part_dram, both_dram, out)
            if True:
                c.slot_read, c.slot_write, c.slot_prob = m.sb("slot_read", [P, FT], U32), m.sb("slot_write", [P, FT], U32), m.sb("slot_prob", [P, FT])
                route_phase(nc, m, c)
                expert_phase(nc, m, c, expert_w, expert_b, both_dram, out)


def kernel(x, src, dst, L0_gnn_W, L0_gnn_a, L0_gnn_base_w, L0_gnn_spline_w, L0_ffn_switch_w,
           L0_ffn_switch_b, L0_ffn_expert_w, L0_ffn_expert_b):
    import numpy as np
    import concourse.bacc as bacc
    from concourse.bass_utils import run_bass_kernel_spmd as run

    lay = np.ascontiguousarray
    pad = EP - N_EDGES
    arrays = {
        "x": np.concatenate([x, np.zeros((NP - N_NODES, D), np.float32)]),
        "row": np.concatenate([src, np.full((pad,), PAD_ROW, np.int32)]).reshape(ET, P),
        "col": np.concatenate([dst, np.zeros((pad,), np.int32)]).reshape(ET, P),
        "wt": lay(np.transpose(L0_gnn_W)),
        "a2": lay(np.transpose(np.reshape(L0_gnn_a, (2, D)))),
        "base_w": lay(np.transpose(L0_gnn_base_w)),
        "spline_w": lay(np.transpose(L0_gnn_spline_w, (1, 2, 0))),
        "switch_w": lay(np.transpose(L0_ffn_switch_w)),
        "switch_b": np.reshape(L0_ffn_switch_b, (1, NEXP)),
        "expert_w": lay(np.transpose(L0_ffn_expert_w, (0, 2, 1))),
        "expert_b": lay(L0_ffn_expert_b),
    }
    nc = bacc.Bacc("TRN2", target_bir_lowering=False, num_devices=1)
    args = [nc.dram_tensor(f"in_{k}", a.shape, mybir.dt.from_np(a.dtype), kind="ExternalInput").ap()
            for k, a in arrays.items()]
    out = nc.dram_tensor("out_0", (NP, D), F32, kind="ExternalOutput").ap()
    build(nc, *args, out)
    r = run(nc, [{f"in_{k}": a for k, a in arrays.items()}], core_ids=[0])
    return r.results[0]["out_0"][:N_NODES]
```

```python
from contextlib import ExitStack

import concourse.bass as bass
from concourse import mybir

P = 128
N_NODES, D, N_EDGES = 10000, 512, 12500
CH = D // P
NT = 80
NP = NT * P
LT = -(-N_NODES // P)
ET = 98
EP = ET * P
PAD_ROW = NP - 1
NB = 8
NF = NB + 1
NEXP, CAP = 16, int(1.2 * N_NODES / 16)
ST = -(-CAP // P)
FT = NEXP * ST
EPS = 1e-5
BIG = 1e30
ALPHA = 0.2

F32, BF16, F16 = mybir.dt.float32, mybir.dt.bfloat16, mybir.dt.float16
I32, U32 = mybir.dt.int32, mybir.dt.uint32
ALU = mybir.AluOpType
ACT = mybir.ActivationFunctionType
AX = mybir.AxisListType


def wide(ap, shape):
    return ap.broadcast_to(shape)


def past(v):
    return max(v, 0) if isinstance(v, int) else v


class Phase:

    def __init__(self, nc, ctx, tag):
        self.nc, self.ctx, self.tag, self.sems = nc, ctx, tag, []
        ctx.callback(self.reset)

    def reset(self):
        with self.nc.Block() as block:

            @block.gpsimd
            def _(pool):
                for s in self.sems:
                    pool.sem_clear(s)

    def sb(self, name, shape, dt=F32):
        return self.ctx.enter_context(self.nc.sbuf_tensor(f"{self.tag}_{name}", shape, dt))

    def ps(self, name, shape, dt=F32):
        return self.ctx.enter_context(self.nc.psum_tensor(f"{self.tag}_{name}", shape, dt))

    def sem(self, name, n=None):
        def one(s):
            self.sems.append(self.ctx.enter_context(self.nc.semaphore(f"{self.tag}_{s}")))
            return self.sems[-1]

        return one(name) if n is None else [one(f"{name}{i}") for i in range(n)]


def swdge(c, n):
    return [c.swdge.pop() for _ in range(n)]


def constants(nc, m, c):
    with nc.Block() as block:
        ramp, cleared = m.sem("c_ramp"), m.sem("c_cleared")

        @block.gpsimd
        def _(pool):
            pool.iota(c.iota_f[:, :], [[1, P]], base=0, channel_multiplier=0,
                      allow_small_or_imprecise_dtypes=True)
            pool.iota(c.iota_p[:, :], [[0, 1]], base=0, channel_multiplier=1,
                      allow_small_or_imprecise_dtypes=True)
            pool.memset(c.ones[:, :], 1.0).then_inc(ramp, 1)
            pool.memset(c.ident[:, :], 0.0).then_inc(cleared, 1)
            pool.memset(c.tri[:, :], 0.0).then_inc(cleared, 1)
            pool.memset(c.after[:, :], 0.0).then_inc(cleared, 1)
            pool.wait_ge(cleared, 3)
            pool.affine_select(out=c.ident[:, :], in_=c.ident[:, :], compare_op=ALU.not_equal, fill=1.0,
                               base=0, pattern=[[-1, P]], channel_multiplier=1)
            pool.affine_select(out=c.tri[:, :], in_=c.tri[:, :], compare_op=ALU.is_ge, fill=1.0,
                               base=0, pattern=[[-1, P]], channel_multiplier=1)
            pool.affine_select(out=c.after[:, :], in_=c.after[:, :], compare_op=ALU.is_ge, fill=1.0,
                               base=0, pattern=[[1, P]], channel_multiplier=-1)


def node_phase(nc, m, c, x, wt, a2):
    U = 8
    H = U // 2
    with ExitStack() as ctx, nc.Block() as block:
        m = Phase(nc, ctx, "n")
        xt = [m.sb(f"x{b}", [P, D]) for b in range(U)]
        xT = [m.sb(f"xT{b}", [P, CH, P]) for b in range(2)]
        wt_sb = m.sb("wt", [P, CH, D])
        a_sb = m.sb("a", [P, CH, 2])
        a_wide = m.sb("a_wide", [P, 2, CH, P])
        wa = m.sb("wa", [P, CH, 2])
        wa_row = m.sb("wa_row", [P, 2, D])
        wa_sum = m.sb("wa_sum", [P, 2])
        stats = m.sb("stats", [P, U, 6])
        mv = m.sb("mv", [P, NT, 2])
        product2 = m.sb("product2", [P, 2, D])
        sum2, unused = m.sb("sum2", [P, 2]), m.sb("unused", [P, 2, D])
        mv_turn, mv_kept = m.sb("mv_turn", [P, U, 2]), m.sem("mv_kept")
        raw = m.sb("raw", [P, 2, NT])
        junk = m.sb("junk", [P, H, D])
        ve, rstd_turn, mhalf = m.sb("ve", [P, U]), m.sb("rstd_turn", [P, U]), m.sb("mhalf", [P, U])
        rstd, rstd_kept = m.sb("rstd", [P, NT]), m.sem("rstd_kept")
        psT = [m.ps(f"psT{b}", [P, CH, P]) for b in range(2)]
        psS = [m.ps(f"psS{b}", [P, 2]) for b in range(2)]
        psW = m.ps("psW", [P, CH, 2])
        psR = [m.ps(f"psR{k}", [P, D]) for k in range(2)]
        w_loaded, a_ready, wa_mm, wa_ready, row_mm, row_ready, half = (
            m.sem(s) for s in ("w_loaded", "a_ready", "wa_mm", "wa_ready", "row_mm", "row_ready", "half"))
        x_loaded = m.sem("x_loaded", U)
        bn_done, aggr_done, dots_done = m.sem("bn_done"), m.sem("aggr_done"), m.sem("dots_done")
        turned, copied, st_done, st_copied = (m.sem(s) for s in ("turned", "copied", "st_done", "st_copied"))
        product2_ready, sum2_ready, sum2_kept = m.sem("product2_ready"), m.sem("sum2_ready"), m.sem("sum2_kept")
        ve_ready, rstd_ready, fixed = m.sem("ve_ready"), m.sem("rstd_ready"), m.sem("fixed")
        x_t = x.rearrange("(t p) d -> t p d", p=P)
        K = NT // U

        @block.sync
        def _(sp):
            sp.dma_start(wt_sb[:, :, :], wt.rearrange("(c p) i -> p c i", p=P)).then_inc(w_loaded, 16)
            sp.dma_start(a_sb[:, :, :], a2.rearrange("(c p) k -> p c k", p=P)).then_inc(w_loaded, 16)
            for b in range(U):
                sp.dma_start(xt[b][:, :], x_t[b, :, :]).then_inc(x_loaded[b], 16)
            with sp.Fori(0, K - 1) as k:
                for b in range(U):
                    sp.wait_ge(dots_done, k * H + b // 2 + 1)
                    if b % 2 == 0:
                        sp.wait_ge(turned, k * H + b // 2 + 1)
                    else:
                        sp.wait_ge(product2_ready, k * H + b // 2 + 1)
                    sp.dma_start(xt[b][:, :], x_t[bass.ds(k * U + U + b, 1), :, :].squeeze(0)).then_inc(x_loaded[b], 16)

        @block.gpsimd
        def _(pool):
            pool.memset(mhalf[:, :], -0.5).then_inc(half, 1)
            pool.wait_ge(half, 1)
            pool.wait_ge(row_ready, 1)

            def turn(k):
                for p in range(H):
                    pool.wait_ge(x_loaded[2 * p + 1], 16 * (k + 1))
                    pool.wait_ge(sum2_ready, past(k * H + p - 1))
                    pool.tensor_tensor(product2[:, p % 2, :], xt[2 * p + 1][:, :], wa_row[:, 1, :], ALU.mult).then_inc(product2_ready, 1)
                pool.wait_ge(aggr_done, k * H + H)
                pool.wait_ge(rstd_kept, k)
                pool.nop(nofuse=True)
                pool.tensor_scalar(ve[:, :], mv_turn[:, :, 1], EPS, None, ALU.add).then_inc(ve_ready, 1)
                pool.wait_ge(ve_ready, k + 1)
                pool.tensor_tensor(rstd_turn[:, :], ve[:, :], mhalf[:, :], ALU.pow).then_inc(rstd_ready, 1)
                pool.wait_ge(rstd_ready, k + 1)
                pool.tensor_copy(rstd[:, bass.ds(k * U, U)], rstd_turn[:, :]).then_inc(rstd_kept, 1)

            turn(0)
            with pool.Fori(1, K) as k:
                turn(k)

        @block.vector
        def _(dve):
            dve.wait_ge(w_loaded, 32)
            for k in range(2):
                for co in range(CH):
                    done = dve.tensor_scalar(a_wide[:, k, co, :], c.ones[:, :], a_sb[:, co, k:k + 1], None, ALU.mult)
            done.then_inc(a_ready, 1)
            dve.wait_ge(row_mm, 1)
            for k in range(2):
                done = dve.tensor_copy(wa_row[:, k, :], psR[k][:, :])
            done.then_inc(row_ready, 1)
            dve.wait_ge(row_ready, 1)
            dve.tensor_reduce(wa_sum[:, :], wa_row[:, :, :], AX.X, ALU.add)

            def turn(k):
                for p in range(H):
                    dve.wait_ge(aggr_done, past(k * H + p - 3))
                    for b in (2 * p, 2 * p + 1):
                        dve.wait_ge(x_loaded[b], 16 * (k + 1))
                        dve.bn_stats(stats[:, b, :], xt[b][:, :]).then_inc(bn_done, 1)
                    second = k * U + 2 * p + 1
                    dve.scalar_tensor_tensor(junk[:, p, :], xt[2 * p + 1][:, :], 1.0, wa_row[:, 0, :], ALU.mult, ALU.mult,
                                             accum_out=raw[:, 0, bass.ds(second, 1)]).then_inc(dots_done, 1)
                    dve.wait_ge(bn_done, k * U + 2 * p + 2)
                    dve.wait_ge(mv_kept, k)
                    dve.wait_ge(ve_ready, k)
                    dve.nop(nofuse=True)
                    for b in (2 * p, 2 * p + 1):
                        done = dve.bn_aggr(mv_turn[:, b, :], stats[:, b, :])
                    done.then_inc(aggr_done, 1)
                dve.wait_ge(aggr_done, k * H + H)
                dve.tensor_copy(mv[:, bass.ds(k * U, U), :], mv_turn[:, :, :]).then_inc(mv_kept, 1)

            turn(0)
            with dve.Fori(1, K) as k:
                turn(k)
            dve.wait_ge(mv_kept, K)
            dve.wait_ge(st_copied, NT // 2)
            dve.wait_ge(sum2_kept, NT // 2)
            dve.wait_ge(dots_done, NT // 2)
            dve.tensor_scalar(wa_sum[:, :], wa_sum[:, :], -1.0, None, ALU.mult).then_inc(fixed, 1)
            dve.wait_ge(fixed, 1)
            for j in range(2):
                dve.scalar_tensor_tensor(raw[:, j, :], mv[:, :, 0], wa_sum[:, j:j + 1], raw[:, j, :], ALU.mult, ALU.add).then_inc(fixed, 1)
            dve.wait_ge(fixed, 3)
            dve.wait_ge(rstd_kept, K)
            for j in range(2):
                dve.tensor_tensor(c.st[:, j, :], raw[:, j, :], rstd[:, :], ALU.mult)

        @block.tensor
        def _(pe):
            pe.wait_ge(w_loaded, 32)
            pe.wait_ge(a_ready, 1)
            for k in range(2):
                for co in range(CH):
                    mm = pe.matmul(psR[k][:, :], a_wide[:, k, co, :], wt_sb[:, co, :], start=co == 0, stop=co == CH - 1)
            mm.then_inc(row_mm, 1)
            for ci in range(CH):
                for co in range(CH):
                    mm = pe.matmul(psW[:, ci, :], wt_sb[:, co, ci * P:(ci + 1) * P], a_sb[:, co, :],
                                   start=co == 0, stop=co == CH - 1)
            mm.then_inc(wa_mm, 1)
            pe.wait_ge(wa_ready, 1)

            def transposes(k, p):
                pe.wait_ge(x_loaded[2 * p], 16 * (k + 1))
                pe.wait_ge(copied, past(k * H + p - 1))
                for ch in range(CH):
                    t = pe.transpose(psT[p % 2][:, ch, :], xt[2 * p][:, ch * P:(ch + 1) * P], c.ident[:, :])
                t.then_inc(turned, 1)

            def product(n, b):
                pe.wait_ge(copied, n + 1)
                pe.wait_ge(st_copied, past(n - 1))
                for ch in range(CH):
                    mm = pe.matmul(psS[b][:, :], xT[b][:, ch, :], wa[:, ch, :], start=ch == 0, stop=ch == CH - 1)
                mm.then_inc(st_done, 1)

            def turn(k):
                for p in range(H):
                    transposes(k, p)
                    if p > 0 or not isinstance(k, int):
                        product(k * H + p - 1, (p - 1) % 2)

            turn(0)
            with pe.Fori(1, K) as k:
                turn(k)
            product(NT // 2 - 1, 1)

        @block.scalar
        def _(act):
            act.wait_ge(wa_mm, 1)
            act.copy(wa[:, :, :], psW[:, :, :]).then_inc(wa_ready, 1)

            def scores(n, b):
                act.wait_ge(st_done, n + 1)
                act.copy(raw[:, :, bass.ds(n * 2, 1)].rearrange("p a b -> p (a b)"), psS[b][:, :]).then_inc(st_copied, 1)
                act.wait_ge(product2_ready, n + 1)
                act.wait_ge(sum2_kept, past(n - 1))
                act.activation(unused[:, b, :], product2[:, b, :], ACT.Copy, accum_out=sum2[:, b:b + 1]).then_inc(sum2_ready, 1)
                act.wait_ge(sum2_ready, n + 1)
                act.copy(raw[:, 1, bass.ds(n * 2 + 1, 1)], sum2[:, b:b + 1]).then_inc(sum2_kept, 1)

            def turn(k):
                for p in range(H):
                    n = k * H + p
                    act.wait_ge(turned, n + 1)
                    act.wait_ge(st_done, past(n - 1))
                    act.copy(xT[p % 2][:, :, :], psT[p % 2][:, :, :]).then_inc(copied, 1)
                    if p > 0 or not isinstance(k, int):
                        scores(n - 1, (p - 1) % 2)

            turn(0)
            with act.Fori(1, K) as k:
                turn(k)
            scores(NT // 2 - 1, 1)


def sort_phase(nc, m, c, row, col, base_w, spline_w):
    U = 2
    with ExitStack() as ctx:
        m = Phase(nc, ctx, "s")
        rowb = m.sb("rowb", [P, ET, P], I32)
        nat = m.sb("nat", [ET, 2, P], I32)
        natf = m.sb("natf", [ET, 2, P])
        payload = m.sb("payload", [P, 3, ET])
        rc, score = payload[:, 0:2, :], payload[:, 2, :]
        rci = m.sb("rci", [P, 2, ET], I32)
        lowi = m.sb("lowi", [P, 2, ET], I32)
        low = m.sb("low", [P, 2, ET])
        high = m.sb("high", [P, 2, ET])
        one_low = m.sb("one_low", [P, 2, ET, P], BF16)
        one_high = m.sb("one_high", [P, ET, 2, NT], BF16)
        ident = m.sb("ident", [P, P], BF16)
        count = m.sb("count", [P, NT])
        start = m.sb("start", [P, NT])
        base = m.sb("base", [P, NT])
        zeros = m.sb("zeros", [P, NT])
        some = m.sb("some", [P, NT])
        last = m.sb("last", [P, NT])
        running = m.sb("running", [P, U, 2, NT])
        hotT = m.sb("hotT", [P, U, 2, P])
        junk = m.sb("junk", [P, U, P + 3 * NT])
        rank = m.sb("rank", [P, ET])
        first = m.sb("first", [P, ET])
        pos = m.sb("pos", [P, ET])
        posi = m.sb("posi", [P, ET], I32)
        poshi = m.sb("poshi", [P, ET], I32)
        pos_tile = m.sb("pos_tile", [P, ET])
        pos_lane = m.sb("pos_lane", [P, ET])
        B3 = 4
        tile_hot = [m.sb(f"tile_hot{b}", [P, ET]) for b in range(B3)]
        lane_hot = [m.sb(f"lane_hot{b}", [P, P]) for b in range(B3)]
        values = [m.sb(f"values{b}", [P, 3, P]) for b in range(B3)]
        psC = m.ps("psC", [P, NT])
        psX = m.ps("psX", [P, 2, P])
        psH = [psC[:, :], psX[:, 0, 0:NT]]
        psT = [m.ps(f"psT{b}", [P, 2, P], BF16) for b in range(U)]
        psG = [m.ps(f"psG{b}", [P, 3, NT]) for b in range(U)]
        psV = m.ps("psV", [ET, 3, P])
        step = m.sem("step")
        row_bc, nat_loaded, split_ready = m.sem("row_bc"), m.sem("nat_loaded"), m.sem("split_ready")

        with nc.Block() as block:
            turned, counted, summed = m.sem("turned"), m.sem("counted"), m.sem("summed")

            @block.sync
            def _(sp):
                sp.dma_start(nat[:, 0, :], row).then_inc(nat_loaded, 16)
                sp.dma_start(nat[:, 1, :], col).then_inc(nat_loaded, 16)
                sp.dma_start(rowb[:, :, :].rearrange("p t e -> p (t e)"),
                             row.rearrange("(o t) p -> o (t p)", o=1).broadcast_to([P, EP])).then_inc(row_bc, 16)
                load_weights(sp, c, base_w, spline_w, range(EARLY))
                sp.wait_ge(row_bc, 16)

            @block.vector
            def _(dve):
                dve.wait_ge(nat_loaded, 32)
                dve.tensor_copy(natf[:, :, :], nat[:, :, :]).then_inc(step, 1)
                dve.memset(zeros[:, :], 0.0)
                dve.tensor_copy(ident[:, :], c.ident[:, :])
                for b in range(U):
                    dve.tensor_copy(running[:, b, 1, :], c.st[:, 0, :])
                dve.wait_ge(turned, 1)
                dve.tensor_copy(rc, psX[:, :, 0:ET]).then_inc(step, 1)
                dve.wait_ge(step, 2)
                dve.tensor_copy(rci[:, :, :], rc).then_inc(step, 1)
                dve.wait_ge(step, 3)
                dve.tensor_scalar(lowi[:, :, :], rci[:, :, :], P - 1, None, ALU.bitwise_and).then_inc(step, 1)
                dve.wait_ge(step, 4)
                dve.tensor_copy(low[:, :, :], lowi[:, :, :]).then_inc(step, 1)
                dve.wait_ge(step, 5)
                dve.tensor_tensor(high[:, :, :], rc, low[:, :, :], ALU.subtract).then_inc(step, 1)
                dve.wait_ge(step, 6)
                dve.tensor_scalar(high[:, :, :], high[:, :, :], 1.0 / P, None, ALU.mult).then_inc(split_ready, 1)
                dve.wait_ge(split_ready, 1)
                dve.tensor_tensor(one_low[:, 0, :, :], wide(c.iota_f[:, :].unsqueeze(1), [P, ET, P]),
                                  wide(low[:, 0, :].unsqueeze(2), [P, ET, P]), ALU.is_equal)
                dve.tensor_tensor(one_high[:, :, 0, :], wide(c.iota_f[:, 0:NT].unsqueeze(1), [P, ET, NT]),
                                  wide(high[:, 0, :].unsqueeze(2), [P, ET, NT]), ALU.is_equal).then_inc(step, 1)
                dve.tensor_tensor(one_low[:, 1, :, :], wide(c.iota_f[:, :].unsqueeze(1), [P, ET, P]),
                                  wide(low[:, 1, :].unsqueeze(2), [P, ET, P]), ALU.is_equal)
                dve.tensor_tensor(one_high[:, :, 1, :], wide(c.iota_f[:, 0:NT].unsqueeze(1), [P, ET, NT]),
                                  wide(high[:, 1, :].unsqueeze(2), [P, ET, NT]), ALU.is_equal)
                dve.wait_ge(counted, 1)
                dve.tensor_copy(count[:, :], psC[:, :]).then_inc(step, 1)
                dve.wait_ge(summed, 1)
                dve.tensor_tensor_scan(base[:, :], psX[:, 0, 0:NT], zeros[:, :], 0.0, ALU.add, ALU.add).then_inc(step, 1)
                dve.wait_ge(step, 9)
                dve.tensor_tensor(base[:, :], base[:, :], psX[:, 0, 0:NT], ALU.subtract).then_inc(step, 1)
                dve.wait_ge(step, 10)
                dve.tensor_tensor(start[:, :], psX[:, 1, 0:NT], base[:, :], ALU.add).then_inc(step, 1)
                dve.tensor_scalar(some[:, :], count[:, :], 0.0, None, ALU.is_gt).then_inc(step, 1)
                dve.wait_ge(step, 12)
                dve.tensor_copy(running[:, 0, 0, :], start[:, :])
                dve.tensor_tensor(last[:, :], start[:, :], count[:, :], ALU.add).then_inc(step, 1)
                dve.wait_ge(step, 13)
                dve.scalar_tensor_tensor(last[:, :], last[:, :], -1.0 - EP, some[:, :], ALU.add, ALU.mult).then_inc(step, 1)
                dve.wait_ge(step, 14)
                dve.tensor_scalar(c.last_edge[:, :], last[:, :], float(EP), None, ALU.add)

            @block.tensor
            def _(pe):
                pe.wait_ge(step, 1)
                pe.transpose(psX[:, 0, 0:ET], natf[:, 0, :], c.ident[0:ET, 0:ET])
                pe.transpose(psX[:, 1, 0:ET], natf[:, 1, :], c.ident[0:ET, 0:ET]).then_inc(turned, 1)
                pe.wait_ge(step, 7)
                V = 14

                def histogram(k):
                    for t in range(V):
                        at = bass.ds(k * V + t, 1)
                        g = pe.matmul(psC[:, :], one_low[:, 0, at, :].squeeze(1), one_high[:, at, 0, :].squeeze(1),
                                      start=isinstance(k, int) and k == t == 0, stop=isinstance(k, int) and k > 0 and t == V - 1)
                    return g

                histogram(0)
                with pe.Fori(1, ET // V - 1) as k:
                    histogram(k)
                histogram(ET // V - 1).then_inc(counted, 1)
                pe.wait_ge(step, 8)
                pe.matmul(psX[:, 0, 0:NT], c.ones[:, :], count[:, :], start=True, stop=True)
                pe.matmul(psX[:, 1, 0:NT], c.tri[:, :], count[:, :], start=True, stop=True).then_inc(summed, 1)

        with nc.Block() as block:
            hist_done, hot_turned, hots_ready, looked_up, added = (
                m.sem(s) for s in ("hist_done", "hot_turned", "hots_ready", "looked_up", "added"))
            picked = m.sem("picked")

            def turns(eng, tile, buffers=U):
                V = 8
                for t in range(V):
                    tile(t, t % buffers)
                with eng.Fori(1, ET // V) as k:
                    for n in range(V):
                        tile(k * V + n, n % buffers)
                for t in range(ET // V * V, ET):
                    tile(t, t % buffers)

            @block.tensor
            def _(pe):
                def ahead(t, b):
                    pe.wait_ge(added, past(t - 1))
                    pe.matmul(psH[b], one_low[:, 0, bass.ds(t, 1), :].squeeze(1),
                              one_high[:, bass.ds(t, 1), 0, :].squeeze(1), start=True, stop=True).then_inc(hist_done, 1)
                    pe.wait_ge(hots_ready, past(t - 1))
                    pe.nop(nofuse=True)
                    for j in range(2):
                        g = pe.transpose(psT[b][:, j, :], one_low[:, j, bass.ds(t, 1), :].squeeze(1), ident[:, :])
                    g.then_inc(hot_turned, 1)

                def tile(t, b):
                    if not (isinstance(t, int) and t + 1 == ET):
                        ahead(t + 1, 1 - b)
                    pe.wait_ge(hots_ready, t + 1)
                    pe.wait_ge(added, t)
                    pe.wait_ge(picked, past(t - 1))
                    pe.matmul(psG[b][:, 0:2, :], hotT[:, b, 0, :], running[:, b, :, :], start=True, stop=True)
                    pe.matmul(psG[b][:, 2, :], hotT[:, b, 1, :], c.st[:, 1, :], start=True, stop=True).then_inc(looked_up, 1)

                ahead(0, 0)
                turns(pe, tile)

            @block.scalar
            def _(act):
                def tile(t, b):
                    act.wait_ge(hot_turned, t + 1)
                    act.wait_ge(looked_up, past(t - 1))
                    act.copy(hotT[:, b, :, :], psT[b][:, :, :]).then_inc(hots_ready, 1)

                turns(act, tile)

            @block.vector
            def _(dve):
                def pick(t, b):
                    at = bass.ds(t, 1)
                    dve.scalar_tensor_tensor(junk[:, b, P:P + NT], psG[b][:, 0, :], 1.0, one_high[:, at, 0, :].squeeze(1),
                                             ALU.mult, ALU.mult, accum_out=first[:, at])
                    dve.scalar_tensor_tensor(junk[:, b, P + NT:].rearrange("p (a n) -> p a n", a=2), psG[b][:, 1:3, :], 1.0,
                                             one_high[:, at, :, :].squeeze(1), ALU.mult, ALU.mult,
                                             accum_out=score[:, at]).then_inc(picked, 1)

                def tile(t, b):
                    at = bass.ds(t, 1)
                    dve.wait_ge(hist_done, t + 1)
                    dve.wait_ge(added, t)
                    dve.wait_ge(looked_up, t)
                    dve.tensor_tensor(running[:, 1 - b, 0, :], running[:, b, 0, :], psH[b], ALU.add).then_inc(added, 1)
                    if not (isinstance(t, int) and t == 0):
                        pick(t - 1, 1 - b)
                    dve.scalar_tensor_tensor(junk[:, b, 0:P], rowb[:, at, :].squeeze(1), rc[:, 0, at], c.after[:, :],
                                             ALU.is_equal, ALU.mult, accum_out=rank[:, at])

                turns(dve, tile)
                dve.wait_ge(looked_up, ET)
                pick(ET - 1, 1)

        with nc.Block() as block:
            place_ready, lane_ready, values_ready, hot_ready, moved, all_moved = (
                m.sem(s) for s in ("place_ready", "lane_ready", "values_ready", "hot_ready", "moved", "all_moved"))
            s3 = m.sem("s3")

            @block.scalar
            def _(act):
                def tile(t, b):
                    act.wait_ge(lane_ready, t + 1)
                    act.wait_ge(moved, past(t - B3 + 1))
                    for j in range(2):
                        done = act.activation(values[b][:, j, :], lane_hot[b][:, :], ACT.Copy, scale=payload[:, j, bass.ds(t, 1)])
                    done.then_inc(values_ready, 1)

                turns(act, tile, B3)

            @block.vector
            def _(dve):
                dve.tensor_tensor(pos[:, :], first[:, :], rank[:, :], ALU.add).then_inc(s3, 1)
                dve.wait_ge(s3, 1)
                dve.tensor_copy(posi[:, :], pos[:, :]).then_inc(s3, 1)
                dve.wait_ge(s3, 2)
                dve.tensor_scalar(poshi[:, :], posi[:, :], 7, None, ALU.logical_shift_right).then_inc(s3, 1)
                dve.wait_ge(s3, 3)
                dve.tensor_copy(pos_tile[:, :], poshi[:, :]).then_inc(s3, 1)
                dve.wait_ge(s3, 4)
                dve.scalar_tensor_tensor(pos_lane[:, :], pos_tile[:, :], -float(P), pos[:, :], ALU.mult, ALU.add).then_inc(place_ready, 1)
                dve.wait_ge(place_ready, 1)

                def tile(t, b):
                    at = bass.ds(t, 1)
                    dve.wait_ge(values_ready, past(t - B3 + 1))
                    dve.tensor_scalar(lane_hot[b][:, :], c.iota_f[:, :], pos_lane[:, at], None, ALU.is_equal).then_inc(lane_ready, 1)
                    dve.wait_ge(moved, past(t - B3 + 1))
                    dve.tensor_scalar(tile_hot[b][:, :], c.iota_f[:, 0:ET], pos_tile[:, at], None, ALU.is_equal)
                    dve.tensor_scalar(values[b][:, 2, :], c.iota_f[:, :], pos_lane[:, at], score[:, at],
                                      ALU.is_equal, ALU.mult).then_inc(hot_ready, 1)

                turns(dve, tile, B3)
                dve.wait_ge(all_moved, 1)
                dve.tensor_copy(c.sorted[:, :, :], psV[:, :, :])

            @block.tensor
            def _(pe):
                pe.matmul(psV[:, :, :], zeros_row(c)[:, 0:ET], zeros_row(c)[:, :], start=True, stop=False)

                def tile(t, b):
                    pe.wait_ge(values_ready, t + 1)
                    pe.wait_ge(hot_ready, t + 1)
                    pe.matmul(psV[:, :, :], tile_hot[b][:, :], values[b][:, :, :], start=False, stop=False).then_inc(moved, 1)

                turns(pe, tile, B3)
                pe.matmul(psV[:, :, :], zeros_row(c)[:, 0:ET], zeros_row(c)[:, :], start=False, stop=True).then_inc(all_moved, 1)


def zeros_row(c):
    return c.zrow[:, :]


def softmax_phase(nc, m, c, row_dram):
    with ExitStack() as ctx:
        m = Phase(nc, ctx, "a")
        row, col, score = c.sorted[:, 0, :], c.sorted[:, 1, :], c.sorted[:, 2, :]
        e, ex, tot = (m.sb(s, [ET, P]) for s in ("e", "ex", "tot"))
        row1 = m.sb("row1", [ET, P])
        near = m.sb("near", [ET, 2, P])
        same = m.sb("same", [ET, 2, P])
        wall = m.sb("wall", [ET, 2, P])
        through = m.sb("through", [ET, 2, 2])
        scan = m.sb("scan", [ET, 2, P])
        ends = m.sb("ends", [1, 4, ET])
        carried = m.sb("carried", [1, 2, P])
        carry = m.sb("carry", [ET, 2])
        shift = m.sb("shift", [ET, 2, ET])
        ps = m.ps("ps", [P, 4, P])
        ps1 = m.ps("ps1", [1, 4, P])
        psc = m.ps("psc", [ET, 2])
        with nc.Block() as block:
            v, t, landed = m.sem("v"), m.sem("t"), m.sem("landed")
            done = {"v": 0, "t": 0}

            def vec(dve, ins):
                done["v"] += 1
                ins.then_inc(v, 1)
                return done["v"]

            @block.vector
            def _(dve):
                n = 0

                def step(ins):
                    nonlocal n
                    ins.then_inc(v, 1)
                    n += 1
                    dve.wait_ge(v, n)

                dve.memset(shift[:, :, :], 0.0).then_inc(v, 1)
                n += 1
                dve.wait_ge(v, n)
                dve.tensor_copy(shift[:, 0, 1:ET], c.ident[0:ET, 0:ET - 1])
                step(dve.tensor_copy(shift[:, 1, 0:ET - 1], c.ident[0:ET, 1:ET]))
                step(dve.tensor_scalar(row1[:, :], row, 1.0, None, ALU.add))
                dve.wait_ge(t, 1)
                dve.tensor_copy(near[:, 0, 1:P], row[:, 0:P - 1])
                dve.tensor_copy(near[:, 1, 0:P - 1], row[:, 1:P])
                dve.tensor_scalar(near[:, 0, 0:1], psc[:, 0:1], -1.0, None, ALU.add)
                step(dve.tensor_scalar(near[:, 1, P - 1:P], psc[:, 1:2], -1.0, None, ALU.add))
                dve.tensor_tensor(same[:, 0, :], near[:, 0, :], row, ALU.is_equal)
                step(dve.tensor_tensor(same[:, 1, :], near[:, 1, :], row, ALU.is_equal))
                step(dve.tensor_scalar(wall[:, :, :], same[:, :, :], -1.0, BIG, ALU.add, ALU.mult))
                dve.tensor_reduce(through[:, :, 0], wall[:, :, :], AX.X, ALU.min)
                dve.tensor_reduce(through[:, :, 1], same[:, :, :], AX.X, ALU.min)
                step(dve.scalar_tensor_tensor(e[:, :], score, ALPHA, score, ALU.mult, ALU.max))
                turn = 1
                for what, (value, gate, k, op0, op1, low) in enumerate((
                        (e, wall, 0, ALU.add, ALU.max, -BIG), (ex, same, 1, ALU.mult, ALU.add, 0.0))):
                    def scans(initial):
                        f = dve.tensor_tensor_scan(scan[:, 0, :], gate[:, 0, :], value[:, :], initial(0), op0, op1)
                        step(dve.tensor_tensor_scan(scan[:, 1, ::-1], gate[:, 1, ::-1], value[:, ::-1], initial(1), op0, op1))

                    scans(lambda d: low)
                    turn += 1
                    dve.wait_ge(t, turn)
                    step(dve.tensor_copy(ends[:, :, :], ps1[:, :, 0:ET]))
                    dve.tensor_tensor_scan(carried[:, 0, 0:ET], ends[:, 2, 0:ET], ends[:, 0, 0:ET], low, op0, op1)
                    step(dve.tensor_tensor_scan(carried[:, 1, 0:ET][:, ::-1], ends[:, 3, 0:ET][:, ::-1],
                                                ends[:, 1, 0:ET][:, ::-1], low, op0, op1))
                    turn += 1
                    dve.wait_ge(t, turn)
                    step(dve.tensor_copy(carry[:, :], psc[:, :]))
                    turn += 1
                    dve.wait_ge(t, turn)
                    step(dve.tensor_copy(carry[:, :], psc[:, :]))
                    scans(lambda d: carry[:, d:d + 1])
                    if what == 0:
                        step(dve.tensor_tensor(tot[:, :], scan[:, 0, :], scan[:, 1, :], ALU.max))
                        step(dve.tensor_tensor(tot[:, :], e[:, :], tot[:, :], ALU.subtract))
                        turn += 1
                        dve.wait_ge(t, turn)
                    else:
                        step(dve.tensor_tensor(tot[:, :], scan[:, 0, :], scan[:, 1, :], ALU.add))
                        step(dve.tensor_tensor(tot[:, :], tot[:, :], ex[:, :], ALU.subtract))
                        step(dve.reciprocal(tot[:, :], tot[:, :]))
                        step(dve.tensor_tensor(ex[:, :], ex[:, :], tot[:, :], ALU.mult))
                step(dve.tensor_tensor(carry[:, 0:1], row1[:, P - 1:P], same[:, 1, P - 1:P], ALU.mult))
                step(dve.tensor_scalar(c.run_on[:, :], carry[:, 0:1], -1.0, None, ALU.add))
                turn += 1
                dve.wait_ge(t, turn)
                dve.tensor_copy(c.row_l[:, :], ps[:, 0, 0:ET])
                dve.tensor_copy(c.col_l[:, :], ps[:, 1, 0:ET])
                dve.tensor_copy(c.att_l[:, :], ps[:, 2, 0:ET])
                done["v"] = n

            @block.tensor
            def _(pe):
                pe.wait_ge(v, 3)
                pe.matmul(psc[:, 0:1], shift[:, 0, :], row1[:, P - 1:P], start=True, stop=True)
                pe.matmul(psc[:, 1:2], shift[:, 1, :], row1[:, 0:1], start=True, stop=True).then_inc(t, 1)
                at = 7
                for k in range(2):
                    at += 1
                    pe.wait_ge(v, at)
                    for d, end in ((0, P - 1), (1, 0)):
                        pe.matmul(ps1[:, d, 0:ET], scan[:, d, end:end + 1], c.ident[0:ET, 0:ET], start=True, stop=True)
                        g = pe.matmul(ps1[:, 2 + d, 0:ET], through[:, d, k:k + 1], c.ident[0:ET, 0:ET], start=True, stop=True)
                    g.then_inc(t, 1)
                    at += 2
                    pe.wait_ge(v, at)
                    for d in range(2):
                        g = pe.matmul(psc[:, d:d + 1], carried[:, d, 0:ET], c.ones[0:1, 0:1], start=True, stop=True)
                    g.then_inc(t, 1)
                    at += 1
                    pe.wait_ge(v, at)
                    for d in range(2):
                        g = pe.matmul(psc[:, d:d + 1], shift[:, d, :], carry[:, d:d + 1], start=True, stop=True)
                    g.then_inc(t, 1)
                    at += 2 + 2
                    if k == 1:
                        at += 2
                at += 2
                pe.wait_ge(v, at)
                for j, a in enumerate((row, col, ex[:, :])):
                    g = pe.transpose(ps[:, j, 0:ET], a, c.ident[0:ET, 0:ET])
                g.then_inc(t, 1)

            @block.scalar
            def _(act):
                act.wait_ge(v, 7 + 8)
                act.activation(ex[:, :], tot[:, :], ACT.Exp).then_inc(t, 1)

            @block.sync
            def _(sp):
                sp.dma_start(row_dram, row).then_inc(landed, 16)
                sp.wait_ge(landed, 16)
                sp.dma_start(c.rowb[:, :, :].rearrange("p t e -> p (t e)"),
                             row_dram.rearrange("(o t) p -> o (t p)", o=1).broadcast_to([P, EP])).then_inc(landed, 16)
                sp.wait_ge(landed, 32)

def edge_phase(nc, m, c, x, part_dram, base_w, spline_w):
    U = 7
    G = ET // U
    with ExitStack() as ctx, nc.Block() as block:
        m = Phase(nc, ctx, "e")
        rowb = c.rowb
        index = [[m.sb(f"index{h}_{b}", [P, 1], U32) for b in range(U)] for h in range(2)]
        got = [[m.sb(f"got{h}_{b}", [P, D]) for b in range(U)] for h in range(2)]
        stats, mv = [m.sb(f"stats{h}", [P, U, 6]) for h in range(2)], [m.sb(f"mv{h}", [P, U, 2]) for h in range(2)]
        ve, rstd = [m.sb(f"ve{h}", [P, U]) for h in range(2)], [m.sb(f"rstd{h}", [P, U]) for h in range(2)]
        mhalf = m.sb("mhalf", [P, U])
        normal = [m.sb(f"normal{b}", [P, D]) for b in range(U)]
        weight = [m.sb(f"weight{b}", [P, P]) for b in range(U)]
        part = [m.sb(f"part{b}", [P, D]) for b in range(U)]
        none = m.sb("none", [P, D])
        ps = [m.ps(f"ps{b}", [P, D]) for b in range(U)]
        zeroed, zero_stored = m.sem("zeroed"), m.sem("zero_stored")
        index_ready, gathered = m.sem("index_ready"), swdge(c, 2)
        bn_done, mv_ready, ve_ready, rstd_ready = (m.sem(s) for s in ("bn_done", "mv_ready", "ve_ready", "rstd_ready"))
        weight_ready, normal_ready, summed, copied = (m.sem(s) for s in ("weight_ready", "normal_ready", "summed", "copied"))
        stored = m.sem("stored", U)
        part_t = part_dram.rearrange("(t p) d -> t p d", p=P)

        def groups(eng, step):
            for g in range(4):
                step(g, g // 2, g % 2, lambda n: n < G)
            with eng.Fori(2, G // 2 - 1) as k:
                for h in range(2):
                    step(k * 2 + h, k, h, lambda n: True)
            for g in range(G - 2, G):
                step(g, g // 2, g % 2, lambda n: isinstance(n, int) and n < G)

        @block.gpsimd
        def _(pool):
            pool.memset(none[:, :], 0.0).then_inc(zeroed, 1)
            pool.memset(mhalf[:, :], -0.5).then_inc(zeroed, 1)

            def indices(g, h):
                for b in range(U):
                    pool.tensor_copy(index[h][b][:, :], c.col_l[:, bass.ds(g * U + b, 1)]).then_inc(index_ready, 1)

            def gather(g, h):
                for b in range(U):
                    pool.wait_ge(index_ready, g * U + b + 1)
                    pool.wait_ge(normal_ready, past(U * (g - 2) + b + 1))
                    pool.nop(nofuse=True)
                    pool.indirect_dma_start(got[h][b][:, :], None, x,
                                            bass.IndirectOffsetOnAxis(index[h][b][:, :], 0)).then_inc(gathered[h], 16)

            def step(g, k, h, ok):
                pool.wait_ge(mv_ready, g + 1)
                pool.wait_ge(normal_ready, past(U * (g - 1)))
                pool.nop(nofuse=True)
                pool.tensor_scalar(ve[h][:, :], mv[h][:, :, 1], EPS, None, ALU.add).then_inc(ve_ready, 1)
                pool.wait_ge(ve_ready, g + 1)
                pool.tensor_tensor(rstd[h][:, :], ve[h][:, :], mhalf[:, :], ALU.pow).then_inc(rstd_ready, 1)
                if ok(g + 2):
                    indices(g + 2, h)
                    gather(g + 2, h)

            for g in range(2):
                indices(g, g)
                gather(g, g)
            pool.wait_ge(zeroed, 2)
            groups(pool, step)

        @block.vector
        def _(dve):
            def statistics(g, k, h):
                dve.wait_ge(gathered[h], 16 * U * (k + 1))
                for b in range(U):
                    done = dve.bn_stats(stats[h][:, b, :], got[h][b][:, :])
                done.then_inc(bn_done, 1)
                dve.wait_ge(bn_done, g + 1)
                dve.nop(nofuse=True)
                for b in range(U):
                    done = dve.bn_aggr(mv[h][:, b, :], stats[h][:, b, :])
                done.then_inc(mv_ready, 1)

            def step(g, k, h, ok):
                for b in range(U):
                    at = bass.ds(g * U + b, 1)
                    dve.wait_ge(summed, past(U * (g - 1) + b + 1))
                    dve.tensor_scalar(weight[b][:, :], rowb[:, at, :].squeeze(1), c.row_l[:, at], c.att_l[:, at],
                                      ALU.is_equal, ALU.mult).then_inc(weight_ready, 1)
                dve.wait_ge(rstd_ready, g + 1)
                for b in range(U):
                    dve.tensor_scalar(normal[b][:, :], got[h][b][:, :], mv[h][:, b, 0:1], rstd[h][:, b:b + 1],
                                      ALU.subtract, ALU.mult).then_inc(normal_ready, 1)
                if ok(g + 1):
                    statistics(g + 1, k + h, 1 - h)

            statistics(0, 0, 0)
            groups(dve, step)

        @block.tensor
        def _(pe):
            def step(g, k, h, ok):
                for b in range(U):
                    pe.wait_ge(weight_ready, g * U + b + 1)
                    pe.wait_ge(normal_ready, g * U + b + 1)
                    pe.wait_ge(copied, past(U * (g - 1) + b + 1))
                    pe.matmul(ps[b][:, :], weight[b][:, :], normal[b][:, :], start=True, stop=True).then_inc(summed, 1)

            groups(pe, step)

        @block.scalar
        def _(act):
            def step(g, k, h, ok):
                for b in range(U):
                    act.wait_ge(summed, g * U + b + 1)
                    act.wait_ge(stored[b], 16 * g)
                    act.copy(part[b][:, :], ps[b][:, :]).then_inc(copied, 1)

            groups(act, step)

        @block.sync
        def _(sp):
            sp.wait_ge(zeroed, 1)
            sp.dma_start(part_t[ET, :, :], none[:, :]).then_inc(zero_stored, 16)

            def step(g, k, h, ok):
                for b in range(U):
                    sp.wait_ge(copied, g * U + b + 1)
                    at = g * U + b
                    sp.dma_start(part_t[bass.ds(at, 1), :, :].squeeze(0), part[b][:, :]).then_inc(stored[b], 16)

            groups(sp, step)
            load_weights(sp, c, base_w, spline_w, range(EARLY, NPC))
            for b in range(U):
                sp.wait_ge(stored[b], 16 * G)
            sp.wait_ge(zero_stored, 16)


def carry_phase(nc, m, c, part_dram):
    with ExitStack() as ctx, nc.Block() as block:
        m = Phase(nc, ctx, "y")
        row = c.sorted[:, 0, :]
        equal = m.sb("equal", [ET, P])
        count, onward, wanted, other, last = (m.sb(s, [ET, 1]) for s in ("count", "onward", "wanted", "other", "last"))
        index = m.sb("index", [ET, 1], U32)
        spread, began = m.sb("spread", [ET, ET]), m.sb("began", [ET, ET])
        ends, got, total = (m.sb(s, [ET, D]) for s in ("ends", "got", "total"))
        ps_wanted, ps_carry = m.ps("ps_wanted", [ET, ET]), m.ps("ps_carry", [ET, D])
        v, ends_loaded, index_ready = m.sem("v"), m.sem("ends_loaded"), m.sem("index_ready")
        spread_done, carried, summed = m.sem("spread_done"), m.sem("carried"), m.sem("summed")
        gathered, stored = swdge(c, 2)

        @block.sync
        def _(sp):
            sp.dma_start(ends[:, :], part_dram.rearrange("(t p) d -> t p d", p=P)[0:ET, P - 1, :]).then_inc(ends_loaded, 16)

        @block.vector
        def _(dve):
            dve.scalar_tensor_tensor(equal[:, :], row, row[:, 0:1], c.ones[0:ET, :], ALU.is_equal, ALU.mult, accum_out=count[:, :])
            dve.tensor_tensor(onward[:, :], row[:, 0:1], c.run_on[:, :], ALU.is_equal).then_inc(v, 1)
            dve.wait_ge(v, 1)
            dve.scalar_tensor_tensor(wanted[:, :], onward[:, :], 65536.0, row[:, 0:1], ALU.mult, ALU.add)
            dve.scalar_tensor_tensor(last[:, :], c.iota_p[0:ET, :], float(P), count[:, :], ALU.mult, ALU.add).then_inc(v, 1)
            dve.wait_ge(v, 2)
            dve.tensor_scalar(other[:, :], c.iota_p[0:ET, :], float(EP + 1), None, ALU.add)
            dve.tensor_scalar(last[:, :], last[:, :], -1.0, None, ALU.add)
            dve.tensor_scalar(spread[:, :], c.ident[0:ET, 0:ET], wanted[:, :], None, ALU.mult).then_inc(v, 1)
            dve.wait_ge(v, 3)
            dve.tensor_tensor(other[:, :], other[:, :], last[:, :], ALU.subtract).then_inc(v, 1)
            dve.wait_ge(v, 4)
            dve.scalar_tensor_tensor(index[:, :], other[:, :], onward[:, :], last[:, :], ALU.mult, ALU.add).then_inc(index_ready, 1)
            dve.wait_ge(spread_done, 1)
            dve.tensor_scalar(began[:, :], ps_wanted[:, :], c.run_on[:, :], None, ALU.is_equal).then_inc(v, 1)
            dve.wait_ge(carried, 1)
            dve.wait_ge(gathered, 16)
            dve.tensor_tensor(total[:, :], got[:, :], ps_carry[:, :], ALU.add).then_inc(summed, 1)

        @block.tensor
        def _(pe):
            pe.wait_ge(v, 3)
            pe.matmul(ps_wanted[:, :], c.ones[0:ET, 0:ET], spread[:, :], start=True, stop=True).then_inc(spread_done, 1)
            pe.wait_ge(v, 5)
            pe.wait_ge(ends_loaded, 16)
            pe.matmul(ps_carry[:, :], began[:, :], ends[:, :], start=True, stop=True).then_inc(carried, 1)

        @block.gpsimd
        def _(pool):
            pool.wait_ge(index_ready, 1)
            pool.nop(nofuse=True)
            pool.indirect_dma_start(got[:, :], None, part_dram, bass.IndirectOffsetOnAxis(index[:, :], 0)).then_inc(gathered, 16)
            pool.wait_ge(summed, 1)
            pool.nop(nofuse=True)
            pool.indirect_dma_start(part_dram, bass.IndirectOffsetOnAxis(index[:, :], 0), total[:, :], None,
                                    bounds_check=EP + P - 1, oob_is_err=False).then_inc(stored, 16)
            pool.wait_ge(stored, 16)


NPC = 1 + 2 * CH
EARLY = 4


def weight_pieces(base_w, spline_w):
    base_v = base_w.rearrange("(c p) o -> p c o", p=P)
    spline_v = spline_w.rearrange("(c p) k o -> c p k o", p=P)
    return [(base_v, 0, None)] + [(spline_v[ch, :, 4 * g:4 * g + 4, :], ch, g) for ch in range(CH) for g in range(2)]


def load_weights(sp, c, base_w, spline_w, numbers):
    pieces = weight_pieces(base_w, spline_w)
    for n in numbers:
        sp.dma_start(c.weights[n][:, :, :], pieces[n][0]).then_inc(c.weights_loaded[n], 16)


def weight_phase(nc, m, c, base_w, spline_w):
    with ExitStack() as ctx, nc.Block() as block:
        m = Phase(nc, ctx, "w")
        tops = m.sb("tops", [P, 18])
        top = m.sb("top", [P, 1])
        topT = m.sb("topT", [1, 1])
        bits = m.sb("bits", [P, 1])
        third = m.sb("third", [P, 1])
        ps = m.ps("ps", [P, P])
        v, t, scaled, high = m.sem("v"), m.sem("t"), m.sem("scaled"), m.sem("high")
        w, pieces, measured = c.weights, weight_pieces(base_w, spline_w), m.sem("measured")

        @block.vector
        def _(dve):
            for n in range(NPC):
                dve.wait_ge(c.weights_loaded[n], 16)
                dve.tensor_reduce(tops[:, n:n + 1], w[n][:, :, :], AX.XY, ALU.max, apply_absolute_value=True).then_inc(measured, 1)
            dve.wait_ge(measured, NPC)
            dve.tensor_reduce(top[:, :], tops[:, 0:NPC], AX.X, ALU.max).then_inc(v, 1)
            dve.wait_ge(t, 1)
            dve.tensor_reduce(topT[:, :], ps[0:1, 0:P], AX.X, ALU.max).then_inc(v, 1)
            dve.wait_ge(t, 2)
            dve.tensor_scalar(bits[:, :], ps[:, 0:1], 1e-30, None, ALU.max).then_inc(v, 1)
            dve.wait_ge(v, 3)
            dve.tensor_scalar(bits[:, :].bitcast(I32), bits[:, :].bitcast(I32), 0x7F800000, None, ALU.bitwise_and).then_inc(v, 1)
            dve.wait_ge(v, 4)
            dve.tensor_scalar(c.unscale[:, :], bits[:, :], 2.0 ** -23, None, ALU.mult)
            dve.reciprocal(c.scale[:, :], bits[:, :]).then_inc(v, 1)
            dve.wait_ge(v, 5)
            dve.tensor_scalar(c.scale[:, :], c.scale[:, :], 2.0 ** 13, None, ALU.mult).then_inc(v, 1)
            dve.wait_ge(v, 6)
            dve.tensor_scalar(third[:, :], c.scale[:, :], 1.0 / 3.0, None, ALU.mult).then_inc(scaled, 1)
            dve.wait_ge(scaled, 1)
            for n in range(NPC):
                _, ch, g = pieces[n]
                fac = c.scale if g is None else third
                hi, lo = target(c, ch, g)
                dve.wait_ge(high, n + 1)
                dve.scalar_tensor_tensor(lo, w[n][:, :, :], fac[:, :], hi, ALU.mult, ALU.subtract)

        @block.scalar
        def _(act):
            act.wait_ge(scaled, 1)
            for n in range(NPC):
                _, ch, g = pieces[n]
                fac = c.scale if g is None else third
                hi, lo = target(c, ch, g)
                act.wait_ge(c.weights_loaded[n], 16)
                act.activation(hi, w[n][:, :, :], ACT.Copy, scale=fac[:, :]).then_inc(high, 1)

        @block.tensor
        def _(pe):
            pe.wait_ge(v, 1)
            pe.transpose(ps[0:1, 0:P], top[:, :], c.ident[:, :]).then_inc(t, 1)
            pe.wait_ge(v, 2)
            pe.matmul(ps[:, 0:1], c.ones[0:1, :], topT[:, :], start=True, stop=True).then_inc(t, 1)


def target(c, ch, g):
    if g is None:
        return c.w_hi[:, :, NB, :], c.w_lo[:, :, NB, :]
    return c.w_hi[:, ch, 4 * g:4 * g + 4, :], c.w_lo[:, ch, 4 * g:4 * g + 4, :]


def layer_phase(nc, m, c, x, part_dram, both_dram, out):
    with ExitStack() as ctx, nc.Block() as block:
        m = Phase(nc, ctx, "l")
        pair = lambda name, shape, dt=F32: [m.sb(f"{name}{b}", shape, dt) for b in range(2)]
        index = pair("index", [P, 1], U32)
        f_hi, f_lo = pair("f_hi", [P, NF, D], F16), pair("f_lo", [P, NF, D], F16)
        G = 4
        halves = lambda w: [w[:, 0:2, :], w[:, 2:4, :]]
        quarters = lambda w: [w[:, n, :] for n in range(4)]
        y, a, b1, a2, b2, nn, both = (halves(w) for w in c.weights[0:7])
        agg, xt = quarters(c.weights[7])[0:2], quarters(c.weights[7])[2:4]
        out0, (th, zz) = quarters(c.weights[8])[0:2], quarters(c.weights[8])[2:4]
        h2T = m.sb("h2T", [P, CH, P])
        stats, mv, ve, rstd = pair("stats", [P, 6]), pair("mv", [P, 2]), pair("ve", [P, 1]), pair("rstd", [P, 1])
        mhalf, nothing = m.sb("mhalf", [P, 1]), m.sb("nothing", [P, 2 * D])
        logit, ntop, ex, tot, prob = (pair("logit", [P, NEXP]), pair("ntop", [P, 1]), pair("ex", [P, NEXP]),
                                      pair("tot", [P, 1]), pair("prob", [P, 1]))
        ps_agg = [m.ps(f"ps_agg{b}", [P, CH, P]) for b in range(2)]
        ps_out = [m.ps(f"ps_out{b}", [P, D]) for b in range(2)]
        ps_h2 = m.ps("ps_h2", [P, CH, P])
        ps_logit = [m.ps(f"ps_logit{b}", [P, NEXP]) for b in range(2)]
        gathered = swdge(c, 2)
        x_loaded, both_stored, out_stored = (m.sem(s, 2) for s in ("x_loaded", "both_stored", "out_stored"))
        half, rest_stored = m.sem("half"), m.sem("rest_stored")
        y_ready, ab_ready, sq_ready, b3_ready, n_ready, a3_ready, hi_ready, lo_ready = (
            m.sem(s) for s in ("y_ready", "ab_ready", "sq_ready", "b3_ready", "n_ready", "a3_ready", "hi_ready", "lo_ready"))
        f_used = m.sem("f_used")
        (index_ready, aggT_ready, th_ready, z_ready, zhi_ready, zlo_ready, x1_ready, bn_done, mv_ready, ve_ready,
         rstd_ready, h2_ready, h2T_ready, h2T_copied, logit_done, logit_ready, ntop_ready, ex_ready, prob_ready, out0_ready) = (
            m.sem(s) for s in ("index_ready", "aggT_ready", "th_ready", "z_ready", "zhi_ready", "zlo_ready", "x1_ready",
                               "bn_done", "mv_ready", "ve_ready", "rstd_ready", "h2_ready", "h2T_ready", "h2T_copied",
                               "logit_done", "logit_ready", "ntop_ready", "ex_ready", "prob_ready", "out0_ready"))
        x_t = x.rearrange("(t p) d -> t p d", p=P)
        out_t = out.rearrange("(t p) d -> t p d", p=P)
        both_t = both_dram.rearrange("(t p) d -> t p d", p=P)
        row_of = lambda v, i: v[bass.ds(i, 1), :, :].squeeze(0)

        def steps(eng, step):
            def peeled(i):
                step(i, i // 2, i % 2, lambda o: 0 <= i + o < LT)

            for i in range(-2, 6):
                peeled(i)
            with eng.Fori(3, (LT - 3) // 2) as k:
                for b in range(2):
                    step(k * 2 + b, k, b, lambda o: True)
            for i in range((LT - 3) // 2 * 2, LT + 3):
                peeled(i)

        def slot(k, b, o):
            return (b + o) % 2, k + (b + o) // 2

        @block.gpsimd
        def _(pool):
            pool.memset(mhalf[:, :], -0.5).then_inc(half, 1)
            pool.memset(c.logits[:, LT:NT, :], 0.0)
            pool.memset(c.prob[:, LT:NT], 0.0)
            pool.memset(nothing[:, :], 0.0).then_inc(half, 1)
            pool.wait_ge(half, 1)

            def gather(t, b):
                pool.wait_ge(aggT_ready, past(t - 1))
                pool.tensor_copy(index[b][:, :], c.last_edge[:, bass.ds(t, 1)]).then_inc(index_ready, 1)
                pool.wait_ge(index_ready, t + 1)
                pool.nop(nofuse=True)
                pool.indirect_dma_start(agg[b][:, :], None, part_dram,
                                        bass.IndirectOffsetOnAxis(index[b][:, :], 0)).then_inc(gathered[b], 16)

            def cubes(n, q):
                pool.wait_ge(sq_ready, n + 1)
                pool.tensor_tensor(b2[q][:, :, :], b1[q][:, :, :], b2[q][:, :, :], ALU.mult).then_inc(b3_ready, 1)

            def step(i, k, b, ok):
                for g in range(G):
                    if ok(1 + (g + 1) // G):
                        cubes(4 * i + 4 + g + 1, (g + 1) % 2)
                    if g == 0 and ok(3):
                        gather(i + 3, (b + 3) % 2)
                    if g == 2 and ok(-1):
                        q = (b - 1) % 2
                        pool.wait_ge(mv_ready, i)
                        pool.wait_ge(h2_ready, past(i - 2))
                        pool.nop(nofuse=True)
                        pool.tensor_scalar(ve[q][:, :], mv[q][:, 1:2], EPS, None, ALU.add).then_inc(ve_ready, 1)
                        pool.wait_ge(ve_ready, i)
                        pool.tensor_tensor(rstd[q][:, :], ve[q][:, :], mhalf[:, :], ALU.pow).then_inc(rstd_ready, 1)

            gather(0, 0)
            steps(pool, step)

        @block.sync
        def _(sp):
            def step(i, k, b, ok):
                if ok(0):
                    sp.wait_ge(x1_ready, past(i - 1))
                    sp.dma_start(xt[b][:, :], row_of(x_t, i)).then_inc(x_loaded[b], 16)
                if ok(-3):
                    q = (b - 3) % 2
                    sp.wait_ge(out0_ready, i - 2)
                    sp.dma_start(row_of(out_t, i - 3), out0[q][:, :]).then_inc(out_stored[q], 16)
                if ok(-1):
                    q = (b - 1) % 2
                    sp.wait_ge(h2_ready, i)
                    sp.dma_start(row_of(both_t, i - 1), both[q][:, :, :].rearrange("p a d -> p (a d)")).then_inc(both_stored[q], 16)

            sp.wait_ge(half, 2)
            for t in range(LT, NT):
                sp.dma_start(both_t[t, :, :], nothing[:, :]).then_inc(rest_stored, 16)
            steps(sp, step)
            sp.wait_ge(rest_stored, 16 * (NT - LT))
            for b in range(2):
                sp.wait_ge(both_stored[b], 16 * ((LT + 1 - b) // 2))
                sp.wait_ge(out_stored[b], 16 * ((LT + 1 - b) // 2))

        @block.tensor
        def _(pe):
            def agg_t(t, b, turn):
                pe.wait_ge(gathered[b], 16 * (turn + 1))
                pe.wait_ge(y_ready, past(4 * t - 4))
                pe.wait_ge(z_ready, past(t - 1))
                for ch in range(CH):
                    g = pe.transpose(ps_agg[b][:, ch, :], agg[b][:, ch * P:(ch + 1) * P], c.ident[:, :])
                g.then_inc(aggT_ready, 1)

            def products(b, fs, first, last):
                for f in fs:
                    for ch in range(CH):
                        cols = slice(ch * P, (ch + 1) * P)
                        for part, (lhs, rhs) in enumerate(((f_hi, c.w_hi), (f_hi, c.w_lo), (f_lo, c.w_hi))):
                            mm = pe.matmul(ps_out[b][:, :], lhs[b][:, f, cols], rhs[:, ch, f, :],
                                           start=first and f == fs[0] and ch == 0 and part == 0,
                                           stop=last and f == fs[-1] and ch == CH - 1 and part == 2)
                mm.then_inc(f_used, 1)

            def step(i, k, b, ok):
                if ok(2):
                    agg_t(i + 2, *slot(k, b, 2))
                for g in range(G):
                    if ok(0):
                        if g == 0:
                            pe.wait_ge(x1_ready, past(i - 1))
                        pe.wait_ge(lo_ready, 4 * i + g + 1)
                        products(b, (2 * g, 2 * g + 1), g == 0, False)
                    if g == 0 and ok(-2):
                        pe.wait_ge(h2_ready, i - 1)
                        pe.wait_ge(h2T_copied, past(i - 2))
                        for ch in range(CH):
                            t = pe.transpose(ps_h2[:, ch, :], both[b][:, 1, ch * P:(ch + 1) * P], c.ident[:, :])
                        t.then_inc(h2T_ready, 1)
                    if g == 2 and ok(-2):
                        pe.wait_ge(h2T_copied, i - 1)
                        pe.wait_ge(logit_ready, past(i - 3))
                        for ch in range(CH):
                            t = pe.matmul(ps_logit[b][:, :], h2T[:, ch, :], c.gate_w[:, ch, :], start=ch == 0, stop=ch == CH - 1)
                        t.then_inc(logit_done, 1)
                if ok(0):
                    pe.wait_ge(zlo_ready, i + 1)
                    products(b, (NB,), False, True)

            pe.wait_ge(c.gate_loaded, 32)
            steps(pe, step)

        @block.scalar
        def _(act):
            def squares(n, q):
                act.wait_ge(ab_ready, n + 1)
                act.wait_ge(n_ready, past(n - 1))
                act.activation(a2[q][:, :, :], a[q][:, :, :], ACT.Square)
                act.activation(b2[q][:, :, :], b1[q][:, :, :], ACT.Square, scale=2.0).then_inc(sq_ready, 1)

            def high(t, b, g):
                act.wait_ge(n_ready, 4 * t + g + 1)
                act.wait_ge(f_used, past(5 * t - 10 + g + 1))
                act.copy(f_hi[b][:, 2 * g:2 * g + 2, :], nn[g % 2][:, :, :]).then_inc(hi_ready, 1)

            def bases(t, b, g):
                n = 4 * t + g
                act.wait_ge(aggT_ready, t + 1)
                act.wait_ge(ab_ready, past(n - 1))
                for j in range(2):
                    done = act.activation(y[g % 2][:, j, :], ps_agg[b][:, :, :].rearrange("p c n -> p (c n)"), ACT.Abs,
                                          bias=c.mid[:, 2 * g + j:2 * g + j + 1], scale=20.0)
                done.then_inc(y_ready, 1)

            def step(i, k, b, ok):
                q = (b + 1) % 2
                for g in range(G):
                    if ok(1 + (g + 1) // G):
                        squares(4 * i + 4 + g + 1, (g + 1) % 2)
                    if ok(1):
                        high(i + 1, q, g)
                    if ok(1 + (g + 3) // G):
                        bases(i + 1 + (g + 3) // G, (b + 1 + (g + 3) // G) % 2, (g + 3) % G)
                    if g == 0 and ok(1):
                        act.wait_ge(z_ready, i + 1)
                        act.activation(th[:, :], ps_agg[q][:, :, :].rearrange("p c n -> p (c n)"), ACT.Tanh, scale=0.5).then_inc(th_ready, 1)
                    if g == 0 and ok(-3):
                        act.wait_ge(ntop_ready, i - 2)
                        act.wait_ge(prob_ready, past(i - 4))
                        act.activation(ex[q][:, :], logit[q][:, :], ACT.Exp, bias=ntop[q][:, :], accum_out=tot[q][:, :]).then_inc(ex_ready, 1)
                    if g == 1 and ok(-2):
                        act.wait_ge(h2T_ready, i - 1)
                        act.wait_ge(logit_done, past(i - 2))
                        act.copy(h2T[:, :, :], ps_h2[:, :, :]).then_inc(h2T_copied, 1)
                    if g == 2 and ok(1):
                        act.wait_ge(z_ready, i + 2)
                        act.wait_ge(f_used, past(5 * i))
                        act.activation(f_hi[q][:, NB, :], zz[:, :], ACT.Copy, scale=512.0).then_inc(zhi_ready, 1)

            steps(act, step)

        @block.vector
        def _(dve):
            def sides(n, q):
                dve.wait_ge(y_ready, n + 1)
                dve.wait_ge(b3_ready, past(n - 1))
                dve.wait_ge(a3_ready, past(n - 1))
                dve.tensor_scalar(a[q][:, :, :], y[q][:, :, :], -16.0, 0.0, ALU.add, ALU.min)
                dve.tensor_scalar(b1[q][:, :, :], y[q][:, :, :], -8.0, 0.0, ALU.add, ALU.min).then_inc(ab_ready, 1)

            def cubes(n, q):
                dve.wait_ge(sq_ready, n + 1)
                dve.tensor_tensor(a2[q][:, :, :], a[q][:, :, :], a2[q][:, :, :], ALU.mult).then_inc(a3_ready, 1)

            def basis(n, q):
                dve.wait_ge(b3_ready, n + 1)
                dve.wait_ge(a3_ready, n + 1)
                dve.wait_ge(lo_ready, past(n - 1))
                dve.tensor_tensor(nn[q][:, :, :], b2[q][:, :, :], a2[q][:, :, :], ALU.subtract).then_inc(n_ready, 1)

            def low(t, b, g):
                dve.wait_ge(hi_ready, 4 * t + g + 1)
                dve.tensor_tensor(f_lo[b][:, 2 * g:2 * g + 2, :], nn[g % 2][:, :, :], f_hi[b][:, 2 * g:2 * g + 2, :],
                                  ALU.subtract).then_inc(lo_ready, 1)

            def step(i, k, b, ok):
                q, turn = slot(k, b, -1)
                for g in range(G):
                    if ok(1 + (g + 2) // G):
                        sides(4 * i + 4 + g + 2, g % 2)
                    if g == 0 and ok(-3):
                        dve.wait_ge(logit_done, i - 2)
                        dve.wait_ge(ex_ready, past(i - 4))
                        dve.tensor_tensor(logit[q][:, :], ps_logit[q][:, :], c.gate_b[:, :], ALU.add).then_inc(logit_ready, 1)
                        dve.wait_ge(logit_ready, i - 2)
                        dve.tensor_copy(c.logits[:, bass.ds(i - 3, 1), :].squeeze(1), logit[q][:, :])
                        dve.tensor_reduce(ntop[q][:, :], logit[q][:, :], AX.X, ALU.max, negate=True).then_inc(ntop_ready, 1)
                    if g == 1 and ok(-3):
                        dve.wait_ge(ex_ready, i - 2)
                        dve.reciprocal(prob[q][:, :], tot[q][:, :]).then_inc(prob_ready, 1)
                    if g == 1 and ok(1):
                        dve.wait_ge(th_ready, i + 2)
                        dve.wait_ge(zlo_ready, i + 1)
                        dve.scalar_tensor_tensor(zz[:, :], th[:, :], 1.0, ps_agg[q][:, :, :].rearrange("p c n -> p (c n)"),
                                                 ALU.add, ALU.mult).then_inc(z_ready, 1)
                    if g == 2 and ok(-1):
                        dve.wait_ge(x1_ready, i)
                        dve.bn_stats(stats[q][:, :], both[q][:, 0, :]).then_inc(bn_done, 1)
                    if ok(1 + (g + 1) // G):
                        cubes(4 * i + 4 + g + 1, (g + 1) % 2)
                    if g == 1 and ok(-3):
                        dve.wait_ge(prob_ready, i - 2)
                        dve.wait_ge(out_stored[q], 16 * past(turn - 1))
                        dve.tensor_copy(c.prob[:, bass.ds(i - 3, 1)], prob[q][:, :])
                        dve.scalar_tensor_tensor(out0[q][:, :], both[q][:, 1, :], prob[q][:, :], both[q][:, 0, :],
                                                 ALU.mult, ALU.add).then_inc(out0_ready, 1)
                    if g == 2 and ok(-1):
                        dve.wait_ge(bn_done, i)
                        dve.nop(nofuse=True)
                        dve.bn_aggr(mv[q][:, :], stats[q][:, :]).then_inc(mv_ready, 1)
                    if g == 3 and ok(1):
                        dve.wait_ge(zhi_ready, i + 2)
                        dve.scalar_tensor_tensor(f_lo[q][:, NB, :], zz[:, :], 512.0, f_hi[q][:, NB, :], ALU.mult, ALU.subtract).then_inc(zlo_ready, 1)
                    if ok(1):
                        low(i + 1, q, g)
                    if g == 1 and ok(-1):
                        dve.wait_ge(f_used, 5 * i)
                        dve.wait_ge(x_loaded[q], 16 * (turn + 1))
                        dve.wait_ge(both_stored[q], 16 * turn)
                        dve.wait_ge(out0_ready, past(i - 2))
                        dve.scalar_tensor_tensor(both[q][:, 0, :], ps_out[q][:, :], c.unscale[:, :], xt[q][:, :],
                                                 ALU.mult, ALU.add).then_inc(x1_ready, 1)
                    if g == 3 and ok(-1):
                        dve.wait_ge(rstd_ready, i)
                        dve.tensor_scalar(both[q][:, 1, :], both[q][:, 0, :], mv[q][:, 0:1], rstd[q][:, :],
                                          ALU.subtract, ALU.mult).then_inc(h2_ready, 1)
                    if ok(1 + (g + 1) // G):
                        basis(4 * i + 4 + g + 1, (g + 1) % 2)

            dve.wait_ge(c.gate_loaded, 32)
            steps(dve, step)


def route_phase(nc, m, c, expert_w, expert_b):
    with ExitStack() as ctx:
        m = Phase(nc, ctx, "r")
        te = lambda ap: wide(ap.unsqueeze(2), [P, NT, NEXP])
        best = m.sb("best", [P, NT])
        countdown = m.sb("countdown", [P, NEXP])
        points = m.sb("points", [P, NT, NEXP])
        first = m.sb("first", [P, NT])
        route = m.sb("route", [P, NEXP, NT], BF16)
        tri, ones = m.sb("tri", [P, P], BF16), m.sb("ones", [P, P], BF16)
        keep_on = m.sb("keep_on", [P, NEXP, NT])
        totals = m.sb("totals", [P, NEXP, NT])
        upto = m.sb("upto", [P, NEXP, NT])
        before = m.sb("before", [P, NEXP, NT])
        mine = m.sb("mine", [P, NEXP, NT])
        pos, over, expert, place = (m.sb(s, [P, NT]) for s in ("pos", "over", "expert", "place"))
        placei, tilei = m.sb("placei", [P, NT], I32), m.sb("tilei", [P, NT], I32)
        place_tile, place_lane = m.sb("place_tile", [P, NT]), m.sb("place_lane", [P, NT])
        token = m.sb("token", [P, NT])
        B = 4
        lane_hot = [m.sb(f"lane_hot{b}", [P, P]) for b in range(B)]
        values = [m.sb(f"values{b}", [P, 2, FT]) for b in range(B)]
        tile_hot = [m.sb(f"tile_hot{b}", [P, FT]) for b in range(B)]
        tile_ready, values_ready = m.sem("tile_ready"), m.sem("values_ready")
        slots = m.sb("slots", [P, 2, FT])
        empty = m.sb("empty", [P, FT])
        PIECE = 6
        pieces = [(e, min(e + PIECE, NEXP)) for e in range(0, NEXP, PIECE)]
        ps_in = [m.ps(f"ps_in{n}", [P, PIECE, NT]) for n in range(len(pieces))]
        ps_all = [m.ps(f"ps_all{n}", [P, PIECE, NT]) for n in range(len(pieces))]
        ps_slots = m.ps("ps_slots", [P, 2, FT])
        v, made, counted, hot_ready, moved, all_moved = (m.sem("v"), m.sem("made"), m.sem("counted"),
                                                         m.sem("hot_ready"), m.sem("moved"), m.sem("all_moved"))
        V = 8

        with nc.Block() as block:

            @block.sync
            def _(sp):
                for h in range(2):
                    sp.dma_start(c.expert_w[h][:, :, :], expert_w.rearrange("e (c p) f -> p e c f", p=P)[:, h, :, :]).then_inc(c.experts_loaded[h], 16)
                sp.dma_start(c.expert_b[:, :, :].rearrange("p e d -> p (e d)"),
                             expert_b.rearrange("(o e) d -> o (e d)", o=1).broadcast_to([P, NEXP * D])).then_inc(c.experts_loaded[2], 16)

            @block.gpsimd
            def _(pool):
                pool.iota(countdown[:, :], [[-1, NEXP]], base=NEXP, channel_multiplier=0, allow_small_or_imprecise_dtypes=True)
                pool.iota(token[:, :], [[P, NT]], base=1, channel_multiplier=1, allow_small_or_imprecise_dtypes=True).then_inc(made, 1)

            @block.vector
            def _(dve):
                n = 0

                def step(ins):
                    nonlocal n
                    ins.then_inc(v, 1)
                    n += 1
                    dve.wait_ge(v, n)

                dve.memset(keep_on[:, :, :], 1.0)
                dve.tensor_copy(tri[:, :], c.tri[:, :])
                dve.tensor_copy(ones[:, :], c.ones[:, :])
                step(dve.tensor_reduce(best[:, :], c.logits[:, :, :], AX.X, ALU.max))
                dve.memset(keep_on[:, :, 0], 0.0)
                step(dve.tensor_tensor(points[:, :, :], c.logits[:, :, :], te(best[:, :]), ALU.is_equal))
                dve.wait_ge(made, 1)
                step(dve.tensor_tensor(points[:, :, :], points[:, :, :], wide(countdown[:, :].unsqueeze(1), [P, NT, NEXP]), ALU.mult))
                step(dve.tensor_reduce(first[:, :], points[:, :, :], AX.X, ALU.max))
                step(dve.tensor_tensor(route[:, :, :].rearrange("p e t -> p t e"), wide(countdown[:, :].unsqueeze(1), [P, NT, NEXP]),
                                       te(first[:, :]), ALU.is_equal))
                dve.wait_ge(counted, 1)
                for q, (e0, e1) in enumerate(pieces):
                    done = dve.tensor_copy(totals[:, e0:e1, :], ps_all[q][:, 0:e1 - e0, :])
                step(done)
                flat = lambda a: a[:, :, :].rearrange("p e t -> p (e t)")
                step(dve.tensor_tensor_scan(flat(upto), flat(keep_on), flat(totals), 0.0, ALU.mult, ALU.add))
                step(dve.tensor_tensor(before[:, :, :], upto[:, :, :], totals[:, :, :], ALU.subtract))
                for q, (e0, e1) in enumerate(pieces):
                    done = dve.tensor_tensor(mine[:, e0:e1, :], ps_in[q][:, 0:e1 - e0, :], before[:, e0:e1, :], ALU.add)
                step(done)
                step(dve.tensor_tensor(mine[:, :, :], mine[:, :, :], route[:, :, :], ALU.mult))
                step(dve.tensor_reduce(pos[:, :], mine[:, :, :].rearrange("p e t -> p t e"), AX.X, ALU.add))
                step(dve.tensor_scalar(over[:, :], pos[:, :], float(CAP), 32768.0, ALU.is_ge, ALU.mult))
                step(dve.tensor_scalar(expert[:, :], first[:, :], -float(ST * P), float(NEXP * ST * P), ALU.mult, ALU.add))
                step(dve.tensor_tensor(place[:, :], pos[:, :], over[:, :], ALU.add))
                step(dve.tensor_tensor(place[:, :], place[:, :], expert[:, :], ALU.add))
                step(dve.tensor_copy(placei[:, :], place[:, :]))
                step(dve.tensor_scalar(tilei[:, :], placei[:, :], 7, None, ALU.logical_shift_right))
                step(dve.tensor_copy(place_tile[:, :], tilei[:, :]))
                step(dve.scalar_tensor_tensor(place_lane[:, :], place_tile[:, :], -float(P), place[:, :], ALU.mult, ALU.add))
                def turn(k):
                    for n in range(V):
                        b, at = n % B, bass.ds(k * V + n, 1)
                        dve.wait_ge(moved, past(k * V + n - B + 1))
                        dve.tensor_scalar(tile_hot[b][:, :], c.iota_f[:, 0:FT], place_tile[:, at], None, ALU.is_equal).then_inc(tile_ready, 1)
                        dve.tensor_scalar(lane_hot[b][:, :], c.iota_f[:, :], place_lane[:, at], None, ALU.is_equal).then_inc(hot_ready, 1)

                turn(0)
                with dve.Fori(1, NT // V) as k:
                    turn(k)
                dve.wait_ge(all_moved, 1)
                step(dve.tensor_copy(slots[:, :, :], ps_slots[:, :, :]))
                dve.tensor_copy(c.slot_prob[:, :], slots[:, 1, :])
                dve.tensor_scalar(c.slot_read[:, :], slots[:, 0, :], -1.0, 0.0, ALU.add, ALU.max)
                step(dve.tensor_scalar(empty[:, :], slots[:, 0, :], 0.0, float(NP + 1), ALU.is_equal, ALU.mult))
                step(dve.scalar_tensor_tensor(empty[:, :], slots[:, 0, :], -1.0, empty[:, :], ALU.add, ALU.add))
                dve.tensor_copy(c.slot_write[:, :], empty[:, :])

            @block.scalar
            def _(act):
                def turn(k):
                    for n in range(V):
                        b, at = n % B, bass.ds(k * V + n, 1)
                        act.wait_ge(tile_ready, k * V + n + 1)
                        act.activation(values[b][:, 0, :], tile_hot[b][:, :], ACT.Copy, scale=token[:, at])
                        act.activation(values[b][:, 1, :], tile_hot[b][:, :], ACT.Copy, scale=c.prob[:, at]).then_inc(values_ready, 1)

                turn(0)
                with act.Fori(1, NT // V) as k:
                    turn(k)

            @block.tensor
            def _(pe):
                pe.wait_ge(v, 5)
                for q, (e0, e1) in enumerate(pieces):
                    pe.matmul(ps_in[q][:, 0:e1 - e0, :], tri[:, :], route[:, e0:e1, :], start=True, stop=True)
                    g = pe.matmul(ps_all[q][:, 0:e1 - e0, :], ones[:, :], route[:, e0:e1, :], start=True, stop=True)
                g.then_inc(counted, 1)
                pe.matmul(ps_slots[:, :, :], c.zrow[:, 0:P], c.zrow[:, 0:2 * FT], start=True, stop=False)

                def turn(k):
                    for n in range(V):
                        pe.wait_ge(hot_ready, k * V + n + 1)
                        pe.wait_ge(values_ready, k * V + n + 1)
                        pe.matmul(ps_slots[:, :, :], lane_hot[n % B][:, :], values[n % B][:, :, :], start=False, stop=False).then_inc(moved, 1)

                turn(0)
                with pe.Fori(1, NT // V) as k:
                    turn(k)
                pe.matmul(ps_slots[:, :, :], c.zrow[:, 0:P], c.zrow[:, 0:2 * FT], start=False, stop=True).then_inc(all_moved, 1)


def expert_phase(nc, m, c, expert_w, both_dram, out):
    U = ST
    with ExitStack() as ctx, nc.Block() as block:
        m = Phase(nc, ctx, "x")
        pair = lambda name, shape, dt=F32: [m.sb(f"{name}{b}", shape, dt) for b in range(2)]
        w, bias = c.expert_w, c.expert_b
        w_hi, w_lo = pair("w_hi", [P, CH, D], F16), pair("w_lo", [P, CH, D], F16)
        read = [m.sb(f"read{b}", [P, 1], U32) for b in range(U)]
        write = [m.sb(f"write{b}", [P, 1], U32) for b in range(U)]
        both = [m.sb(f"both{b}", [P, 2 * D]) for b in range(U)]
        hT_hi = [m.sb(f"hT_hi{b}", [P, D], F16) for b in range(3)]
        hT_lo = [m.sb(f"hT_lo{b}", [P, D], F16) for b in range(3)]
        y = pair("y", [P, D])
        o = [m.sb(f"o{b}", [P, D]) for b in range(U)]
        tops, topT, bits, scale, unscale = m.sb("tops", [P, 1]), m.sb("topT", [1, 1]), m.sb("bits", [P, 1]), m.sb("scale", [P, 1]), pair("unscale", [P, 1])
        ps_t = [m.ps(f"ps_t{b}", [P, D]) for b in range(3)]
        ps_y = [m.ps(f"ps_y{b}", [P, D]) for b in range(3)]
        ps_top = m.ps("ps_top", [P, P])
        w_loaded, bias_loaded = c.experts_loaded[0:2], c.experts_loaded[2]
        gathered, stored = swdge(c, U), swdge(c, U)
        top_ready, top_row, topT_ready, top_all, max_ready, bits_ready, recip_ready, scale_ready, w_high, w_ready = (
            m.sem(s) for s in ("top_ready", "top_row", "topT_ready", "top_all", "max_ready", "bits_ready", "recip_ready",
                               "scale_ready", "w_high", "w_ready"))
        read_ready, write_ready, turned, t_high, t_low, multiplied, y_ready, o_ready = (
            m.sem(s) for s in ("read_ready", "write_ready", "turned", "t_high", "t_low", "multiplied", "y_ready", "o_ready"))

        def turns(eng, slot):
            def pair_of_experts(k, ok):
                for j in range(2 * U):
                    slot(k * (2 * U) + j, j, k, k * 2 + j // U, j % U, ok)

            for j in range(-4, 0):
                slot(j, j, 0, -1, j % U, lambda n: 0 <= n < FT)
            pair_of_experts(0, lambda n: 0 <= n < FT)
            with eng.Fori(1, NEXP // 2 - 1) as k:
                pair_of_experts(k, lambda n: True)
            pair_of_experts(NEXP // 2 - 1, lambda n: 0 <= n < FT)
            for j in range(2):
                slot(FT + j, j, NEXP // 2, NEXP, j, lambda n: 0 <= n < FT)

        @block.sync
        def _(sp):
            w_v = expert_w.rearrange("e (c p) f -> p e c f", p=P)
            with sp.Fori(0, NEXP // 2 - 1) as k:
                for h in range(2):
                    sp.wait_ge(w_ready, k * 2 + h + 1)
                    sp.dma_start(w[h][:, :, :], w_v[:, bass.ds(k * 2 + h + 2, 1), :, :].squeeze(1)).then_inc(w_loaded[h], 16)

        @block.gpsimd
        def _(pool):
            def slot(n, j, k, e, q, ok):
                if ok(n + 4):
                    r = (q + 4) % U
                    pool.wait_ge(o_ready, past(n - 1))
                    pool.wait_ge(read_ready, n + 5)
                    pool.nop(nofuse=True)
                    pool.indirect_dma_start(both[r][:, :], None, both_dram,
                                            bass.IndirectOffsetOnAxis(read[r][:, :], 0)).then_inc(gathered[r], 16)
                if ok(n + 5):
                    r, t = (q + 5) % U, e + (q + 5) // U
                    pool.wait_ge(gathered[r], 16 * t)
                    pool.tensor_copy(read[r][:, :], c.slot_read[:, bass.ds(n + 5, 1)]).then_inc(read_ready, 1)
                if ok(n - 2):
                    r = (q - 2) % U
                    pool.wait_ge(o_ready, n - 1)
                    pool.wait_ge(write_ready, n - 1)
                    pool.nop(nofuse=True)
                    pool.indirect_dma_start(out, bass.IndirectOffsetOnAxis(write[r][:, :], 0), o[r][:, :], None,
                                            bounds_check=NP - 1, oob_is_err=False).then_inc(stored[r], 16)
                if ok(n - 1):
                    r, t = (q - 1) % U, e + (q - 1) // U
                    pool.wait_ge(stored[r], 16 * t)
                    pool.tensor_copy(write[r][:, :], c.slot_write[:, bass.ds(n - 1, 1)]).then_inc(write_ready, 1)

            pool.tensor_copy(read[0][:, :], c.slot_read[:, 0:1]).then_inc(read_ready, 1)
            turns(pool, slot)
            for r in range(U):
                pool.wait_ge(stored[r], 16 * NEXP)

        @block.tensor
        def _(pe):
            def top_to_row(e):
                pe.wait_ge(top_ready, e + 1)
                pe.transpose(ps_top[0:1, 0:P], tops[:, :], c.ident[:, :]).then_inc(top_row, 1)

            def top_to_all(e):
                pe.wait_ge(topT_ready, e + 1)
                pe.matmul(ps_top[:, 0:1], c.ones[0:1, :], topT[:, :], start=True, stop=True).then_inc(top_all, 1)

            def slot(n, j, k, e, q, ok):
                if ok(n + 2):
                    r, t, b = (q + 2) % U, e + (q + 2) // U, (j + 2) % 3
                    pe.wait_ge(gathered[r], 16 * (t + 1))
                    pe.wait_ge(t_low, past(n))
                    for ch in range(CH):
                        g = pe.transpose(ps_t[b][:, ch * P:(ch + 1) * P], both[r][:, D + ch * P:D + (ch + 1) * P], c.ident[:, :])
                    g.then_inc(turned, 1)
                if ok(n):
                    h = (j // U) % 2
                    if q == 0:
                        pe.wait_ge(w_ready, e + 1)
                    pe.wait_ge(t_low, n + 1)
                    pe.wait_ge(y_ready, past(n - 2))
                    for ch in range(CH):
                        for part, (lhs, rhs) in enumerate(((hT_hi, w_hi), (hT_hi, w_lo), (hT_lo, w_hi))):
                            g = pe.matmul(ps_y[j % 3][:, :], lhs[j % 3][:, ch * P:(ch + 1) * P], rhs[h][:, ch, :],
                                          start=ch == 0 and part == 0, stop=ch == CH - 1 and part == 2)
                    g.then_inc(multiplied, 1)
                    if q == 1 and ok(n + U):
                        top_to_row(e + 1)
                    if q == 2 and ok(n + U):
                        top_to_all(e + 1)

            top_to_row(0)
            top_to_all(0)
            turns(pe, slot)

        @block.scalar
        def _(act):
            def weights_high(e, h, half):
                act.wait_ge(scale_ready, e + 1)
                act.activation(w_hi[h][:, 2 * half:2 * half + 2, :], w[h][:, 2 * half:2 * half + 2, :], ACT.Copy,
                               scale=scale[:, :]).then_inc(w_high, 1)

            def slot(n, j, k, e, q, ok):
                if ok(n + 2):
                    d = (j + 2) % 3
                    act.wait_ge(turned, n + 3)
                    act.wait_ge(multiplied, past(n))
                    act.activation(hT_hi[d][:, :], ps_t[d][:, :], ACT.Copy, scale=1024.0).then_inc(t_high, 1)
                if q in (3, 4) and ok(n) and ok(n + U):
                    act.wait_ge(multiplied, past(n - q))
                    weights_high(e + 1, 1 - (j // U) % 2, q - 3)

            weights_high(0, 0, 0)
            weights_high(0, 0, 1)
            turns(act, slot)

        @block.vector
        def _(dve):
            def largest(e, h, turn):
                dve.wait_ge(w_loaded[h], 16 * (turn + 1))
                dve.tensor_reduce(tops[:, :], w[h][:, :, :], AX.XY, ALU.max, apply_absolute_value=True).then_inc(top_ready, 1)

            def largest_of_row(e):
                dve.wait_ge(top_row, e + 1)
                dve.tensor_reduce(topT[:, :], ps_top[0:1, 0:P], AX.X, ALU.max).then_inc(topT_ready, 1)

            def scales(e, h):
                dve.wait_ge(top_all, e + 1)
                dve.tensor_scalar(bits[:, :], ps_top[:, 0:1], 1e-30, None, ALU.max).then_inc(max_ready, 1)
                dve.wait_ge(max_ready, e + 1)
                dve.tensor_scalar(bits[:, :].bitcast(I32), bits[:, :].bitcast(I32), 0x7F800000, None, ALU.bitwise_and).then_inc(bits_ready, 1)
                dve.wait_ge(bits_ready, e + 1)
                dve.tensor_scalar(unscale[h][:, :], bits[:, :], 2.0 ** -23, None, ALU.mult)
                dve.wait_ge(w_ready, past(e))
                dve.reciprocal(scale[:, :], bits[:, :]).then_inc(recip_ready, 1)
                dve.wait_ge(recip_ready, e + 1)
                dve.tensor_scalar(scale[:, :], scale[:, :], 2.0 ** 13, None, ALU.mult).then_inc(scale_ready, 1)

            def weights_low(e, h, half):
                at = slice(2 * half, 2 * half + 2)
                dve.wait_ge(w_high, e * 2 + half + 1)
                done = dve.scalar_tensor_tensor(w_lo[h][:, at, :], w[h][:, at, :], scale[:, :], w_hi[h][:, at, :], ALU.mult, ALU.subtract)
                if half == 1:
                    done.then_inc(w_ready, 1)

            def slot(n, j, k, e, q, ok):
                h = (j // U) % 2
                if ok(n - 1):
                    he = h if q >= 1 else 1 - h
                    dve.wait_ge(multiplied, n)
                    dve.wait_ge(o_ready, past(n - 2))
                    dve.scalar_tensor_tensor(y[(j - 1) % 2][:, :], ps_y[(j - 1) % 3][:, :], unscale[he][:, :],
                                             bias[:, bass.ds(e if q >= 1 else e - 1, 1), :].squeeze(1), ALU.mult, ALU.add).then_inc(y_ready, 1)
                if ok(n + 2):
                    d = (j + 2) % 3
                    dve.wait_ge(t_high, n + 3)
                    dve.scalar_tensor_tensor(hT_lo[d][:, :], ps_t[d][:, :], 1024.0, hT_hi[d][:, :], ALU.mult, ALU.subtract).then_inc(t_low, 1)
                if ok(n - 1):
                    r, t = (q - 1) % U, e + (q - 1) // U
                    dve.wait_ge(y_ready, n)
                    dve.wait_ge(stored[r], 16 * t)
                    dve.scalar_tensor_tensor(o[r][:, :], y[(j - 1) % 2][:, :], c.slot_prob[:, bass.ds(n - 1, 1)], both[r][:, 0:D],
                                             ALU.mult, ALU.add).then_inc(o_ready, 1)
                if ok(n) and ok(n + U):
                    if q == 0:
                        largest(e + 1, 1 - h, k + h)
                    if q == 1:
                        largest_of_row(e + 1)
                    if q == 2:
                        scales(e + 1, 1 - h)
                    if q in (4, 5):
                        weights_low(e + 1, 1 - h, q - 4)

            largest(0, 0, 0)
            largest_of_row(0)
            scales(0, 0)
            weights_low(0, 0, 0)
            weights_low(0, 0, 1)
            dve.wait_ge(bias_loaded, 16)
            turns(dve, slot)


class Consts:
    pass


def build(nc, x, row, col, wt, a2, base_w, spline_w, switch_w, switch_b, expert_w, expert_b, out):
    with ExitStack() as ctx:
        m = Phase(nc, ctx, "g")
        c = Consts()
        c.iota_f, c.iota_p = m.sb("iota_f", [P, P]), m.sb("iota_p", [P, 1])
        c.ones, c.ident, c.tri, c.after = (m.sb(s, [P, P]) for s in ("ones", "ident", "tri", "after"))
        c.swdge = m.sem("swdge", 2 + 2 + 2 + 2 * ST)
        c.st = m.sb("st", [P, 2, NT])
        constants(nc, m, c)
        node_phase(nc, m, c, x, wt, a2)
        row_dram = nc.dram_tensor("row_dram", [ET, P], F32, kind="Internal").ap()
        c.zrow = m.sb("zrow", [1, 3 * P])
        c.last_edge = m.sb("last_edge", [P, NT], U32)
        c.sorted = m.sb("sorted", [ET, 3, P])
        c.row_l, c.att_l, c.col_l = m.sb("row_l", [P, ET]), m.sb("att_l", [P, ET]), m.sb("col_l", [P, ET], U32)
        c.run_on = m.sb("run_on", [ET, 1])
        c.gate_w, c.gate_b, c.mid = m.sb("gate_w", [P, CH, NEXP]), m.sb("gate_b", [P, NEXP]), m.sb("mid", [P, NB])
        c.gate_loaded = m.sem("gate_loaded")
        with nc.Block() as block:

            @block.gpsimd
            def _(pool):
                pool.memset(c.zrow[:, :], 0.0)
                pool.iota(c.mid[:, :], [[-8, NB]], base=28, channel_multiplier=0, allow_small_or_imprecise_dtypes=True)

            @block.sync
            def _(sp):
                sp.dma_start(c.gate_w[:, :, :], switch_w.rearrange("(c p) e -> p c e", p=P)).then_inc(c.gate_loaded, 16)
                sp.dma_start(c.gate_b[:, :], switch_b.broadcast_to([P, NEXP])).then_inc(c.gate_loaded, 16)

        part_dram = nc.dram_tensor("part_dram", [EP + P, D], F32, kind="Internal").ap()
        both_dram = nc.dram_tensor("both_dram", [NP, 2 * D], F32, kind="Internal").ap()
        c.logits, c.prob = m.sb("logits", [P, NT, NEXP]), m.sb("prob", [P, NT])
        c.scale, c.unscale = m.sb("scale", [P, 1]), m.sb("unscale", [P, 1])
        c.slot_read, c.slot_write, c.slot_prob = m.sb("slot_read", [P, FT], U32), m.sb("slot_write", [P, FT], U32), m.sb("slot_prob", [P, FT])
        c.weights_loaded, c.experts_loaded = m.sem("weights_loaded", NPC), m.sem("experts_loaded", 3)
        with ExitStack() as whole:
            memory = lambda numbers: [whole.enter_context(nc.sbuf_tensor(f"weights{n}", [P, 4, D], F32)) for n in numbers]
            c.weights = memory(range(EARLY))
            sort_phase(nc, m, c, row, col, base_w, spline_w)
            c.weights += memory(range(EARLY, NPC))
            with ExitStack() as ectx:
                c.rowb = ectx.enter_context(nc.sbuf_tensor("rowb", [P, ET, P], F32))
                softmax_phase(nc, m, c, row_dram)
                edge_phase(nc, m, c, x, part_dram, base_w, spline_w)
            carry_phase(nc, m, c, part_dram)
            with ExitStack() as split:
                c.w_hi, c.w_lo = (split.enter_context(nc.sbuf_tensor(s, [P, CH, NF, D], F16)) for s in ("w_hi", "w_lo"))
                weight_phase(nc, m, c, base_w, spline_w)
                layer_phase(nc, m, c, x, part_dram, both_dram, out)
        c.expert_w = [m.sb(f"expert_w{b}", [P, CH, D]) for b in range(2)]
        c.expert_b = m.sb("expert_b", [P, NEXP, D])
        route_phase(nc, m, c, expert_w, expert_b)
        expert_phase(nc, m, c, expert_w, both_dram, out)


def kernel(x, src, dst, L0_gnn_W, L0_gnn_a, L0_gnn_base_w, L0_gnn_spline_w, L0_ffn_switch_w,
           L0_ffn_switch_b, L0_ffn_expert_w, L0_ffn_expert_b):
    import numpy as np
    import concourse.bacc as bacc
    from concourse.bass_utils import run_bass_kernel_spmd as run

    lay = np.ascontiguousarray
    pad = EP - N_EDGES
    arrays = {
        "x": np.concatenate([x, np.zeros((NP - N_NODES, D), np.float32)]),
        "row": np.concatenate([src, np.full((pad,), PAD_ROW, np.int32)]).reshape(ET, P),
        "col": np.concatenate([dst, np.zeros((pad,), np.int32)]).reshape(ET, P),
        "wt": lay(np.transpose(L0_gnn_W)),
        "a2": lay(np.transpose(np.reshape(L0_gnn_a, (2, D)))),
        "base_w": lay(np.transpose(L0_gnn_base_w)),
        "spline_w": lay(np.transpose(L0_gnn_spline_w, (1, 2, 0))),
        "switch_w": lay(np.transpose(L0_ffn_switch_w)),
        "switch_b": np.reshape(L0_ffn_switch_b, (1, NEXP)),
        "expert_w": lay(np.transpose(L0_ffn_expert_w, (0, 2, 1))),
        "expert_b": lay(L0_ffn_expert_b),
    }
    nc = bacc.Bacc("TRN2", target_bir_lowering=False, num_devices=1)
    args = [nc.dram_tensor(f"in_{k}", a.shape, mybir.dt.from_np(a.dtype), kind="ExternalInput").ap()
            for k, a in arrays.items()]
    out = nc.dram_tensor("out_0", (NP, D), F32, kind="ExternalOutput").ap()
    build(nc, *args, out)
    r = run(nc, [{f"in_{k}": a for k, a in arrays.items()}], core_ids=[0])
    return r.results[0]["out_0"][:N_NODES]
```
